# Optimizing a Trainium2 kernel written in Bass

```python
import numpy as np
import jax
import jax.numpy as jnp

def _softmax(x, axis=-1):
    return jax.nn.softmax(x, axis=axis)

def _gelu(x):
    return jax.nn.gelu(x, approximate=True)

def _silu(x):
    return jax.nn.silu(x)

def _sigmoid(x):
    return jax.nn.sigmoid(x)

def _layernorm(x, axis=-1, eps=1e-05):
    m = jnp.mean(x, axis=axis, keepdims=True)
    v = jnp.var(x, axis=axis, keepdims=True)
    return (x - m) / jnp.sqrt(v + eps)

def _scatter_add(tgt, idx, src, axis=0):
    return tgt.at[idx].add(src)

def _segment_sum(src, seg, n):
    return jax.ops.segment_sum(src, seg, n)
kernel_name = 'mk_decoder_postln_d1_seqx_r8_bbde1d'

def setup_inputs(seed: int=0):
    np.random.seed(seed)
    _w = jnp.asarray

    def _rec_inputs():
        import jax
        import jax.numpy as jnp
        _rk = jax.random.key(seed)
        x = -0.0002928 + 1 * jax.random.normal(jax.random.fold_in(_rk, 1), (32, 128, 128), jnp.float32)
        _lenS = 128 - jax.random.randint(jax.random.fold_in(_rk, 7), (32,), 0, max(1, 128 // 4) + 1, jnp.int32)
        _lenS2 = 128 - jax.random.randint(jax.random.fold_in(_rk, 8), (32,), 0, max(1, 128 // 4) + 1, jnp.int32)
        _ctx_1024P = jax.random.normal(jax.random.fold_in(_rk, 11), (32, 16, 128), jnp.float32)
        _ctx_1024c = jax.random.dirichlet(jax.random.fold_in(_rk, 511), 0.3 * jnp.ones((16,), jnp.float32), (32, 128))
        _ctx_1024t = jnp.einsum('bsk,bkd->bsd', _ctx_1024c, _ctx_1024P)
        _ctx_1024t = _ctx_1024t * jax.lax.rsqrt(jnp.mean(jnp.square(_ctx_1024t)) + 1e-12) * 0.953939
        ctx_1024 = -1.39393e-06 + 0.999914 * (_ctx_1024t + 0.3 * jax.random.normal(jax.random.fold_in(_rk, 611), (32, 128, 128), jnp.float32))
        _validS = jnp.arange(128)[None, :] < _lenS[:, None]
        _validS2 = jnp.arange(128)[None, :] < _lenS2[:, None]
        _causal = jnp.tril(jnp.ones((128, 128), dtype=bool))
        mask_BxS2_if1 = jnp.where(jnp.ones((32, 128), dtype=bool), 1, 0).astype(jnp.int32)
        return (x, ctx_1024, mask_BxS2_if1)
    x, ctx_1024, mask_BxS2_if1 = _rec_inputs()

    def _L0_attn_setup():
        import jax, jax.numpy as jnp
        import numpy as np
        B_, L_, DIM_, DIN_, N_, DTR_, DCONV_ = (2, 256, 128, 256, 16, 64, 4)

        def _ssm_scan(deltaA, deltaB_u):

            def combine(e1, e2):
                a1, b1 = e1
                a2, b2 = e2
                return (a2 * a1, a2 * b1 + b2)
            _, hs = jax.lax.associative_scan(combine, (deltaA, deltaB_u), axis=1)
            return hs
        key = jax.random.key(seed)
        ks = jax.random.split(key, 7)
        s = 0.02
        inp = {'x': jax.random.normal(ks[0], (B_, L_, DIM_), dtype=jnp.float32), 'W_in': jax.random.normal(ks[1], (DIM_, 2 * DIN_), dtype=jnp.float32) * s, 'conv_w': jax.random.normal(ks[2], (DIN_, 1, DCONV_), dtype=jnp.float32) * s, 'conv_b': jnp.zeros((DIN_,), dtype=jnp.float32), 'W_x': jax.random.normal(ks[3], (DIN_, DTR_ + 2 * N_), dtype=jnp.float32) * s, 'W_dt': jax.random.normal(ks[4], (DTR_, DIN_), dtype=jnp.float32) * s, 'b_dt': jnp.zeros((DIN_,), dtype=jnp.float32), 'W_out': jax.random.normal(ks[5], (DIN_, DIM_), dtype=jnp.float32) * s, 'A_log': jnp.log(jnp.broadcast_to(jnp.arange(1, N_ + 1, dtype=jnp.float32), (DIN_, N_))), 'D': jnp.ones((DIN_,), dtype=jnp.float32)}
        return inp
    _L0_attn_all = _L0_attn_setup()
    _L0_attn_in = {k: v for k, v in _L0_attn_all.items() if k in ('W_in', 'conv_w', 'conv_b', 'W_x', 'W_dt', 'b_dt', 'W_out', 'A_log', 'D')}
    del _L0_attn_all

    def _L0_xattn_setup():
        import jax, jax.numpy as jnp
        import numpy as np
        D_MODEL = 128
        N_HEADS = 16
        HEAD_DIM = D_MODEL // N_HEADS
        ROPE_BASE = 10000.0

        def apply_rope(x):
            b, s, h, d = x.shape
            h_half = d // 2
            theta = 1.0 / ROPE_BASE ** (jnp.arange(0, d, 2, dtype=jnp.float32) / d)
            idx_theta = jnp.arange(s, dtype=jnp.float32)[:, None] * theta[None, :]
            cos = jnp.cos(idx_theta)[None, :, None, :]
            sin = jnp.sin(idx_theta)[None, :, None, :]
            xs = x.reshape(b, s, h, h_half, 2)
            x0, x1 = (xs[..., 0], xs[..., 1])
            out = jnp.stack((x0 * cos - x1 * sin, x1 * cos + x0 * sin), axis=-1)
            return out.reshape(b, s, h, d)
        key = jax.random.key(seed)
        ks = jax.random.split(key, 8)
        B, S, D = (2, 256, D_MODEL)
        scale = 0.02
        return {'Q': jax.random.normal(ks[0], (B, S, D), dtype=jnp.float32), 'K': jax.random.normal(ks[1], (B, S, D), dtype=jnp.float32), 'V': jax.random.normal(ks[2], (B, S, D), dtype=jnp.float32), 'attention_mask': jnp.ones((B, S), dtype=jnp.int32), 'Wq': jax.random.normal(ks[3], (D, D), dtype=jnp.float32) * scale, 'Wk': jax.random.normal(ks[4], (D, D), dtype=jnp.float32) * scale, 'Wv': jax.random.normal(ks[5], (D, D), dtype=jnp.float32) * scale, 'Wo': jax.random.normal(ks[6], (D, D), dtype=jnp.float32) * scale, 'bo': jax.random.normal(ks[7], (D,), dtype=jnp.float32) * scale}
    _L0_xattn_all = _L0_xattn_setup()
    _L0_xattn_in = {k: v for k, v in _L0_xattn_all.items() if k in ('Wq', 'Wk', 'Wv', 'Wo', 'bo')}
    del _L0_xattn_all

    def _L0_ffn_setup():
        import jax, jax.numpy as jnp
        import numpy as np
        JITTER_EPS = 0.01

        def phi_routing(logits, jitter_eps=JITTER_EPS):
            m, sel = jax.lax.top_k(logits, 2)
            T, E = logits.shape
            m1 = m[:, :1]
            factor1 = jnp.maximum(jnp.abs(logits), m1)
            mask1 = (m1 - logits) / factor1 > 2.0 * jitter_eps
            p1 = jax.nn.softmax(jnp.where(mask1, -jnp.inf, logits), axis=-1)
            mult1 = jnp.take_along_axis(p1, sel[:, :1], axis=-1)
            m2 = m[:, 1:2]
            factor2 = jnp.maximum(jnp.abs(logits), m2)
            mask2 = (m2 - logits) / factor2 > 2.0 * jitter_eps
            drop_top1 = jnp.arange(E)[None, :] == sel[:, :1]
            p2 = jax.nn.softmax(jnp.where(mask2 | drop_top1, -jnp.inf, logits), axis=-1)
            mult2 = jnp.take_along_axis(p2, sel[:, 1:2], axis=-1)
            return (jnp.concatenate([mult1, mult2], axis=-1), sel)
        key = jax.random.key(seed)
        k = jax.random.split(key, 5)
        B, S, H, F, E = (1, 64, 128, 512, 8)
        return {'hidden_states': jax.random.normal(k[0], (B, S, H), jnp.float32), 'gate_w': jax.random.normal(k[1], (E, H), jnp.float32) * 0.02, 'w1': jax.random.normal(k[2], (E, F, H), jnp.float32) * 0.02, 'w2': jax.random.normal(k[3], (E, H, F), jnp.float32) * 0.02, 'w3': jax.random.normal(k[4], (E, F, H), jnp.float32) * 0.02}
    _L0_ffn_all = _L0_ffn_setup()
    _L0_ffn_in = {k: v for k, v in _L0_ffn_all.items() if k in ('gate_w', 'w1', 'w2', 'w3')}
    del _L0_ffn_all
    return {'x': x, 'ctx_1024': ctx_1024, 'mask_BxS2_if1': mask_BxS2_if1, 'L0_attn_W_in': _L0_attn_in['W_in'], 'L0_attn_conv_w': _L0_attn_in['conv_w'], 'L0_attn_conv_b': _L0_attn_in['conv_b'], 'L0_attn_W_x': _L0_attn_in['W_x'], 'L0_attn_W_dt': _L0_attn_in['W_dt'], 'L0_attn_b_dt': _L0_attn_in['b_dt'], 'L0_attn_W_out': _L0_attn_in['W_out'], 'L0_attn_A_log': _L0_attn_in['A_log'], 'L0_attn_D': _L0_attn_in['D'], 'L0_xattn_Wq': _L0_xattn_in['Wq'], 'L0_xattn_Wk': _L0_xattn_in['Wk'], 'L0_xattn_Wv': _L0_xattn_in['Wv'], 'L0_xattn_Wo': _L0_xattn_in['Wo'], 'L0_xattn_bo': _L0_xattn_in['bo'], 'L0_ffn_gate_w': _L0_ffn_in['gate_w'], 'L0_ffn_w1': _L0_ffn_in['w1'], 'L0_ffn_w2': _L0_ffn_in['w2'], 'L0_ffn_w3': _L0_ffn_in['w3']}

def reference(x, ctx_1024, mask_BxS2_if1, L0_attn_W_in, L0_attn_conv_w, L0_attn_conv_b, L0_attn_W_x, L0_attn_W_dt, L0_attn_b_dt, L0_attn_W_out, L0_attn_A_log, L0_attn_D, L0_xattn_Wq, L0_xattn_Wk, L0_xattn_Wv, L0_xattn_Wo, L0_xattn_bo, L0_ffn_gate_w, L0_ffn_w1, L0_ffn_w2, L0_ffn_w3):
    import jax
    import jax.numpy as jnp

    def _L0_attn_ref(x, W_in, conv_w, conv_b, W_x, W_dt, b_dt, W_out, A_log, D):
        import jax, jax.numpy as jnp
        import numpy as np
        B_, L_, DIM_, DIN_, N_, DTR_, DCONV_ = (2, 256, 128, 256, 16, 64, 4)

        def _ssm_scan(deltaA, deltaB_u):

            def combine(e1, e2):
                a1, b1 = e1
                a2, b2 = e2
                return (a2 * a1, a2 * b1 + b2)
            _, hs = jax.lax.associative_scan(combine, (deltaA, deltaB_u), axis=1)
            return hs
        b, l, dim = x.shape
        d_in, n = A_log.shape
        dt_rank = W_dt.shape[0]
        d_conv = conv_w.shape[-1]
        xr = x @ W_in
        xs, res = (xr[..., :d_in], xr[..., d_in:])
        xc = jax.lax.conv_general_dilated(xs.transpose(0, 2, 1), conv_w, (1,), [(d_conv - 1, 0)], dimension_numbers=('NCH', 'OIH', 'NCH'), feature_group_count=d_in) + conv_b[None, :, None]
        u = jax.nn.silu(xc.transpose(0, 2, 1))
        x_dbl = u @ W_x
        delta = jax.nn.softplus(x_dbl[..., :dt_rank] @ W_dt + b_dt)
        Bm = x_dbl[..., dt_rank:dt_rank + n]
        Cm = x_dbl[..., dt_rank + n:]
        A = -jnp.exp(A_log)
        deltaA = jnp.exp(delta[..., None] * A)
        deltaB_u = delta[..., None] * Bm[:, :, None, :] * u[..., None]
        hs = _ssm_scan(deltaA, deltaB_u)
        y = jnp.einsum('bldn,bln->bld', hs, Cm) + u * D
        y = y * jax.nn.silu(res)
        return y @ W_out

    def _L0_xattn_ref(Q, K, V, attention_mask, Wq, Wk, Wv, Wo, bo):
        import jax, jax.numpy as jnp
        import numpy as np
        D_MODEL = 128
        N_HEADS = 16
        HEAD_DIM = D_MODEL // N_HEADS
        ROPE_BASE = 10000.0

        def apply_rope(x):
            b, s, h, d = x.shape
            h_half = d // 2
            theta = 1.0 / ROPE_BASE ** (jnp.arange(0, d, 2, dtype=jnp.float32) / d)
            idx_theta = jnp.arange(s, dtype=jnp.float32)[:, None] * theta[None, :]
            cos = jnp.cos(idx_theta)[None, :, None, :]
            sin = jnp.sin(idx_theta)[None, :, None, :]
            xs = x.reshape(b, s, h, h_half, 2)
            x0, x1 = (xs[..., 0], xs[..., 1])
            out = jnp.stack((x0 * cos - x1 * sin, x1 * cos + x0 * sin), axis=-1)
            return out.reshape(b, s, h, d)
        b, s, d = Q.shape
        q = (Q @ Wq.T).reshape(b, s, N_HEADS, HEAD_DIM)
        k = (K @ Wk.T).reshape(b, s, N_HEADS, HEAD_DIM)
        v = (V @ Wv.T).reshape(b, s, N_HEADS, HEAD_DIM)
        q = apply_rope(q)
        k = apply_rope(k)
        scores = jnp.einsum('bnhd,bmhd->bhnm', q, k) / jnp.sqrt(jnp.float32(HEAD_DIM))
        pad = (attention_mask != 0)[:, None, None, :]
        scores = jnp.where(pad, scores, -jnp.inf)
        causal = jnp.tril(jnp.ones((s, s), dtype=bool))[None, None]
        scores = jnp.where(causal, scores, -jnp.inf)
        attn = jax.nn.softmax(scores, axis=-1)
        out = jnp.einsum('bhnm,bmhd->bnhd', attn, v).reshape(b, s, d)
        return out @ Wo.T + bo

    def _L0_ffn_ref(hidden_states, gate_w, w1, w2, w3):
        import jax, jax.numpy as jnp
        import numpy as np
        JITTER_EPS = 0.01

        def phi_routing(logits, jitter_eps=JITTER_EPS):
            m, sel = jax.lax.top_k(logits, 2)
            T, E = logits.shape
            m1 = m[:, :1]
            factor1 = jnp.maximum(jnp.abs(logits), m1)
            mask1 = (m1 - logits) / factor1 > 2.0 * jitter_eps
            p1 = jax.nn.softmax(jnp.where(mask1, -jnp.inf, logits), axis=-1)
            mult1 = jnp.take_along_axis(p1, sel[:, :1], axis=-1)
            m2 = m[:, 1:2]
            factor2 = jnp.maximum(jnp.abs(logits), m2)
            mask2 = (m2 - logits) / factor2 > 2.0 * jitter_eps
            drop_top1 = jnp.arange(E)[None, :] == sel[:, :1]
            p2 = jax.nn.softmax(jnp.where(mask2 | drop_top1, -jnp.inf, logits), axis=-1)
            mult2 = jnp.take_along_axis(p2, sel[:, 1:2], axis=-1)
            return (jnp.concatenate([mult1, mult2], axis=-1), sel)
        B, S, H = hidden_states.shape
        E = w1.shape[0]
        x = hidden_states.reshape(-1, H)
        logits = x @ gate_w.T
        routing_weights, selected = phi_routing(logits)
        T = x.shape[0]
        wte = jnp.zeros((T, E), x.dtype).at[jnp.arange(T)[:, None], selected].add(routing_weights)
        out = jnp.zeros_like(x)
        for e in range(E):
            h = jax.nn.silu(x @ w1[e].T) * (x @ w3[e].T)
            out = out + wte[:, e:e + 1] * (h @ w2[e].T)
        return out.reshape(B, S, H)
    x = _layernorm(x + _L0_attn_ref(x, L0_attn_W_in, L0_attn_conv_w, L0_attn_conv_b, L0_attn_W_x, L0_attn_W_dt, L0_attn_b_dt, L0_attn_W_out, L0_attn_A_log, L0_attn_D), axis=-1)
    x = _layernorm(x + _L0_xattn_ref(x, ctx_1024, ctx_1024, mask_BxS2_if1, L0_xattn_Wq, L0_xattn_Wk, L0_xattn_Wv, L0_xattn_Wo, L0_xattn_bo), axis=-1)
    x = _layernorm(x + _L0_ffn_ref(x, L0_ffn_gate_w, L0_ffn_w1, L0_ffn_w2, L0_ffn_w3), axis=-1)
    return x

_drawn_inputs = setup_inputs


def setup_inputs(seed=0):
    import zlib

    import numpy as np

    out = dict(_drawn_inputs(seed))
    spreads = {'L0_attn_conv_b': (0.0, 0.8), 'L0_attn_b_dt': (0.0, 0.8), 'L0_attn_D': (1.0, 0.6)}
    factors = {'L0_attn_W_in': 8.0,
     'L0_attn_conv_w': 8.0,
     'L0_attn_W_x': 8.0,
     'L0_attn_W_dt': 8.0,
     'L0_attn_W_out': 8.0,
     'L0_attn_A_log': 8.0,
     'L0_xattn_Wq': 8.0,
     'L0_xattn_Wk': 8.0,
     'L0_xattn_bo': 2.673,
     'L0_ffn_gate_w': 3.985,
     'L0_ffn_w1': 3.483,
     'L0_ffn_w2': 3.47,
     'L0_ffn_w3': 3.468}
    for name, (base, spread) in spreads.items():
        noise = np.random.default_rng([zlib.crc32(name.encode()), seed]).standard_normal(out[name].shape)
        drawn = base * np.exp(spread * noise) if base else spread * noise
        out[name] = jnp.asarray(drawn.astype(out[name].dtype))
    for name, factor in factors.items():
        out[name] = (out[name] * factor).astype(out[name].dtype)
    return out
```

```python
import concourse.bass as bass
from concourse import mybir
from contextlib import ExitStack

F32 = mybir.dt.float32
BF16 = mybir.dt.bfloat16
I32 = mybir.dt.int32
U32 = mybir.dt.uint32
ALU = mybir.AluOpType
ACT = mybir.ActivationFunctionType
AX = mybir.AxisListType

P = 128
B, L, D = 32, 128, 128
S = 4
G = B // S
T = S * L
DIN, NST, DTR, KCONV = 256, 16, 64, 4
H, HD = 16, 8
AHEAD = 3
E, F = 8, 512
FC = F // P
STRIDE = B * L + P
NT = (2 * B * L + E * (P - 1)) // P + 1
NT += -NT % 4
EPS = 1e-5
NEG = -1e30
RESET = 1e25
ROUTER_LINKS = 21


def build(nc, a, out):
    ctx = ExitStack()
    with ctx:
        def sb(name, shape, dt=F32):
            return ctx.enter_context(nc.sbuf_tensor(name, shape, dt))

        def sem(name):
            return ctx.enter_context(nc.semaphore(name))

        ident = sb("ident", [P, P])
        identb = sb("identb", [P, P], BF16)
        w_in = sb("w_in", [P, 2 * DIN])
        w_conv = sb("w_conv", [P, KCONV, DIN])
        conv_b = sb("conv_b", [P, 2])
        w_dtl = sb("w_dtl", [P, 2, DTR])
        w_bc = sb("w_bc", [P, 2, 3, 2 * NST])
        w_dt = sb("w_dt", [DTR, DIN])
        b_dt = sb("b_dt", [P, 2])
        w_out = sb("w_out", [P, 2, D])
        a_log = sb("a_log", [P, 2, NST])
        a_neg = sb("a_neg", [P, 2, NST])
        d_col = sb("d_col", [P, 2])
        d_diag = sb("d_diag", [P, 2, P])
        sel32 = sb("sel32", [96, 2 * NST])
        sel = sb("sel", [96, 2 * NST, P], BF16)
        wqT = sb("wqT", [P, P])
        wqrT = sb("wqrT", [P, P])
        wkT = sb("wkT", [P, P])
        wkrT = sb("wkrT", [P, P])
        wvT = sb("wvT", [P, P])
        woT = sb("woT", [P, P])
        bo_b = sb("bo_b", [P, P])
        rope = sb("rope", [P, 4, L])
        causal = sb("causal", [P, L])
        mask_b = sb("mask_b", [P, T], I32)
        gate_wT = sb("gate_wT", [P, E])
        w1 = sb("w1", [P, E, F])
        w3 = sb("w3", [P, E, F])
        eps_col = sb("eps_col", [P, 1])
        one_col = sb("one_col", [P, 1])
        iota8 = sb("iota8", [P, E])
        tri = sb("tri", [P, P], BF16)
        ones_b = sb("ones_b", [P, P], BF16)
        zrow = sb("zrow", [P, D])

        xn = sb("xn", [P, S, D])
        xT = sb("xT", [P, S, KCONV - 1 + L])
        u = sb("u", [P, 2, T])
        sres = sb("sres", [P, 2, T])
        bc3 = sb("bc3", [96, T], BF16)
        bc_rest = sb("bc_rest", [96, T])
        bc_mid = sb("bc_mid", [96, T], BF16)
        dtl = sb("dtl", [DTR, T])
        zabs = sb("zabs", [P, 2, T])
        zpos = sb("zpos", [P, 2, T])
        delta = sb("delta", [P, 2, T])
        du = sb("du", [P, 2, T])
        b_row = sb("b_row", [P, AHEAD + 1, T])
        scan = sb("scan", [P, 2, 2, 2, T])
        bu = scan[:, 0]
        hst = scan[:, 1]
        hc = sb("hc", [P, 2, 2, T])
        yg = zabs
        sx = sb("sx", [P, S, D])
        stats = sb("stats", [P, S, 6])
        mv = sb("mv", [P, S, 2])
        lnv = sb("lnv", [P, S])
        rstd = sb("rstd", [P, S])
        x1 = sb("x1", [P, S, D])
        x1b = sb("x1b", [P, S, D])
        cn = sb("cn", [P, S, D])
        x1T = sb("x1T", [P, T])
        cT = sb("cT", [P, T])
        rot = sb("rot", [P, 4, T])
        conv_taps = rot[:, 0:2, :].rearrange("p a t -> p (a t)").rearrange("p (k c) -> p k c", k=KCONV)
        qk = sb("qk", [P, 2, T])
        qk_al = scan[:, :, :, :, :].rearrange("p i a b t -> p i (a b) t")
        q_al, k_al = qk_al[:, 0], qk_al[:, 1]
        v_ext = sb("v_ext", [P, S, H, HD + 1])
        pad = sb("pad", [P, T])
        mbias = sb("mbias", [P, S, L], BF16)
        nmax = sb("nmax", [P, 2, H])
        prob = sb("prob", [P, 2, 4, 4, L])
        w2 = prob[:, :, :, :, :].rearrange("p a j c m -> p (a j) c m")
        pT = sb("pT", [P, 2, 4, L])
        rden = sb("rden", [P, 2, H])
        ao = sb("ao", [P, 2, H, HD])
        aoT = sb("aoT", [P, T])
        x2 = sb("x2", [P, S, D])
        x2_all = sb("x2_all", [P, B, D])
        x2T = sb("x2T", [P, T])
        lg = sb("lg", [P, S, E])
        m8 = sb("m8", [P, S, 8])
        i8 = sb("i8", [P, S, 8], U32)
        idxf = sb("idxf", [P, S, 2])
        oh = sb("oh", [P, S, 2, E])
        ohb = sb("ohb", [P, S, E], BF16)
        lab = sb("lab", [P, S, E])
        fac = sb("fac", [P, S, 2, E])
        gap = sb("gap", [P, S, 2, E])
        thr = sb("thr", [P, S, 2, E])
        keep = sb("keep", [P, S, 2, E])
        gexp = sb("gexp", [P, S, 2, E])
        gsum = sb("gsum", [P, S, 2])
        gates_all = sb("gates_all", [P, B, 2])
        base = sb("base", [P, E])
        rank = sb("rank", [P, S, E])
        prk = sb("prk", [P, S, 2, E])
        posf = sb("posf", [P, S, 2])
        pos = sb("pos", [P, S, 2], I32)
        posf_all = sb("posf_all", [P, B, 2])
        idxf_all = sb("idxf_all", [P, B, 2])
        shift = sb("shift", [P, E])
        part = sb("part", [P, B, 2])
        pos_all = sb("pos_all", [P, B, 2], I32)
        tail_f = sb("tail_f", [P, E])
        tail_i = sb("tail_i", [P, E], I32)
        pcol = sb("pcol", [P, 1])
        erow = sb("erow", [P, E])
        cnt = sb("cnt", [P, E])
        k128 = sb("k128", [P, B])
        full = u[:, 0:2, :].rearrange("p h t -> p (h t)")[:, 0:(E) * B].rearrange("p (a b) -> p a b", b=B)
        ntile = sb("ntile", [P, E])
        ones8 = sb("ones8", [P, E])
        cum = sb("cum", [P, E])
        lastt = sb("lastt", [1, 1])
        jrow = sb("jrow", [1, NT + 4])
        jc = sb("jc", [1, NT + 4])
        ind = sres[0:1, 0:2, :].rearrange("p h t -> p (h t)")[:, 0:(NT + 4) * E].rearrange("p (a b) -> p a b", b=E)
        jump = sb("jump", [1, E])
        wsum = yg[0:1, 0:2, :].rearrange("p h t -> p (h t)")[:, 0:(NT + 4) * E].rearrange("p (a b) -> p a b", b=E)
        t_e = sb("t_e", [1, NT + 4])
        t_row = sb("t_row", [1, NT + 4])
        t_tmp = sb("t_tmp", [1, NT + 4])
        table = sb("table", [1, 2, NT + 4], I32)
        xs = qk[:, 0, :].rearrange("p (b d) -> p b d", b=4)
        xsT = qk[:, 1, 0:2 * P].rearrange("p (b n) -> p b n", b=2)
        sl = zabs
        gg = zpos
        gT = delta[:, :, :].rearrange("p b (c n) -> p b c n", c=FC)
        ys = aoT[:, 0:2 * D].rearrange("p (b d) -> p b d", b=2)
        idx = sb("idx", [P, 2 * S], I32)
        yk = du[:, :, :].rearrange("p k (s d) -> p (k s) d", s=S)
        acc = sx
        fin = x1

        bank = [ctx.enter_context(nc.psum_tensor(f"bank{i}", [P, 512], F32)) for i in (0, 1)]
        quad = ctx.enter_context(nc.psum_tensor("quad", [P, 4, 512], F32))
        bank += [quad[:, i] for i in range(4)]
        pair = ctx.enter_context(nc.psum_tensor("pair", [P, 2, 512], F32))
        bank += [pair[:, i] for i in range(2)]
        bank = [b if i > 1 else b[:, :] for i, b in enumerate(bank)]
        y_ps = quad[:, 2:4]

        xg = nc.dram_tensor("xg", (E * STRIDE, D), F32, kind="Internal").ap()
        qk_d = nc.dram_tensor("qk_d", (P, 2, T), F32, kind="Internal").ap()
        qk_heads = qk_d.rearrange("(j c d) i t -> j d i c t", j=4, c=4)
        yl = nc.dram_tensor("yl", (NT * P, D), F32, kind="Internal").ap()

        names = """passed w_load pool_const dve_const act_const
        x_load ctx_load mask_load w2_load xT_ps xT_sb conv_ps res_ps u_sb sres_sb bc_ps dtl_ps bc_hi bc_res1 bc_mid_s bc3_sb dtl_sb
        z_ps zabs_sb zexp_sb softp delta_sb du_sb delta_set
        b_ps b_sb bu_sb a_ps h_sb c_ps hc_sb y_sum yg_sb o_ps
        ln_sum ln_stat ln_var ln_log ln_rstd x1_sb x1b_sb x1T_ps x1T_sb cT_ps cT_sb proj_ps v_ps v_sb rot_sb qk_sb qk_out qk_al
        pad_sb mask_sb s_ps s_max s_sub p_sb pT_ps pT_sb pv_ps den_sb ao_sb aoT_ps aoT_sb wo_ps
        x2_sb x2T_ps x2T_sb lg_ps route gexp_sb rank_ps pos_sb scat x2_sent
        tail tail_scat table_sb table_link
        xs_load0 xs_load1 xs_load2 xs_load3 xsT_ps xsT_sb up_ps silu_sb gate_sb gT_ps gT_sb y_ps_s y_sb y_store0 y_store1
        idx_sb gath acc_s f_sum f_stat f_var f_log f_rstd fin_sb fin_store""".split()
        s = {n: sem(n) for n in names}

        xr = a["x"].rearrange("(g s) t d -> g t s d", s=S)
        cr = a["ctx_1024"].rearrange("(g s) t d -> g t s d", s=S)
        mr = a["mask"].rearrange("(g t) -> g t", t=T)
        outr = out.rearrange("(g s) t d -> g t s d", s=S)
        block = ctx.enter_context(nc.Block())

        W_LOADS = []

        def load(dst, src):
            W_LOADS.append((dst, src))

        load(w_in[:, :], a["W_in"])
        load(conv_taps, a["conv_w"].partition_broadcast(P))
        load(conv_b[:, :], a["conv_b"])
        load(w_dtl[:, :, :], a["W_x"][:, :, 0:DTR])
        for r in range(3):
            load(w_bc[:, :, r, :], a["W_x"][:, :, DTR:DTR + 2 * NST])
        load(w_dt[:, :], a["W_dt"])
        load(b_dt[:, :], a["b_dt"])
        load(w_out[:, :, :], a["W_out"])
        load(a_log[:, :, :], a["A_log"])
        load(d_col[:, :], a["D"])
        for dst, n in ((wqT, "WqT"), (wqrT, "WqrT"), (wkT, "WkT"), (wkrT, "WkrT"), (wvT, "WvT"), (woT, "WoT")):
            load(dst[:, :], a[n])
        load(bo_b[:, :], a["bo"].partition_broadcast(P))
        load(rope[:, :, :], a["rope"])
        load(gate_wT[:, :], a["gate_wT"])
        load(w1[:, :, :], a["w1T"])
        load(w3[:, :, :], a["w3T"])
        NW = len(W_LOADS)

        def early(eng, which):
            for n in which.split():
                eng.sem_inc(s[n], 16 if n in ("y_store0", "y_store1", "fin_store") else 1)

        def plain(eng):
            eng.sem_inc(s["passed"], 1)

        @block.sync
        def _(sp):
            early(sp, "y_store0 y_store1 fin_store")
            for dst, src in W_LOADS:
                sp.dma_start(dst, src).then_inc(s["w_load"], 16)
            with sp.Fori(0, G) as g:
                sp.wait_ge(s["ln_sum"], 1 + g * 2)
                plain(sp)
                sp.dma_start(xn[:, :, :], xr[bass.ds(g, 1)].rearrange("g t s d -> (g t) s d")).then_inc(s["x_load"], 16)
                sp.wait_ge(s["cT_ps"], 1 + g)
                plain(sp)
                sp.dma_start(cn[:, :, :], cr[bass.ds(g, 1)].rearrange("g t s d -> (g t) s d")).then_inc(s["ctx_load"], 16)
                sp.wait_ge(s["pad_sb"], 1 + g)
                plain(sp)
                sp.dma_start(mask_b[:, :], mr[bass.ds(g, 1)].rearrange("a t -> (a t)").partition_broadcast(P)).then_inc(s["mask_load"], 16)
                sp.wait_ge(s["qk_sb"], g * 2 + 2)
                plain(sp)
                sp.wait_ge(s["s_ps"], 1 + g * 8)
                plain(sp)
                sp.dma_start(qk_d[:, :, :], qk[:, :, :]).then_inc(s["qk_out"], 16)
                sp.wait_ge(s["qk_out"], g * 16 + 16)
                for j in range(4):
                    sp.dma_start(qk_al[32 * j:32 * j + HD], qk_heads[j]).then_inc(s["qk_al"], 16)
            sp.wait_ge(s["pv_ps"], G * 4 * S)
            sp.dma_start(w2, a["w2T"]).then_inc(s["w2_load"], 16)
            sp.wait_ge(s["table_sb"], 1)
            sp.wait_ge(s["scat"], G * 2 * S * 16)
            sp.wait_ge(s["tail_scat"], E * 16)

            def rows_in(j, b):
                r = sp.value_load(table[0:1, 1, bass.ds(j, 1)], min_val=0, max_val=E * STRIDE - P)
                sp.dma_start(xs[:, b, :], xg[bass.ds(r, P), :]).then_inc(s[f"xs_load{b}"], 16)

            for j in range(3):
                rows_in(j, j)
            with sp.Fori(0, NT // 4) as it:
                for b in range(4):
                    j = it * 4 + b
                    sp.wait_ge(s["xsT_ps"], 1 + j)
                    plain(sp)
                    rows_in(j + 3, (b + 3) % 4)
                    sp.wait_ge(s["y_sb"], 1 + j + 1)
                    plain(sp)
                    sp.dma_start(yl[bass.ds(j * P, P), :], ys[:, b % 2, :]).then_inc(s[f"y_store{b % 2}"], 16)
            with sp.Fori(0, G) as g:
                sp.wait_ge(s["fin_sb"], g * S + S)
                plain(sp)
                sp.dma_start(outr[bass.ds(g, 1)].rearrange("g t s d -> (g t) s d"), fin[:, :, :]).then_inc(s["fin_store"], 16)
            sp.wait_ge(s["fin_store"], 16 + 16 * G)

        @block.gpsimd
        def _(pool):
            g_ = nc.gpsimd
            early(pool, "pad_sb delta_sb bu_sb x2_sent")
            cs = [0]

            def link(ins):
                cs[0] += 1
                ins.then_inc(s["pool_const"], 1)
                pool.wait_ge(s["pool_const"], cs[0])

            pool.wait_ge(s["w_load"], 16 * NW)
            link(g_.memset(ident[:, :], 0.0))
            link(g_.affine_select(out=ident[:, :], in_=ident[:, :], compare_op=ALU.not_equal, fill=1.0, base=0,
                                  pattern=[[-1, P]], channel_multiplier=1))
            link(g_.memset(causal[:, :], 0.0))
            link(g_.affine_select(out=causal[:, :], in_=causal[:, :], compare_op=ALU.is_ge, fill=NEG, base=0,
                                  pattern=[[-1, L]], channel_multiplier=1))
            link(g_.memset(ones_b[:, :], 1.0))
            link(g_.affine_select(out=tri[:, :], in_=ones_b[:, :], compare_op=ALU.is_gt, fill=0.0, base=0,
                                  pattern=[[1, P]], channel_multiplier=-1))
            link(g_.memset(zrow[:, :], 0.0))
            link(g_.memset(xT[:, :, :], 0.0))
            link(g_.memset(v_ext[:, :, :, :], 1.0))
            link(g_.memset(eps_col[:, :], EPS))
            link(g_.memset(one_col[:, :], 1.0))
            link(g_.memset(ones8[:, :], 1.0))
            link(g_.iota(iota8[:, :], pattern=[[1, E]], base=0, channel_multiplier=0, allow_small_or_imprecise_dtypes=True))
            link(g_.iota(base[:, :], pattern=[[STRIDE, E]], base=0, channel_multiplier=0, allow_small_or_imprecise_dtypes=True))
            link(g_.iota(erow[:, :], pattern=[[STRIDE, E]], base=0, channel_multiplier=0, allow_small_or_imprecise_dtypes=True))
            link(g_.iota(pcol[:, :], pattern=[[1, 1]], base=0, channel_multiplier=1, allow_small_or_imprecise_dtypes=True))
            link(g_.iota(k128[:, :], pattern=[[P, B]], base=0, channel_multiplier=0, allow_small_or_imprecise_dtypes=True))
            link(g_.iota(jrow[:, :], pattern=[[1, NT + 4]], base=0, channel_multiplier=0, allow_small_or_imprecise_dtypes=True))

            with pool.Fori(0, G) as g:
                pool.wait_ge(s["softp"], g + 1)
                pool.wait_ge(s["a_ps"], 1 + g * 2 * NST)
                g_.tensor_tensor(delta[:, :, :], zpos[:, :, :], zabs[:, :, :], ALU.add).then_inc(s["delta_sb"], 1)
                pool.wait_ge(s["delta_sb"], 1 + g + 1)
                g_.tensor_tensor(du[:, :, :], delta[:, :, :], u[:, :, :], ALU.mult).then_inc(s["du_sb"], 1)
                pool.wait_ge(s["du_sb"], g + 1)
                plain(pool)
                for h in range(2):
                    last = g_.memset(delta[:, h, :].rearrange("p (s t) -> p s t", s=S)[:, :, 0:1], RESET)
                    last.then_inc(s["delta_set"], 1)
                for n in range(NST):
                    pool.wait_ge(s["b_sb"], 1 + g * NST + n + 1)
                    pool.wait_ge(s["h_sb"], 1 + g * 2 * NST + max(0, 2 * n - 2))
                    g_.tensor_tensor(bu[:, n % 2], du[:, :, :], b_row[:, n % (AHEAD + 1), :].unsqueeze(1).broadcast_to((P, 2, T)),
                                     ALU.mult).then_inc(s["bu_sb"], 1)
                pool.wait_ge(s["mask_load"], g * 16 + 16)
                plain(pool)
                g_.tensor_scalar(pad[:, :], mask_b[:, :], 0.0, NEG, ALU.is_equal, ALU.mult).then_inc(s["pad_sb"], 1)
                pool.wait_ge(s["pad_sb"], 1 + g + 1)
                pool.wait_ge(s["s_ps"], 1 + g * 8)
                g_.tensor_tensor(mbias[:, :, :], pad[:, :].rearrange("p (s t) -> p s t", s=S),
                                 causal[:, :].unsqueeze(1).broadcast_to((P, S, L)), ALU.add).then_inc(s["mask_sb"], 1)
                pool.wait_ge(s["x1_sb"], g * S + S)
                pool.wait_ge(s["ln_sum"], 1 + g * 2)
                g_.tensor_tensor(x1b[:, :, :], x1[:, :, :], bo_b[:, :].unsqueeze(1).broadcast_to((P, S, D)), ALU.add).then_inc(s["x1b_sb"], 1)
                for i in range(2):
                    pool.wait_ge(s["rot_sb"], g * 4 + 2 * i + 2)
                    g_.tensor_tensor(qk[:, i, :], rot[:, 2 * i, :], rot[:, 2 * i + 1, :], ALU.add).then_inc(s["qk_sb"], 1)
                pool.wait_ge(s["pos_sb"], 1 + g + 1)
                plain(pool)
                for t in range(S):
                    for k in range(2):
                        pool.indirect_dma_start(xg[:, :], bass.IndirectOffsetOnAxis(ap=pos[:, t, k:k + 1], axis=0),
                                                x2[:, t, :], None).then_inc(s["scat"], 16)
                pool.wait_ge(s["scat"], (g + 1) * 2 * S * 16)
                pool.sem_inc(s["x2_sent"], 1)
            pool.wait_ge(s["tail"], 2)
            for e in range(E):
                pool.indirect_dma_start(xg[:, :], bass.IndirectOffsetOnAxis(ap=tail_i[:, e:e + 1], axis=0),
                                        zrow[:, :], None).then_inc(s["tail_scat"], 16)
            for b in range(2):
                pool.wait_ge(s[f"y_store{b}"], 16 + NT // 2 * 16)
            with pool.Fori(0, G) as g:
                pool.wait_ge(s["idx_sb"], g + 1)
                pool.wait_ge(s["acc_s"], 1 + g * 2 * S)
                plain(pool)
                for i in range(2 * S):
                    pool.indirect_dma_start(yk[:, i, :], None, yl[:, :], bass.IndirectOffsetOnAxis(ap=idx[:, i:i + 1], axis=0)).then_inc(s["gath"], 16)

        @block.scalar
        def _(act):
            A = nc.scalar.activation
            early(act, "a_ps b_sb pT_sb")
            act.wait_ge(s["w_load"], 16 * NW)
            act.wait_ge(s["pool_const"], 18)
            A(a_neg[:, :, :], a_log[:, :, :], ACT.Exp).then_inc(s["act_const"], 1)
            act.wait_ge(s["dve_const"], 7)
            with act.Fori(0, G) as g:
                act.wait_ge(s["xT_ps"], g + 1)
                A(xT[:, :, KCONV - 1:], bank[0].rearrange("p (s t) -> p s t", s=S), ACT.Copy).then_inc(s["xT_sb"], 1)
                nc.scalar.preload_act_table_set("silu_and_others")
                act.wait_ge(s["hc_sb"], 1 + g * NST)
                for h in range(2):
                    act.wait_ge(s["conv_ps"], g * 2 + h + 1)
                    A(u[:, h, :], bank[1 + h], ACT.Silu, bias=conv_b[:, h:h + 1]).then_inc(s["u_sb"], 1)
                for h in range(2):
                    act.wait_ge(s["res_ps"], g * 2 + h + 1)
                    A(sres[:, h, :], bank[3 + h], ACT.Silu).then_inc(s["sres_sb"], 1)
                act.wait_ge(s["bc_ps"], g + 1)
                A(bc3[:, :], bank[6][0:96, :], ACT.Copy).then_inc(s["bc_hi"], 1)
                act.wait_ge(s["dtl_ps"], g + 1)
                A(dtl[:, :], bank[7][0:DTR, :], ACT.Copy).then_inc(s["dtl_sb"], 1)
                act.wait_ge(s["bc_res1"], g + 1)
                A(bc_mid[:, :], bc_rest[:, :], ACT.Copy).then_inc(s["bc_mid_s"], 1)
                act.wait_ge(s["delta_sb"], 1 + g)
                for h in range(2):
                    act.wait_ge(s["z_ps"], g * 2 + h + 1)
                    A(zabs[:, h, :], bank[1 + h], ACT.Abs, bias=b_dt[:, h:h + 1]).then_inc(s["zabs_sb"], 1)
                    A(zpos[:, h, :], bank[1 + h], ACT.Relu, bias=b_dt[:, h:h + 1]).then_inc(s["zabs_sb"], 1)
                nc.scalar.preload_act_table_set("natural_log_exp_and_others")
                act.wait_ge(s["zabs_sb"], g * 4 + 4)
                A(zabs[:, :, :], zabs[:, :, :], ACT.Exp, scale=-1.0).then_inc(s["zexp_sb"], 1)
                act.wait_ge(s["zexp_sb"], g + 1)
                A(zabs[:, :, :], zabs[:, :, :], ACT.Ln, bias=one_col[:, :]).then_inc(s["softp"], 1)
                def b_out(n):
                    act.wait_ge(s["b_ps"], g * NST + n + 1)
                    act.wait_ge(s["bu_sb"], 1 + g * NST + max(0, n - AHEAD))
                    A(b_row[:, n % (AHEAD + 1), :], bank[1], ACT.Copy).then_inc(s["b_sb"], 1)

                for n in range(AHEAD - 1):
                    b_out(n)
                for n in range(NST):
                    for h in range(2):
                        if n == 0:
                            act.wait_ge(s["delta_set"], g * 2 + 2)
                        act.wait_ge(s["h_sb"], 1 + g * 2 * NST + max(0, 2 * n + h - 1))
                        A(bank[6 + h], delta[:, h, :], ACT.Exp, scale=a_neg[:, h, n:n + 1]).then_inc(s["a_ps"], 1)
                    if n + AHEAD - 1 < NST:
                        b_out(n + AHEAD - 1)

                def ln_scale(k):
                    act.wait_ge(s["ln_var"], g * 2 + k + 1)
                    A(lnv[:, :], mv[:, :, 1], ACT.Ln, bias=eps_col[:, :]).then_inc(s["ln_log"], 1)
                    act.wait_ge(s["ln_log"], g * 2 + k + 1)
                    A(rstd[:, :], lnv[:, :], ACT.Exp, scale=-0.5).then_inc(s["ln_rstd"], 1)

                ln_scale(0)
                act.wait_ge(s["cT_ps"], 1 + g + 1)
                A(cT[:, :], bank[1], ACT.Copy).then_inc(s["cT_sb"], 1)
                act.wait_ge(s["x1T_ps"], g + 1)
                A(x1T[:, :], bank[0], ACT.Copy).then_inc(s["x1T_sb"], 1)
                act.wait_ge(s["v_ps"], g + 1)
                A(v_ext[:, :, :, 0:HD], bank[6].rearrange("p (s h d) -> p s h d", s=S, h=H), ACT.Copy).then_inc(s["v_sb"], 1)
                for t in range(S):
                    for k in range(2):
                        act.wait_ge(s["s_sub"], 1 + g * 8 + 2 * t + k + 1)
                        A(prob[:, t % 2, 2 * k:2 * k + 2], prob[:, t % 2, 2 * k:2 * k + 2], ACT.Exp).then_inc(s["p_sb"], 1)
                    for j in range(4):
                        act.wait_ge(s["pT_ps"], g * 16 + 4 * t + j + 1)
                        A(pT[:, j % 2], bank[6 + j % 2].rearrange("p (c n) -> p c n", c=4), ACT.Copy).then_inc(s["pT_sb"], 1)
                act.wait_ge(s["aoT_ps"], g * S + S)
                A(aoT[:, :], bank[1], ACT.Copy).then_inc(s["aoT_sb"], 1)
                ln_scale(1)
                act.wait_ge(s["x2T_ps"], g + 1)
                A(x2T[:, :], bank[0], ACT.Copy).then_inc(s["x2T_sb"], 1)
                act.wait_ge(s["route"], 1 + g * ROUTER_LINKS + 12)
                A(gexp[:, :, :, :], gap[:, :, :, :], ACT.Exp, scale=-1.0).then_inc(s["gexp_sb"], 1)
            def x_out(j, b):
                act.wait_ge(s["xsT_ps"], 1 + j + 1)
                A(xsT[:, b, :], bank[7][:, b * P:(b + 1) * P], ACT.Copy).then_inc(s["xsT_sb"], 1)

            def silu(j, b):
                act.wait_ge(s["up_ps"], 1 + 2 * j + 1)
                A(sl[:, b, :], bank[b], ACT.Silu).then_inc(s["silu_sb"], 1)

            nc.scalar.preload_act_table_set("silu_and_others")
            x_out(0, 0)
            x_out(1, 1)
            silu(0, 0)
            with act.Fori(0, NT // 2) as it:
                for b in range(2):
                    j = it * 2 + b
                    act.wait_ge(s["gT_ps"], j + 1)
                    A(gT[:, b], bank[4 + b].rearrange("p (c n) -> p c n", c=FC), ACT.Copy).then_inc(s["gT_sb"], 1)
                    x_out(j + 2, b)
                    silu(j + 1, 1 - b)
            with act.Fori(0, G) as g:
                act.wait_ge(s["f_var"], g + 1)
                A(lnv[:, :], mv[:, :, 1], ACT.Ln, bias=eps_col[:, :]).then_inc(s["f_log"], 1)
                act.wait_ge(s["f_log"], g + 1)
                A(rstd[:, :], lnv[:, :], ACT.Exp, scale=-0.5).then_inc(s["f_rstd"], 1)

        @block.vector
        def _(dve):
            v_ = nc.vector
            TT = v_.tensor_tensor
            early(dve, "ln_sum h_sb hc_sb acc_s route pos_sb s_sub gate_sb y_sb")
            dve.wait_ge(s["w_load"], 16 * NW)
            dve.wait_ge(s["pool_const"], 18)
            v_.tensor_copy(identb[:, :], ident[:, :]).then_inc(s["dve_const"], 1)
            TT(w_conv[:, :, :], conv_taps, w_in[:, 0:DIN].unsqueeze(1).broadcast_to((P, KCONV, DIN)), ALU.mult).then_inc(s["dve_const"], 1)
            for h in range(2):
                last = v_.tensor_scalar(d_diag[:, h, :], ident[:, :], d_col[:, h:h + 1], None, ALU.mult)
            last.then_inc(s["dve_const"], 1)
            v_.tensor_reduce(out=sel32[:, :], in_=ident[0:96, 0:96].rearrange("p (r j) -> p j r", r=3), axis=AX.X, op=ALU.add).then_inc(s["dve_const"], 1)
            dve.wait_ge(s["dve_const"], 4)
            v_.tensor_copy(sel[:, :, :], sel32[:, :].unsqueeze(2).broadcast_to((96, 2 * NST, P))).then_inc(s["dve_const"], 1)
            dve.wait_ge(s["act_const"], 1)
            v_.tensor_scalar(a_neg[:, :, :], a_neg[:, :, :], -1.0, None, ALU.mult).then_inc(s["dve_const"], 1)
            v_.tensor_scalar(jump[:, :], erow[0:1, :], 1.0, None, ALU.mult).then_inc(s["dve_const"], 1)
            dve.wait_ge(s["dve_const"], 7)

            def layer_norm(src, res, dst, g, k, names, per):
                n_sum, n_stat, n_var, n_rstd, n_out = names
                TT(sx[:, :, :], src, res, ALU.add).then_inc(s[n_sum], 1)
                dve.wait_ge(s[n_sum], 1 + g * per + k + 1)
                for t in range(S):
                    last = v_.bn_stats(stats[:, t, :], sx[:, t, :])
                last.then_inc(s[n_stat], 1)
                dve.wait_ge(s[n_stat], g * per + k + 1)
                plain(dve)
                for t in range(S):
                    last = v_.bn_aggr(mv[:, t, :], stats[:, t, :])
                last.then_inc(s[n_var], 1)
                dve.wait_ge(s[n_rstd], g * per + k + 1)
                for t in range(S):
                    v_.tensor_scalar(dst[:, t, :], sx[:, t, :], mv[:, t, 0:1], rstd[:, t:t + 1], ALU.subtract, ALU.mult).then_inc(s[n_out], 1)

            with dve.Fori(0, G) as g:
                dve.wait_ge(s["bc_hi"], g + 1)
                TT(bc_rest[:, :], bank[6][0:96, :], bc3[:, :], ALU.subtract).then_inc(s["bc_res1"], 1)
                dve.wait_ge(s["bc_mid_s"], g + 1)
                TT(bc3[64:96, :], bc_rest[64:96, :], bc_mid[64:96, :], ALU.subtract).then_inc(s["bc3_sb"], 1)
                v_.tensor_copy(bc3[32:64, :], bc_mid[32:64, :]).then_inc(s["bc3_sb"], 1)

                def times_c(n):
                    dve.wait_ge(s["h_sb"], 1 + g * 2 * NST + 2 * n + 2)
                    dve.wait_ge(s["c_ps"], g * NST + n + 1)
                    dve.wait_ge(s["y_sum"], 1 + g * NST + max(0, n - 1))
                    TT(hc[:, n % 2], hst[:, n % 2], bank[2 + n % 2].unsqueeze(1).broadcast_to((P, 2, T)), ALU.mult).then_inc(s["hc_sb"], 1)

                for n in range(NST):
                    dve.wait_ge(s["hc_sb"], 1 + g * NST + max(0, n - 1))
                    for h in range(2):
                        dve.wait_ge(s["a_ps"], 1 + g * 2 * NST + 2 * n + h + 1)
                        dve.wait_ge(s["bu_sb"], 1 + g * NST + n + 1)
                        v_.tensor_tensor_scan(hst[:, n % 2, h, :], bank[6 + h], bu[:, n % 2, h, :], 0.0, ALU.mult, ALU.add).then_inc(s["h_sb"], 1)
                    if n:
                        times_c(n - 1)
                times_c(NST - 1)
                dve.wait_ge(s["y_sum"], 1 + g * NST + NST)
                dve.wait_ge(s["sres_sb"], g * 2 + 2)
                TT(yg[:, :, :], y_ps, sres[:, :, :], ALU.mult).then_inc(s["yg_sb"], 1)
                dve.wait_ge(s["o_ps"], g + 1)
                layer_norm(bank[0].rearrange("p (s d) -> p s d", s=S), xn[:, :, :], x1, g, 0,
                           ("ln_sum", "ln_stat", "ln_var", "ln_rstd", "x1_sb"), 2)
                for i, (bk, _n) in enumerate(((2, 0), (3, 1), (4, 2), (5, 3))):
                    dve.wait_ge(s["proj_ps"], g * 4 + i + 1)
                    TT(rot[:, i, :].rearrange("p (s t) -> p s t", s=S), bank[bk].rearrange("p (s t) -> p s t", s=S),
                       rope[:, i, :].unsqueeze(1).broadcast_to((P, S, L)), ALU.mult).then_inc(s["rot_sb"], 1)

                def normed(t):
                    pv = bank[0][:, (t % 2) * 144:(t % 2) * 144 + 144].rearrange("p (h d) -> p h d", h=H)
                    dve.wait_ge(s["pv_ps"], g * 4 * S + 4 * t + 4)
                    v_.reciprocal(rden[:, t % 2, :], pv[:, :, HD]).then_inc(s["den_sb"], 1)
                    dve.wait_ge(s["den_sb"], g * S + t + 1)
                    TT(ao[:, t % 2], pv[:, :, 0:HD], rden[:, t % 2, :].unsqueeze(2).broadcast_to((P, H, HD)), ALU.mult).then_inc(s["ao_sb"], 1)

                for t in range(S):
                    for k in range(2):
                        sc = quad[:, 2 * k:2 * k + 2].rearrange("p j (c m) -> p (j c) m", c=4)
                        dve.wait_ge(s["s_ps"], 1 + g * 8 + 2 * t + k + 1)
                        v_.tensor_reduce(out=nmax[:, t % 2, 8 * k:8 * k + 8], in_=sc, axis=AX.X, op=ALU.max).then_inc(s["s_max"], 1)
                        dve.wait_ge(s["s_max"], g * 8 + 2 * t + k + 1)
                        if t >= 2:
                            dve.wait_ge(s["pT_ps"], g * 16 + 4 * (t - 2) + 4)
                        TT(prob[:, t % 2, 2 * k:2 * k + 2].rearrange("p j c m -> p (j c) m"), sc,
                           nmax[:, t % 2, 8 * k:8 * k + 8].unsqueeze(2).broadcast_to((P, 8, L)), ALU.subtract).then_inc(s["s_sub"], 1)
                    if t:
                        normed(t - 1)
                normed(S - 1)
                dve.wait_ge(s["wo_ps"], g + 1)
                dve.wait_ge(s["x1b_sb"], g + 1)
                dve.wait_ge(s["x2_sent"], 1 + g)
                layer_norm(bank[2].rearrange("p (s d) -> p s d", s=S), x1b[:, :, :], x2, g, 1,
                           ("ln_sum", "ln_stat", "ln_var", "ln_rstd", "x2_sb"), 2)
                c = [0]

                def link(ins):
                    c[0] += 1
                    ins.then_inc(s["route"], 1)
                    dve.wait_ge(s["route"], 1 + g * ROUTER_LINKS + c[0])

                def both(x):
                    return x.unsqueeze(2).broadcast_to((P, S, 2, E))

                dve.wait_ge(s["x2_sb"], g * S + S)
                link(v_.tensor_copy(x2_all[:, bass.ds(g * S, S), :], x2[:, :, :]))
                dve.wait_ge(s["lg_ps"], g + 1)
                link(v_.tensor_copy(lg[:, :, :], bank[1][:, 0:S * E].rearrange("p (s e) -> p s e", s=S)))
                plain(dve)
                for t in range(S):
                    last = v_.max(m8[:, t, :], lg[:, t, :])
                link(last)
                plain(dve)
                for t in range(S):
                    last = v_.max_index(i8[:, t, :], m8[:, t, :], lg[:, t, :])
                link(last)
                link(v_.tensor_copy(idxf[:, :, :], i8[:, :, 0:2]))
                link(TT(oh[:, :, :, :], iota8[:, :].unsqueeze(1).unsqueeze(1).broadcast_to((P, S, 2, E)),
                        idxf[:, :, :].unsqueeze(3).broadcast_to((P, S, 2, E)), ALU.is_equal))
                link(TT(ohb[:, :, :], oh[:, :, 0, :], oh[:, :, 1, :], ALU.add))
                link(v_.scalar_tensor_tensor(lab[:, :, :], lg[:, :, :], -1.0, lg[:, :, :], ALU.mult, ALU.max))
                mm = m8[:, :, 0:2].unsqueeze(3).broadcast_to((P, S, 2, E))
                link(TT(fac[:, :, :, :], both(lab[:, :, :]), mm, ALU.max))
                link(TT(gap[:, :, :, :], mm, both(lg[:, :, :]), ALU.subtract))
                link(v_.tensor_scalar(thr[:, :, :, :], fac[:, :, :, :], 0.02, None, ALU.mult))
                link(TT(keep[:, :, :, :], thr[:, :, :, :], gap[:, :, :, :], ALU.is_ge))
                c[0] = 12
                link(TT(keep[:, :, 1, :], keep[:, :, 1, :], oh[:, :, 0, :], ALU.is_gt))
                dve.wait_ge(s["gexp_sb"], g + 1)
                link(v_.tensor_scalar(gexp[:, :, :, :], gexp[:, :, :, :], 1.0, None, ALU.min))
                link(TT(gexp[:, :, :, :], gexp[:, :, :, :], keep[:, :, :, :], ALU.mult))
                link(v_.tensor_reduce(out=gsum[:, :, :], in_=gexp[:, :, :, :], axis=AX.X, op=ALU.add))
                link(v_.reciprocal(gates_all[:, bass.ds(g * S, S), :], gsum[:, :, :]))
                dve.wait_ge(s["rank_ps"], g + 1)
                rk = bank[7][:, 0:(S + 1) * E].rearrange("p (s e) -> p s e", e=E)
                link(TT(rank[:, :, :], rk[:, 0:S, :], base[:, :].unsqueeze(1).broadcast_to((P, S, E)), ALU.add))
                link(TT(base[:, :], base[:, :], rk[:, S, :], ALU.add))
                link(TT(prk[:, :, :, :], both(rank[:, :, :]), oh[:, :, :, :], ALU.mult))
                link(v_.tensor_reduce(out=posf[:, :, :], in_=prk[:, :, :, :], axis=AX.X, op=ALU.add))
                assert c[0] == ROUTER_LINKS
                v_.tensor_copy(posf_all[:, bass.ds(g * S, S), :], posf[:, :, :])
                v_.tensor_copy(idxf_all[:, bass.ds(g * S, S), :], idxf[:, :, :])
                v_.tensor_copy(pos[:, :, :], posf[:, :, :]).then_inc(s["pos_sb"], 1)

            v_.tensor_scalar(tail_f[:, :], base[:, :], pcol[:, 0:1], None, ALU.add).then_inc(s["tail"], 1)
            dve.wait_ge(s["tail"], 1)
            v_.tensor_copy(tail_i[:, :], tail_f[:, :]).then_inc(s["tail"], 1)
            k = [0]

            def tlink(ins):
                k[0] += 1
                ins.then_inc(s["table_link"], 1)
                dve.wait_ge(s["table_link"], k[0])

            N2 = NT + 4
            tlink(TT(cnt[:, :], base[:, :], erow[:, :], ALU.subtract))
            tlink(TT(full[:, :, :], cnt[:, :].unsqueeze(2).broadcast_to((P, E, B)), k128[:, :].unsqueeze(1).broadcast_to((P, E, B)), ALU.is_gt))
            tlink(v_.tensor_reduce(out=ntile[:, :], in_=full[:, :, :], axis=AX.X, op=ALU.add))
            tlink(v_.tensor_tensor_scan(cum[:, :], ones8[:, :], ntile[:, :], 0.0, ALU.mult, ALU.add))
            tlink(v_.tensor_scalar(lastt[:, :], cum[0:1, E - 1:E], -1.0, None, ALU.add))
            tlink(v_.tensor_scalar(jc[:, :], jrow[:, :], lastt[:, 0:1], None, ALU.min))
            tlink(TT(ind[:, :, :], jc[:, :].unsqueeze(2).broadcast_to((1, N2, E)), cum[0:1, :].unsqueeze(1).broadcast_to((1, N2, E)), ALU.is_ge))
            tlink(v_.tensor_reduce(out=t_e[:, :], in_=ind[:, :, :], axis=AX.X, op=ALU.add))
            tlink(v_.tensor_scalar(jump[:, :], ntile[0:1, :], float(-P), float(STRIDE), ALU.mult, ALU.add))
            tlink(TT(wsum[:, :, :], ind[:, :, :], jump[:, :].unsqueeze(1).broadcast_to((1, N2, E)), ALU.mult))
            tlink(v_.tensor_reduce(out=t_row[:, :], in_=wsum[:, :, :], axis=AX.X, op=ALU.add))
            tlink(v_.tensor_scalar(t_tmp[:, :], jc[:, :], float(P), None, ALU.mult))
            tlink(TT(t_row[:, :], t_row[:, :], t_tmp[:, :], ALU.add))
            tlink(v_.tensor_copy(table[:, 0, :], t_e[:, :]))
            v_.tensor_copy(table[:, 1, :], t_row[:, :]).then_inc(s["table_sb"], 1)
            tlink(TT(shift[:, :], cum[:, :], ntile[:, :], ALU.subtract))
            tlink(v_.tensor_scalar(shift[:, :], shift[:, :], float(P), None, ALU.mult))
            tlink(TT(shift[:, :], shift[:, :], erow[:, :], ALU.subtract))
            for e in range(E):
                tlink(v_.tensor_scalar(part[:, :, :], idxf_all[:, :, :], float(e), shift[:, e:e + 1], ALU.is_equal, ALU.mult))
                tlink(TT(posf_all[:, :, :], posf_all[:, :, :], part[:, :, :], ALU.add))
            tlink(v_.tensor_copy(pos_all[:, :, :], posf_all[:, :, :]))

            def gate(j, b):
                dve.wait_ge(s["up_ps"], 1 + 2 * j + 2)
                dve.wait_ge(s["silu_sb"], j + 1)
                TT(gg[:, b, :], sl[:, b, :], bank[2 + b], ALU.mult).then_inc(s["gate_sb"], 1)

            gate(0, 0)
            with dve.Fori(0, NT // 2) as it:
                for b in range(2):
                    j = it * 2 + b
                    gate(j + 1, 1 - b)
                    dve.wait_ge(s["y_ps_s"], j + 1)
                    dve.wait_ge(s[f"y_store{b}"], 16 + it * 16)
                    v_.tensor_copy(ys[:, b, :], bank[6][:, b * P:(b + 1) * P]).then_inc(s["y_sb"], 1)
            with dve.Fori(0, G) as g:
                v_.tensor_copy(idx[:, :].rearrange("p (s k) -> p s k", s=S), pos_all[:, bass.ds(g * S, S), :]).then_inc(s["idx_sb"], 1)
                dve.wait_ge(s["gath"], (g + 1) * 2 * S * 16)
                for k in range(2):
                    for t in range(S):
                        src = x2_all[:, bass.ds(g * S + t, 1), :].rearrange("p a d -> p (a d)") if k == 0 else acc[:, t, :]
                        v_.scalar_tensor_tensor(acc[:, t, :], yk[:, 2 * t + k, :],
                                                gates_all[:, bass.ds(g * S + t, 1), k], src, ALU.mult, ALU.add).then_inc(s["acc_s"], 1)
                    dve.wait_ge(s["acc_s"], 1 + g * 2 * S + (k + 1) * S)
                dve.wait_ge(s["fin_store"], 16 + g * 16)
                for t in range(S):
                    last = v_.bn_stats(stats[:, t, :], acc[:, t, :])
                last.then_inc(s["f_stat"], 1)
                dve.wait_ge(s["f_stat"], g + 1)
                plain(dve)
                for t in range(S):
                    last = v_.bn_aggr(mv[:, t, :], stats[:, t, :])
                last.then_inc(s["f_var"], 1)
                dve.wait_ge(s["f_rstd"], g + 1)
                for t in range(S):
                    v_.tensor_scalar(fin[:, t, :], acc[:, t, :], mv[:, t, 0:1], rstd[:, t:t + 1], ALU.subtract, ALU.mult).then_inc(s["fin_sb"], 1)

        @block.tensor
        def _(pe):
            MM = nc.tensor.matmul
            TR = nc.tensor.transpose
            early(pe, "cT_ps s_ps xsT_ps up_ps y_sum")
            pe.wait_ge(s["w_load"], 16 * NW)
            pe.wait_ge(s["dve_const"], 7)

            with pe.Fori(0, G) as g:
                pe.wait_ge(s["x_load"], g * 16 + 16)
                pe.wait_ge(s["route"], 1 + g * ROUTER_LINKS)
                for t in range(S):
                    last = TR(bank[0][:, t * L:(t + 1) * L], xn[:, t, :], ident[:, :])
                last.then_inc(s["xT_ps"], 1)
                pe.wait_ge(s["xT_sb"], g + 1)
                for h in range(2):
                    for k in range(KCONV):
                        last = MM(bank[1 + h].rearrange("p (s t) -> p s t", s=S), w_conv[:, k, h * P:(h + 1) * P], xT[:, :, k:k + L],
                                  start=(k == 0), stop=(k == KCONV - 1))
                    last.then_inc(s["conv_ps"], 1)
                for h in range(2):
                    MM(bank[3 + h].rearrange("p (s t) -> p s t", s=S), w_in[:, DIN + h * P:DIN + (h + 1) * P], xT[:, :, KCONV - 1:],
                       start=True, stop=True).then_inc(s["res_ps"], 1)
                pe.wait_ge(s["u_sb"], g * 2 + 2)
                pe.wait_ge(s["pos_sb"], 1 + g)
                for h in range(2):
                    last = MM(bank[6][0:96, :], w_bc[:, h].rearrange("p r n -> p (r n)"), u[:, h, :], start=(h == 0), stop=(h == 1))
                last.then_inc(s["bc_ps"], 1)
                for h in range(2):
                    last = MM(bank[7][0:DTR, :], w_dtl[:, h, :], u[:, h, :], start=(h == 0), stop=(h == 1))
                last.then_inc(s["dtl_ps"], 1)
                pe.wait_ge(s["dtl_sb"], g + 1)
                for h in range(2):
                    MM(bank[1 + h], w_dt[:, h * P:(h + 1) * P], dtl[:, :], start=True, stop=True).then_inc(s["z_ps"], 1)
                pe.wait_ge(s["sres_sb"], g * 2 + 2)
                for h in range(2):
                    MM(bank[4 + h], d_diag[:, h, :], u[:, h, :], start=True, stop=False, skip_group_check=True)
                pe.wait_ge(s["bc3_sb"], g * 2 + 2)
                pe.wait_ge(s["zabs_sb"], g * 4 + 4)

                def row_b(n):
                    pe.wait_ge(s["b_sb"], 1 + g * NST + n)
                    MM(bank[1], sel[:, n, :], bc3[:, :], start=True, stop=True).then_inc(s["b_ps"], 1)

                def row_c(n):
                    pe.wait_ge(s["hc_sb"], 1 + g * NST + max(0, n - 1))
                    MM(bank[2 + n % 2], sel[:, NST + n, :], bc3[:, :], start=True, stop=True).then_inc(s["c_ps"], 1)

                for n in range(AHEAD):
                    row_b(n)
                row_c(0)
                for n in range(NST):
                    if n + 1 < NST:
                        row_c(n + 1)
                    if n + AHEAD < NST:
                        row_b(n + AHEAD)
                    pe.wait_ge(s["hc_sb"], 1 + g * NST + n + 1)
                    for h in range(2):
                        last = MM(bank[4 + h], ident[:, :], hc[:, n % 2, h, :], start=False, stop=(n == NST - 1), skip_group_check=True)
                    last.then_inc(s["y_sum"], 1)
                pe.wait_ge(s["yg_sb"], g + 1)
                for t in range(S):
                    for h in range(2):
                        last = MM(bank[0][:, t * D:(t + 1) * D], yg[:, h, t * L:(t + 1) * L], w_out[:, h, :], start=(h == 0), stop=(h == 1))
                last.then_inc(s["o_ps"], 1)
                pe.wait_ge(s["ctx_load"], g * 16 + 16)
                for t in range(S):
                    last = TR(bank[1][:, t * L:(t + 1) * L], cn[:, t, :], ident[:, :])
                last.then_inc(s["cT_ps"], 1)
                pe.wait_ge(s["cT_sb"], g + 1)
                MM(bank[4], wkT[:, :], cT[:, :], start=True, stop=True)
                MM(bank[5], wkrT[:, :], cT[:, :], start=True, stop=True)
                for t in range(S):
                    last = MM(bank[6][:, t * D:(t + 1) * D], cT[:, t * L:(t + 1) * L], wvT[:, :], start=True, stop=True)
                last.then_inc(s["v_ps"], 1)
                pe.wait_ge(s["x1_sb"], g * S + S)
                for t in range(S):
                    last = TR(bank[0][:, t * L:(t + 1) * L], x1[:, t, :], ident[:, :])
                last.then_inc(s["x1T_ps"], 1)
                pe.wait_ge(s["x1T_sb"], g + 1)
                MM(bank[2], wqT[:, :], x1T[:, :], start=True, stop=True).then_inc(s["proj_ps"], 1)
                MM(bank[3], wqrT[:, :], x1T[:, :], start=True, stop=True).then_inc(s["proj_ps"], 3)
                pe.wait_ge(s["rot_sb"], g * 4 + 4)
                pe.wait_ge(s["mask_sb"], g + 1)

                def scores(t):
                    for k in range(2):
                        pe.wait_ge(s["s_sub"], 1 + g * 8 + max(0, 2 * t + k - 1))
                        for j in (2 * k, 2 * k + 1):
                            MM(bank[2 + j].rearrange("p (c m) -> p c m", c=4), identb[:, :],
                               mbias[:, t, :].unsqueeze(1).broadcast_to((P, 4, L)), start=True, stop=False, skip_group_check=True)
                        if t == 0 and k == 0:
                            pe.wait_ge(s["qk_al"], g * 64 + 64)
                        for c in range(4):
                            for j in (2 * k, 2 * k + 1):
                                r = slice(32 * j, 32 * j + HD)
                                last = MM(bank[2 + j][:, c * L:(c + 1) * L], q_al[r, c, t * L:(t + 1) * L], k_al[r, c, t * L:(t + 1) * L],
                                          start=False, stop=True, skip_group_check=True)
                        last.then_inc(s["s_ps"], 1)

                def head_t(t, j):
                    pe.wait_ge(s["p_sb"], g * 8 + 2 * t + j // 2 + 1)
                    pe.wait_ge(s["pT_sb"], 1 + g * 16 + max(0, 4 * t + j - 1))
                    for c in range(4):
                        last = TR(bank[6 + j % 2][:, c * L:(c + 1) * L], prob[:, t % 2, j, c, :], ident[:, :])
                    last.then_inc(s["pT_ps"], 1)

                def head_v(t, j):
                    pe.wait_ge(s["pT_sb"], 1 + g * 16 + 4 * t + j + 1)
                    if j == 0 and t:
                        pe.wait_ge(s["ao_sb"], g * S + t)
                    for c in range(4):
                        hh = 4 * c + j
                        o = (t % 2) * 144 + hh * 9
                        last = MM(bank[0][:, o:o + 9], pT[:, j % 2, c, :], v_ext[:, t, hh, :], start=True, stop=True)
                    last.then_inc(s["pv_ps"], 1)

                def ao_t(t):
                    pe.wait_ge(s["ao_sb"], g * S + t + 1)
                    TR(bank[1][:, t * L:(t + 1) * L], ao[:, t % 2].rearrange("p h d -> p (h d)"), ident[:, :]).then_inc(s["aoT_ps"], 1)

                pe.wait_ge(s["v_sb"], g + 1)
                scores(0)
                for t in range(S):
                    if t + 1 < S:
                        scores(t + 1)
                    head_t(t, 0)
                    for j in range(4):
                        if j + 1 < 4:
                            head_t(t, j + 1)
                        head_v(t, j)
                    if t:
                        ao_t(t - 1)
                ao_t(S - 1)
                pe.wait_ge(s["aoT_sb"], g + 1)
                for t in range(S):
                    last = MM(bank[2][:, t * D:(t + 1) * D], aoT[:, t * L:(t + 1) * L], woT[:, :], start=True, stop=True)
                last.then_inc(s["wo_ps"], 1)
                pe.wait_ge(s["x2_sb"], g * S + S)
                for t in range(S):
                    last = TR(bank[0][:, t * L:(t + 1) * L], x2[:, t, :], ident[:, :])
                last.then_inc(s["x2T_ps"], 1)
                pe.wait_ge(s["x2T_sb"], g + 1)
                for t in range(S):
                    last = MM(bank[1][:, t * E:(t + 1) * E], x2T[:, t * L:(t + 1) * L], gate_wT[:, :], start=True, stop=True)
                last.then_inc(s["lg_ps"], 1)
                pe.wait_ge(s["route"], 1 + g * ROUTER_LINKS + 7)
                for t in range(S + 1):
                    o = bank[7][:, t * E:(t + 1) * E]
                    for r in range(t):
                        last = MM(o, ones_b[:, :], ohb[:, r, :], start=(r == 0), stop=(t == S and r == S - 1))
                    if t < S:
                        last = MM(o, tri[:, :], ohb[:, t, :], start=(t == 0), stop=True)
                last.then_inc(s["rank_ps"], 1)

            def rows_t(j, b, turn, load):
                pe.wait_ge(s[f"xs_load{load}"], turn * 16 + 16)
                pe.wait_ge(s["xsT_sb"], j)
                TR(bank[7][:, b * P:(b + 1) * P], xs[:, load, :], ident[:, :]).then_inc(s["xsT_ps"], 1)

            def up(j, b):
                e = pe.value_load(table[0:1, 0, bass.ds(j, 1)], min_val=0, max_val=E - 1)
                pe.wait_ge(s["xsT_sb"], j + 1)
                MM(bank[b], xsT[:, b, :], w1[:, bass.ds(e, 1), :].rearrange("p a f -> p (a f)"), start=True, stop=True).then_inc(s["up_ps"], 1)
                MM(bank[2 + b], xsT[:, b, :], w3[:, bass.ds(e, 1), :].rearrange("p a f -> p (a f)"), start=True, stop=True).then_inc(s["up_ps"], 1)

            def gated_t(j, b):
                pe.wait_ge(s["gate_sb"], 1 + j + 1)
                for c in range(FC):
                    last = TR(bank[4 + b][:, c * P:(c + 1) * P], gg[:, b, c * P:(c + 1) * P], ident[:, :])
                last.then_inc(s["gT_ps"], 1)

            def down(j, b):
                e = pe.value_load(table[0:1, 0, bass.ds(j, 1)], min_val=0, max_val=E - 1)
                pe.wait_ge(s["gT_sb"], j + 1)
                pe.wait_ge(s["y_sb"], 1 + j)
                for c in range(FC):
                    last = MM(bank[6][:, b * P:(b + 1) * P], gT[:, b, c, :], w2[:, bass.ds(e, 1), c, :].rearrange("p a d -> p (a d)"),
                              start=(c == 0), stop=(c == FC - 1))
                last.then_inc(s["y_ps_s"], 1)

            pe.wait_ge(s["table_sb"], 1)
            pe.wait_ge(s["w2_load"], 16)
            rows_t(0, 0, 0, 0)
            rows_t(1, 1, 0, 1)
            up(0, 0)
            gated_t(0, 0)
            with pe.Fori(0, NT // 4) as it:
                for b in range(4):
                    j = it * 4 + b
                    rows_t(j + 2, b % 2, it + (b + 2) // 4, (b + 2) % 4)
                    up(j + 1, 1 - b % 2)
                    down(j, b % 2)
                    gated_t(j + 1, 1 - b % 2)


def kernel(**inputs):
    import numpy as np
    import concourse.bacc as bacc
    from concourse import mybir as mb
    from concourse.bass_utils import run_bass_kernel_spmd as run

    c = np.ascontiguousarray
    i = {k.replace("L0_attn_", "").replace("L0_xattn_", "").replace("L0_ffn_", ""): np.asarray(v) for k, v in inputs.items()}

    def halves(w):
        return c(np.moveaxis(w.reshape((2, 128) + w.shape[1:]), 0, 1))

    order = np.arange(128).reshape(4, 4, HD).transpose(1, 0, 2).reshape(128)
    swap = np.arange(128).reshape(64, 2)[:, ::-1].reshape(128)
    theta = (1.0 / np.float32(10000.0) ** (np.arange(0, HD, 2, dtype=np.float32) / np.float32(HD))).astype(np.float32)
    ang = (np.arange(L, dtype=np.float32)[:, None] * theta[None, :]).astype(np.float32)
    cos = np.repeat(np.tile(np.cos(ang).T, (H, 1)), 2, axis=0)
    sin = np.repeat(np.tile(np.sin(ang).T, (H, 1)), 2, axis=0)
    sin[0::2] *= -1
    scale = np.float32(1.0 / np.sqrt(np.float32(HD)))
    rope = np.stack([cos * scale, sin * scale, cos, sin], axis=1).astype(np.float32)[order]
    arrays = {
        "x": c(i["x"]), "ctx_1024": c(i["ctx_1024"]), "mask": c(i["mask_BxS2_if1"].reshape(-1)),
        "W_in": c(i["W_in"]), "conv_w": c(i["conv_w"][:, 0, :].T), "conv_b": halves(i["conv_b"]),
        "W_x": halves(i["W_x"]), "W_dt": c(i["W_dt"]), "b_dt": halves(i["b_dt"]), "W_out": halves(i["W_out"]),
        "A_log": halves(i["A_log"]), "D": halves(i["D"]),
        "WqT": c(i["Wq"].T[:, order]), "WqrT": c(i["Wq"].T[:, swap[order]]),
        "WkT": c(i["Wk"].T[:, order]), "WkrT": c(i["Wk"].T[:, swap[order]]),
        "WvT": c(i["Wv"].T), "WoT": c(i["Wo"].T), "bo": c(i["bo"]), "rope": c(rope),
        "gate_wT": c(i["gate_w"].T), "w1T": c(i["w1"].transpose(2, 0, 1)), "w3T": c(i["w3"].transpose(2, 0, 1)),
        "w2T": c(i["w2"].transpose(2, 0, 1).reshape(FC, P, E, D).transpose(1, 2, 0, 3)),
    }
    nc = bacc.Bacc("TRN2", target_bir_lowering=False, num_devices=1)
    aps = {k: nc.dram_tensor(f"in_{k}", v.shape, mb.dt.from_np(v.dtype), kind="ExternalInput").ap() for k, v in arrays.items()}
    o = nc.dram_tensor("out_0", (B, L, D), mb.dt.float32, kind="ExternalOutput").ap()
    build(nc, aps, o)
    r = run(nc, [{f"in_{k}": v for k, v in arrays.items()}], core_ids=[0])
    return r.results[0]["out_0"]
```

```python
import concourse.bass as bass
from concourse import mybir
from contextlib import ExitStack

F32 = mybir.dt.float32
BF16 = mybir.dt.bfloat16
I32 = mybir.dt.int32
U32 = mybir.dt.uint32
ALU = mybir.AluOpType
ACT = mybir.ActivationFunctionType
AX = mybir.AxisListType

P = 128
B, L, D = 32, 128, 128
S = 4
G = B // S
T = S * L
DIN, NST, DTR, KCONV = 256, 16, 64, 4
H, HD = 16, 8
AHEAD = 3
E, F = 8, 512
FC = F // P
STRIDE = B * L + P
NT = (2 * B * L + E * (P - 1)) // P + 1
NT += -NT % 4
EPS = 1e-5
NEG = -1e30
RESET = 1e25
ROUTER_LINKS = 21


def build(nc, a, out):
    ctx = ExitStack()
    with ctx:
        def sb(name, shape, dt=F32):
            return ctx.enter_context(nc.sbuf_tensor(name, shape, dt))

        def sem(name):
            return ctx.enter_context(nc.semaphore(name))

        ident = sb("ident", [P, P])
        identb = sb("identb", [P, P], BF16)
        w_in = sb("w_in", [P, 2 * DIN])
        w_conv = sb("w_conv", [P, KCONV, DIN])
        conv_b = sb("conv_b", [P, 2])
        w_dtl = sb("w_dtl", [P, 2, DTR])
        w_bc = sb("w_bc", [P, 2, 3, 2 * NST])
        w_dt = sb("w_dt", [DTR, DIN])
        b_dt = sb("b_dt", [P, 2])
        w_out = sb("w_out", [P, 2, D])
        a_log = sb("a_log", [P, 2, NST])
        a_neg = sb("a_neg", [P, 2, NST])
        d_col = sb("d_col", [P, 2])
        d_diag = sb("d_diag", [P, 2, P])
        sel32 = sb("sel32", [96, 2 * NST])
        sel = sb("sel", [96, 2 * NST, P], BF16)
        wqT = sb("wqT", [P, P])
        wqrT = sb("wqrT", [P, P])
        wkT = sb("wkT", [P, P])
        wkrT = sb("wkrT", [P, P])
        wvT = sb("wvT", [P, P])
        woT = sb("woT", [P, P])
        bo_b = sb("bo_b", [P, P])
        rope = sb("rope", [P, 4, L])
        causal = sb("causal", [P, L])
        mask_b = sb("mask_b", [P, T], I32)
        gate_wT = sb("gate_wT", [P, E])
        w1 = sb("w1", [P, E, F])
        w3 = sb("w3", [P, E, F])
        eps_col = sb("eps_col", [P, 1])
        one_col = sb("one_col", [P, 1])
        iota8 = sb("iota8", [P, E])
        hot = sb("hot", [P, H])
        own = sb("own", [P, 4])
        tri = sb("tri", [P, P], BF16)
        ones_b = sb("ones_b", [P, P], BF16)
        zrow = sb("zrow", [P, D])

        xn = sb("xn", [P, S, D])
        xT = sb("xT", [P, S, KCONV - 1 + L])
        u = sb("u", [P, 2, T])
        sres = sb("sres", [P, 2, T])
        bc3 = sb("bc3", [96, T], BF16)
        bc_rest = sb("bc_rest", [96, T])
        bc_mid = sb("bc_mid", [96, T], BF16)
        dtl = sb("dtl", [DTR, T])
        zabs = sb("zabs", [P, 2, T])
        zpos = sb("zpos", [P, 2, T])
        delta = sb("delta", [P, 2, T])
        du = sb("du", [P, 2, T])
        b_row = sb("b_row", [P, AHEAD + 1, T])
        scan = sb("scan", [P, 2, 2, 2, T])
        bu = scan[:, 0]
        hst = scan[:, 1]
        hc = sb("hc", [P, 2, 2, T])
        yg = zabs
        sx = sb("sx", [P, S, D])
        stats = sb("stats", [P, S, 6])
        mv = sb("mv", [P, S, 2])
        lnv = sb("lnv", [P, S])
        rstd = sb("rstd", [P, S])
        x1 = sb("x1", [P, S, D])
        x1b = sb("x1b", [P, S, D])
        cn = sb("cn", [P, S, D])
        x1T = sb("x1T", [P, T])
        cT = sb("cT", [P, T])
        rot = sb("rot", [P, 4, T])
        conv_taps = rot[:, 0:2, :].rearrange("p a t -> p (a t)").rearrange("p (k c) -> p k c", k=KCONV)
        qk = sb("qk", [P, 2, T])
        k_heads = scan[:, 0].rearrange("p a b t -> p (a b) t")
        ao_own = scan[:, 1, 0].rearrange("p b (j q) -> p b j q", j=4)
        v = sb("v", [P, S, D])
        pad = sb("pad", [P, T])
        mbias = sb("mbias", [P, S, L], BF16)
        smax = sb("smax", [P, 2, H])
        nmax = sb("nmax", [P, 2, H])
        den = sb("den", [P, 2, H])
        prob = sb("prob", [P, 2, 4, 4, L])
        w2 = prob[:, :, :, :, :].rearrange("p a j c m -> p (a j) c m")
        pT = sb("pT", [P, 2, 4, L])
        rden = sb("rden", [P, 2, H])
        aoT = sb("aoT", [P, T])
        x2 = sb("x2", [P, S, D])
        x2_all = sb("x2_all", [P, B, D])
        x2T = sb("x2T", [P, T])
        lg = sb("lg", [P, S, E])
        m8 = sb("m8", [P, S, 8])
        i8 = sb("i8", [P, S, 8], U32)
        idxf = sb("idxf", [P, S, 2])
        oh = sb("oh", [P, S, 2, E])
        ohb = sb("ohb", [P, S, E], BF16)
        lab = sb("lab", [P, S, E])
        fac = sb("fac", [P, S, 2, E])
        gap = sb("gap", [P, S, 2, E])
        thr = sb("thr", [P, S, 2, E])
        keep = sb("keep", [P, S, 2, E])
        gexp = sb("gexp", [P, S, 2, E])
        gsum = sb("gsum", [P, S, 2])
        gates_all = sb("gates_all", [P, B, 2])
        base = sb("base", [P, E])
        rank = sb("rank", [P, S, E])
        prk = sb("prk", [P, S, 2, E])
        posf = sb("posf", [P, S, 2])
        pos = sb("pos", [P, S, 2], I32)
        posf_all = sb("posf_all", [P, B, 2])
        idxf_all = sb("idxf_all", [P, B, 2])
        shift = sb("shift", [P, E])
        part = sb("part", [P, B, 2])
        pos_all = sb("pos_all", [P, B, 2], I32)
        tail_f = sb("tail_f", [P, E])
        tail_i = sb("tail_i", [P, E], I32)
        pcol = sb("pcol", [P, 1])
        erow = sb("erow", [P, E])
        cnt = sb("cnt", [P, E])
        k128 = sb("k128", [P, B])
        full = u[:, 0:2, :].rearrange("p h t -> p (h t)")[:, 0:(E) * B].rearrange("p (a b) -> p a b", b=B)
        ntile = sb("ntile", [P, E])
        ones8 = sb("ones8", [P, E])
        cum = sb("cum", [P, E])
        lastt = sb("lastt", [1, 1])
        jrow = sb("jrow", [1, NT + 8])
        jc = sb("jc", [1, NT + 8])
        ind = sres[0:1, 0:2, :].rearrange("p h t -> p (h t)")[:, 0:(NT + 8) * E].rearrange("p (a b) -> p a b", b=E)
        jump = sb("jump", [1, E])
        wsum = yg[0:1, 0:2, :].rearrange("p h t -> p (h t)")[:, 0:(NT + 8) * E].rearrange("p (a b) -> p a b", b=E)
        t_e = sb("t_e", [1, NT + 8])
        t_row = sb("t_row", [1, NT + 8])
        t_tmp = sb("t_tmp", [1, NT + 8])
        table = sb("table", [1, 2, NT + 8], I32)
        xs = qk[:, 0, :].rearrange("p (b d) -> p b d", b=4)
        xsT = qk[:, 1, 0:2 * P].rearrange("p (b n) -> p b n", b=2)
        sl = zabs
        gg = zpos
        gT = delta[:, :, :].rearrange("p b (c n) -> p b c n", c=FC)
        ys = aoT[:, 0:2 * D].rearrange("p (b d) -> p b d", b=2)
        idx = sb("idx", [P, 2, 2 * S], I32)
        yk = [x[:, :, :].rearrange("p k (s d) -> p (k s) d", s=S) for x in (du, u)]
        acc = sx
        fin = x1

        bank = [ctx.enter_context(nc.psum_tensor(f"bank{i}", [P, 512], F32)) for i in (0, 1)]
        quad = ctx.enter_context(nc.psum_tensor("quad", [P, 4, 512], F32))
        bank += [quad[:, i] for i in range(4)]
        pair = ctx.enter_context(nc.psum_tensor("pair", [P, 2, 512], F32))
        bank += [pair[:, i] for i in range(2)]
        bank = [b if i > 1 else b[:, :] for i, b in enumerate(bank)]
        y_ps = quad[:, 2:4]

        xg = nc.dram_tensor("xg", (E * STRIDE, D), F32, kind="Internal").ap()
        yl = nc.dram_tensor("yl", (NT * P, D), F32, kind="Internal").ap()

        names = """passed w_load w13_load pool_const dve_const act_const
        x_load ctx_load mask_load w2_load xT_ps xT_sb conv_ps res_ps u_sb sres_sb bc_ps dtl_ps bc_hi bc_res1 bc_mid_s bc3_sb dtl_sb
        z_ps zabs_sb zexp_sb softp delta_sb du_sb delta_set
        b_ps b_sb bu_sb a_ps h_sb c_ps hc_sb y_sum yg_sb o_ps
        ln_sum ln_stat ln_var ln_log ln_rstd x1_sb x1b_sb x1T_ps x1T_sb cT_ps cT_sb proj_ps v_ps v_sb rot_sb qk_sb k_heads_sb
        pad_sb mask_sb s_ps s_max s_neg p_sb rden_sb pn_sb pT_ps pT_sb pv_ps ao_own_sb aoT_sb wo_ps
        x2_sb x2T_ps x2T_sb lg_ps route gexp_sb rank_ps pos_sb scat x2_sent
        tail tail_scat table_sb table_link
        xs_load0 xs_load1 xs_load2 xs_load3 xsT_ps xsT_sb up_ps silu_sb gate_sb gT_ps gT_sb y_ps_s y_sb y_store0 y_store1
        idx_sb gath0 gath1 acc_s f_sum f_stat f_var f_log f_rstd fin_sb fin_store""".split()
        s = {n: sem(n) for n in names}

        xr = a["x"].rearrange("(g s) t d -> g t s d", s=S)
        cr = a["ctx_1024"].rearrange("(g s) t d -> g t s d", s=S)
        mr = a["mask"].rearrange("(g t) -> g t", t=T)
        outr = out.rearrange("(g s) t d -> g t s d", s=S)
        block = ctx.enter_context(nc.Block())

        W_LOADS = []

        def load(dst, src):
            W_LOADS.append((dst, src))

        load(w_in[:, :], a["W_in"])
        load(conv_taps, a["conv_w"].partition_broadcast(P))
        load(conv_b[:, :], a["conv_b"])
        load(w_dtl[:, :, :], a["W_x"][:, :, 0:DTR])
        for r in range(3):
            load(w_bc[:, :, r, :], a["W_x"][:, :, DTR:DTR + 2 * NST])
        load(w_dt[:, :], a["W_dt"])
        load(b_dt[:, :], a["b_dt"])
        load(w_out[:, :, :], a["W_out"])
        load(a_log[:, :, :], a["A_log"])
        load(d_col[:, :], a["D"])
        for dst, n in ((wqT, "WqT"), (wqrT, "WqrT"), (wkT, "WkT"), (wkrT, "WkrT"), (wvT, "WvT"), (woT, "WoT")):
            load(dst[:, :], a[n])
        load(bo_b[:, :], a["bo"].partition_broadcast(P))
        load(rope[:, :, :], a["rope"])
        load(gate_wT[:, :], a["gate_wT"])
        NW = len(W_LOADS)

        def early(eng, which):
            for n in which.split():
                eng.sem_inc(s[n], 16 if n in ("y_store0", "y_store1", "fin_store") else 1)

        def plain(eng):
            eng.sem_inc(s["passed"], 1)

        @block.sync
        def _(sp):
            early(sp, "y_store0 y_store1 fin_store")
            sp.dma_start(xn[:, :, :], xr[0]).then_inc(s["x_load"], 16)
            for dst, src in W_LOADS:
                sp.dma_start(dst, src).then_inc(s["w_load"], 16)

            def group_in(g, dst, src, count):
                sp.dma_start(dst[:, :, :], src[bass.ds(g, 1)].rearrange("g t s d -> (g t) s d")).then_inc(s[count], 16)

            def mask_in(g):
                sp.dma_start(mask_b[:, :], mr[bass.ds(g, 1)].rearrange("a t -> (a t)").partition_broadcast(P)).then_inc(s["mask_load"], 16)

            group_in(0, cn, cr, "ctx_load")
            mask_in(0)
            for dst, src in ((w1, a["w1T"]), (w3, a["w3T"])):
                sp.dma_start(dst[:, :, :], src).then_inc(s["w13_load"], 16)
            with sp.Fori(0, G - 1) as g:
                sp.wait_ge(s["cT_ps"], g + 1)
                plain(sp)
                group_in(g + 1, cn, cr, "ctx_load")
                sp.wait_ge(s["ln_sum"], 1 + g * 2 + 1)
                plain(sp)
                group_in(g + 1, xn, xr, "x_load")
                sp.wait_ge(s["pad_sb"], 1 + g + 1)
                plain(sp)
                mask_in(g + 1)
            sp.wait_ge(s["pv_ps"], G * 4 * S)
            sp.dma_start(w2, a["w2T"]).then_inc(s["w2_load"], 16)
            sp.wait_ge(s["table_sb"], 1)
            sp.wait_ge(s["scat"], G * 2 * S * 16)
            sp.wait_ge(s["tail_scat"], E * 16)

            def rows_in(j, b):
                r = sp.value_load(table[0:1, 1, bass.ds(j, 1)], min_val=0, max_val=E * STRIDE - P)
                sp.dma_start(xs[:, b, :], xg[bass.ds(r, P), :]).then_inc(s[f"xs_load{b}"], 16)

            for j in range(4):
                rows_in(j, j)
            for j in range(3):
                sp.wait_ge(s["xsT_ps"], 1 + j + 1)
                rows_in(j + 4, j)
            with sp.Fori(0, NT // 4) as it:
                for b in range(4):
                    j = it * 4 + b
                    sp.wait_ge(s["xsT_ps"], 1 + j + 4)
                    plain(sp)
                    rows_in(j + 7, (b + 3) % 4)
                    sp.wait_ge(s["y_sb"], 1 + j + 1)
                    plain(sp)
                    sp.dma_start(yl[bass.ds(j * P, P), :], ys[:, b % 2, :]).then_inc(s[f"y_store{b % 2}"], 16)
            with sp.Fori(0, G) as g:
                sp.wait_ge(s["fin_sb"], g * S + S)
                plain(sp)
                sp.dma_start(outr[bass.ds(g, 1)].rearrange("g t s d -> (g t) s d"), fin[:, :, :]).then_inc(s["fin_store"], 16)
            sp.wait_ge(s["fin_store"], 16 + 16 * G)

        @block.gpsimd
        def _(pool):
            g_ = nc.gpsimd
            early(pool, "pad_sb delta_sb bu_sb x2_sent")
            cs = [0]

            def link(ins):
                cs[0] += 1
                ins.then_inc(s["pool_const"], 1)
                pool.wait_ge(s["pool_const"], cs[0])

            pool.wait_ge(s["w_load"], 16 * NW)
            link(g_.memset(ident[:, :], 0.0))
            link(g_.affine_select(out=ident[:, :], in_=ident[:, :], compare_op=ALU.not_equal, fill=1.0, base=0,
                                  pattern=[[-1, P]], channel_multiplier=1))
            link(g_.memset(causal[:, :], 0.0))
            link(g_.affine_select(out=causal[:, :], in_=causal[:, :], compare_op=ALU.is_ge, fill=NEG, base=0,
                                  pattern=[[-1, L]], channel_multiplier=1))
            link(g_.memset(ones_b[:, :], 1.0))
            link(g_.affine_select(out=tri[:, :], in_=ones_b[:, :], compare_op=ALU.is_gt, fill=0.0, base=0,
                                  pattern=[[1, P]], channel_multiplier=-1))
            link(g_.memset(zrow[:, :], 0.0))
            link(g_.memset(xT[:, :, :], 0.0))
            link(g_.memset(eps_col[:, :], EPS))
            link(g_.memset(one_col[:, :], 1.0))
            link(g_.memset(ones8[:, :], 1.0))
            link(g_.iota(iota8[:, :], pattern=[[1, E]], base=0, channel_multiplier=0, allow_small_or_imprecise_dtypes=True))
            link(g_.iota(base[:, :], pattern=[[STRIDE, E]], base=0, channel_multiplier=0, allow_small_or_imprecise_dtypes=True))
            link(g_.iota(erow[:, :], pattern=[[STRIDE, E]], base=0, channel_multiplier=0, allow_small_or_imprecise_dtypes=True))
            link(g_.iota(pcol[:, :], pattern=[[1, 1]], base=0, channel_multiplier=1, allow_small_or_imprecise_dtypes=True))
            link(g_.iota(k128[:, :], pattern=[[P, B]], base=0, channel_multiplier=0, allow_small_or_imprecise_dtypes=True))
            link(g_.iota(jrow[:, :], pattern=[[1, NT + 8]], base=0, channel_multiplier=0, allow_small_or_imprecise_dtypes=True))

            def work(g):
                pool.wait_ge(s["softp"], g + 1)
                pool.wait_ge(s["a_ps"], 1 + g * 2 * NST)
                g_.tensor_tensor(delta[:, :, :], zpos[:, :, :], zabs[:, :, :], ALU.add).then_inc(s["delta_sb"], 1)
                pool.wait_ge(s["delta_sb"], 1 + g + 1)
                g_.tensor_tensor(du[:, :, :], delta[:, :, :], u[:, :, :], ALU.mult).then_inc(s["du_sb"], 1)
                pool.wait_ge(s["du_sb"], g + 1)
                plain(pool)
                for h in range(2):
                    last = g_.memset(delta[:, h, :].rearrange("p (s t) -> p s t", s=S)[:, :, 0:1], RESET)
                    last.then_inc(s["delta_set"], 1)
                for n in range(NST):
                    pool.wait_ge(s["b_sb"], 1 + g * NST + n + 1)
                    pool.wait_ge(s["h_sb"], 1 + g * 2 * NST + max(0, 2 * n - 2))
                    g_.tensor_tensor(bu[:, n % 2], du[:, :, :], b_row[:, n % (AHEAD + 1), :].unsqueeze(1).broadcast_to((P, 2, T)),
                                     ALU.mult).then_inc(s["bu_sb"], 1)
                pool.wait_ge(s["mask_load"], g * 16 + 16)
                plain(pool)
                g_.tensor_scalar(pad[:, :], mask_b[:, :], 0.0, NEG, ALU.is_equal, ALU.mult).then_inc(s["pad_sb"], 1)
                pool.wait_ge(s["pad_sb"], 1 + g + 1)
                pool.wait_ge(s["s_ps"], 1 + g * 8)
                g_.tensor_tensor(mbias[:, :, :], pad[:, :].rearrange("p (s t) -> p s t", s=S),
                                 causal[:, :].unsqueeze(1).broadcast_to((P, S, L)), ALU.add).then_inc(s["mask_sb"], 1)
                for i in (1, 0):
                    pool.wait_ge(s["rot_sb"], g * 4 + 4 - 2 * i)
                    g_.tensor_tensor(qk[:, i, :], rot[:, 2 * i, :], rot[:, 2 * i + 1, :], ALU.add).then_inc(s["qk_sb"], 1)
                pool.wait_ge(s["x1_sb"], g * S + S)
                pool.wait_ge(s["ln_sum"], 1 + g * 2)
                g_.tensor_tensor(x1b[:, :, :], x1[:, :, :], bo_b[:, :].unsqueeze(1).broadcast_to((P, S, D)), ALU.add).then_inc(s["x1b_sb"], 1)

            def scatter(g):
                pool.wait_ge(s["pos_sb"], 1 + g + 1)
                plain(pool)
                for t in range(S):
                    for k in range(2):
                        pool.indirect_dma_start(xg[:, :], bass.IndirectOffsetOnAxis(ap=pos[:, t, k:k + 1], axis=0),
                                                x2[:, t, :], None).then_inc(s["scat"], 16)
                pool.wait_ge(s["scat"], (g + 1) * 2 * S * 16)
                pool.sem_inc(s["x2_sent"], 1)

            work(0)
            with pool.Fori(1, G) as g:
                work(g)
                scatter(g - 1)
            scatter(G - 1)
            pool.wait_ge(s["tail"], 2)
            for e in range(E):
                pool.indirect_dma_start(xg[:, :], bass.IndirectOffsetOnAxis(ap=tail_i[:, e:e + 1], axis=0),
                                        zrow[:, :], None).then_inc(s["tail_scat"], 16)
            for b in range(2):
                pool.wait_ge(s[f"y_store{b}"], 16 + NT // 2 * 16)
            with pool.Fori(0, G // 2) as it:
                for b in range(2):
                    pool.wait_ge(s["idx_sb"], 2 * it + b + 1)
                    plain(pool)
                    for i in range(2 * S):
                        pool.indirect_dma_start(yk[b][:, i, :], None, yl[:, :],
                                                bass.IndirectOffsetOnAxis(ap=idx[:, b, i:i + 1], axis=0)).then_inc(s[f"gath{b}"], 16)

        @block.scalar
        def _(act):
            A = nc.scalar.activation
            early(act, "a_ps b_sb")
            act.wait_ge(s["w_load"], 16 * NW)
            act.wait_ge(s["pool_const"], 17)
            A(a_neg[:, :, :], a_log[:, :, :], ACT.Exp).then_inc(s["act_const"], 1)
            act.wait_ge(s["dve_const"], 9)

            def x_in(m):
                act.wait_ge(s["xT_ps"], m + 1)
                A(xT[:, :, KCONV - 1:], bank[7].rearrange("p (s t) -> p s t", s=S), ACT.Copy).then_inc(s["xT_sb"], 1)

            def silus(m):
                nc.scalar.preload_act_table_set("silu_and_others")
                for h in range(2):
                    act.wait_ge(s["conv_ps"], m * 2 + h + 1)
                    A(u[:, h, :], bank[h], ACT.Silu, bias=conv_b[:, h:h + 1]).then_inc(s["u_sb"], 1)
                for h in range(2):
                    act.wait_ge(s["res_ps"], m * 2 + h + 1)
                    A(sres[:, h, :], bank[6 + h], ACT.Silu).then_inc(s["sres_sb"], 1)
                nc.scalar.preload_act_table_set("natural_log_exp_and_others")

            def bc_hi(m):
                act.wait_ge(s["bc_ps"], m + 1)
                A(bc3[:, :], bank[0][0:96, :], ACT.Copy).then_inc(s["bc_hi"], 1)
                act.wait_ge(s["dtl_ps"], m + 1)
                A(dtl[:, :], bank[1][0:DTR, :], ACT.Copy).then_inc(s["dtl_sb"], 1)

            def bc_middle(m):
                act.wait_ge(s["bc_res1"], m + 1)
                A(bc_mid[:, :], bc_rest[:, :], ACT.Copy).then_inc(s["bc_mid_s"], 1)

            def step_parts(m):
                act.wait_ge(s["delta_sb"], 1 + m)
                for h in range(2):
                    act.wait_ge(s["z_ps"], m * 2 + h + 1)
                    A(zabs[:, h, :], bank[6 + h], ACT.Abs, bias=b_dt[:, h:h + 1]).then_inc(s["zabs_sb"], 1)
                    A(zpos[:, h, :], bank[6 + h], ACT.Relu, bias=b_dt[:, h:h + 1]).then_inc(s["zabs_sb"], 1)

            def step_exp(m):
                act.wait_ge(s["zabs_sb"], m * 4 + 4)
                A(zabs[:, :, :], zabs[:, :, :], ACT.Exp, scale=-1.0).then_inc(s["zexp_sb"], 1)

            def step_log(m):
                act.wait_ge(s["zexp_sb"], m + 1)
                A(zabs[:, :, :], zabs[:, :, :], ACT.Ln, bias=one_col[:, :]).then_inc(s["softp"], 1)

            def b_out(m, n):
                act.wait_ge(s["b_ps"], m * NST + n + 1)
                act.wait_ge(s["bu_sb"], 1 + m * NST + max(0, n - AHEAD))
                A(b_row[:, n % (AHEAD + 1), :], bank[n % 2], ACT.Copy).then_inc(s["b_sb"], 1)

            def decay(m, n):
                for h in range(2):
                    act.wait_ge(s["h_sb"], 1 + m * 2 * NST + max(0, 2 * n + h - 1))
                    A(bank[6 + h], delta[:, h, :], ACT.Exp, scale=a_neg[:, h, n:n + 1]).then_inc(s["a_ps"], 1)

            def scan_start(m):
                for n in range(AHEAD - 1):
                    b_out(m, n)
                act.wait_ge(s["delta_set"], m * 2 + 2)
                decay(m, 0)

            def group(g, last):
                for n in range(1, NST):
                    decay(g, n)
                    if n + AHEAD - 1 < NST:
                        b_out(g, n + AHEAD - 1)

                def ln_scale(k):
                    act.wait_ge(s["ln_var"], g * 2 + k + 1)
                    A(lnv[:, :], mv[:, :, 1], ACT.Ln, bias=eps_col[:, :]).then_inc(s["ln_log"], 1)
                    act.wait_ge(s["ln_log"], g * 2 + k + 1)
                    A(rstd[:, :], lnv[:, :], ACT.Exp, scale=-0.5).then_inc(s["ln_rstd"], 1)

                def exps(t, k):
                    act.wait_ge(s["s_neg"], g * 8 + 2 * t + k + 1)
                    if t >= 2:
                        act.wait_ge(s["pT_ps"], g * 16 + 4 * (t - 2) + 2 * k + 2)
                    for h in range(8 * k, 8 * k + 8):
                        c, j = divmod(h, 4)
                        last = A(prob[:, t % 2, c, j, :], bank[2 + c][:, j * L:(j + 1) * L], ACT.Exp, bias=nmax[:, t % 2, h:h + 1],
                                 accum_out=den[:, t % 2, h:h + 1])
                    last.then_inc(s["p_sb"], 1)

                def pT_out(t, c):
                    act.wait_ge(s["pT_ps"], g * 16 + 4 * t + c + 1)
                    A(pT[:, c % 2], bank[6 + c % 2].rearrange("p (j q) -> p j q", j=4), ACT.Copy).then_inc(s["pT_sb"], 1)

                act.wait_ge(s["cT_ps"], g + 1)
                A(cT[:, :], bank[1], ACT.Copy).then_inc(s["cT_sb"], 1)
                ln_scale(0)
                act.wait_ge(s["x1T_ps"], g + 1)
                A(x1T[:, :], bank[0], ACT.Copy).then_inc(s["x1T_sb"], 1)
                if not last:
                    x_in(g + 1)
                act.wait_ge(s["v_ps"], g + 1)
                A(v[:, :, :], bank[6].rearrange("p (s d) -> p s d", s=S), ACT.Copy).then_inc(s["v_sb"], 1)
                if not last:
                    silus(g + 1)
                exps(0, 0)
                if not last:
                    bc_hi(g + 1)
                exps(0, 1)
                if not last:
                    step_parts(g + 1)
                    bc_middle(g + 1)
                for t in range(S):
                    for k in range(2):
                        pT_out(t, 2 * k)
                        pT_out(t, 2 * k + 1)
                        if t + 1 < S:
                            exps(t + 1, k)
                        if t == 0 and not last:
                            (step_exp, step_log)[k](g + 1)
                ln_scale(1)
                if not last:
                    scan_start(g + 1)
                act.wait_ge(s["x2T_ps"], g + 1)
                A(x2T[:, :], bank[3], ACT.Copy).then_inc(s["x2T_sb"], 1)
                if not last:
                    b_out(g + 1, AHEAD - 1)
                act.wait_ge(s["route"], 1 + g * ROUTER_LINKS + 12)
                A(gexp[:, :, :, :], gap[:, :, :, :], ACT.Exp, scale=-1.0).then_inc(s["gexp_sb"], 1)

            x_in(0)
            silus(0)
            bc_hi(0)
            bc_middle(0)
            step_parts(0)
            step_exp(0)
            step_log(0)
            scan_start(0)
            b_out(0, AHEAD - 1)
            with act.Fori(0, G - 1) as g:
                group(g, False)
            group(G - 1, True)
            def x_out(j, b):
                act.wait_ge(s["xsT_ps"], 1 + j + 1)
                A(xsT[:, b, :], bank[7][:, b * P:(b + 1) * P], ACT.Copy).then_inc(s["xsT_sb"], 1)

            def silu(j, b):
                act.wait_ge(s["up_ps"], 1 + 2 * j + 1)
                A(sl[:, b, :], bank[b], ACT.Silu).then_inc(s["silu_sb"], 1)

            nc.scalar.preload_act_table_set("silu_and_others")
            x_out(0, 0)
            x_out(1, 1)
            silu(0, 0)
            act.wait_ge(s["up_ps"], 1 + 2)
            x_out(2, 0)
            silu(1, 1)
            with act.Fori(0, NT // 2) as it:
                for b in range(2):
                    j = it * 2 + b
                    act.wait_ge(s["gT_ps"], j + 1)
                    A(gT[:, b], bank[4 + b].rearrange("p (c n) -> p c n", c=FC), ACT.Copy).then_inc(s["gT_sb"], 1)
                    x_out(j + 3, 1 - b)
                    silu(j + 2, b)
            with act.Fori(0, G) as g:
                act.wait_ge(s["f_var"], g + 1)
                A(lnv[:, :], mv[:, :, 1], ACT.Ln, bias=eps_col[:, :]).then_inc(s["f_log"], 1)
                act.wait_ge(s["f_log"], g + 1)
                A(rstd[:, :], lnv[:, :], ACT.Exp, scale=-0.5).then_inc(s["f_rstd"], 1)

        @block.vector
        def _(dve):
            v_ = nc.vector
            TT = v_.tensor_tensor
            early(dve, "ln_sum h_sb hc_sb acc_s route pos_sb gate_sb y_sb")
            dve.wait_ge(s["w_load"], 16 * NW)
            dve.wait_ge(s["pool_const"], 17)
            v_.tensor_copy(identb[:, :], ident[:, :]).then_inc(s["dve_const"], 1)
            v_.tensor_reduce(out=hot[:, :], in_=ident[:, :].rearrange("p (h d) -> p h d", h=H), axis=AX.X, op=ALU.add).then_inc(s["dve_const"], 1)
            TT(w_conv[:, :, :], conv_taps, w_in[:, 0:DIN].unsqueeze(1).broadcast_to((P, KCONV, DIN)), ALU.mult).then_inc(s["dve_const"], 1)
            for h in range(2):
                last = v_.tensor_scalar(d_diag[:, h, :], ident[:, :], d_col[:, h:h + 1], None, ALU.mult)
            last.then_inc(s["dve_const"], 1)
            v_.tensor_reduce(out=sel32[:, :], in_=ident[0:96, 0:96].rearrange("p (r j) -> p j r", r=3), axis=AX.X, op=ALU.add).then_inc(s["dve_const"], 1)
            dve.wait_ge(s["dve_const"], 5)
            v_.tensor_reduce(out=own[:, :], in_=hot[:, :].rearrange("p (c j) -> p j c", c=4), axis=AX.X, op=ALU.add).then_inc(s["dve_const"], 1)
            v_.tensor_copy(sel[:, :, :], sel32[:, :].unsqueeze(2).broadcast_to((96, 2 * NST, P))).then_inc(s["dve_const"], 1)
            dve.wait_ge(s["act_const"], 1)
            v_.tensor_scalar(a_neg[:, :, :], a_neg[:, :, :], -1.0, None, ALU.mult).then_inc(s["dve_const"], 1)
            v_.tensor_scalar(jump[:, :], erow[0:1, :], 1.0, None, ALU.mult).then_inc(s["dve_const"], 1)
            dve.wait_ge(s["dve_const"], 9)

            def layer_norm(src, res, dst, g, k, names, per):
                n_sum, n_stat, n_var, n_rstd, n_out = names
                TT(sx[:, :, :], src, res, ALU.add).then_inc(s[n_sum], 1)
                dve.wait_ge(s[n_sum], 1 + g * per + k + 1)
                for t in range(S):
                    last = v_.bn_stats(stats[:, t, :], sx[:, t, :])
                last.then_inc(s[n_stat], 1)
                dve.wait_ge(s[n_stat], g * per + k + 1)
                plain(dve)
                for t in range(S):
                    last = v_.bn_aggr(mv[:, t, :], stats[:, t, :])
                last.then_inc(s[n_var], 1)
                dve.wait_ge(s[n_rstd], g * per + k + 1)
                for t in range(S):
                    v_.tensor_scalar(dst[:, t, :], sx[:, t, :], mv[:, t, 0:1], rstd[:, t:t + 1], ALU.subtract, ALU.mult).then_inc(s[n_out], 1)

            def bc_residue(m):
                dve.wait_ge(s["bc_hi"], m + 1)
                TT(bc_rest[:, :], bank[0][0:96, :], bc3[:, :], ALU.subtract).then_inc(s["bc_res1"], 1)

            def bc_low(m):
                dve.wait_ge(s["bc_mid_s"], m + 1)
                TT(bc3[64:96, :], bc_rest[64:96, :], bc_mid[64:96, :], ALU.subtract).then_inc(s["bc3_sb"], 1)
                v_.tensor_copy(bc3[32:64, :], bc_mid[32:64, :]).then_inc(s["bc3_sb"], 1)

            def states(m, n):
                dve.wait_ge(s["hc_sb"], 1 + m * NST + max(0, n - 1))
                for h in range(2):
                    dve.wait_ge(s["a_ps"], 1 + m * 2 * NST + 2 * n + h + 1)
                    dve.wait_ge(s["bu_sb"], 1 + m * NST + n + 1)
                    v_.tensor_tensor_scan(hst[:, n % 2, h, :], bank[6 + h], bu[:, n % 2, h, :], 0.0, ALU.mult, ALU.add).then_inc(s["h_sb"], 1)

            def group(g, last):
                def times_c(n):
                    dve.wait_ge(s["h_sb"], 1 + g * 2 * NST + 2 * n + 2)
                    dve.wait_ge(s["c_ps"], g * NST + n + 1)
                    dve.wait_ge(s["y_sum"], 1 + g * NST + max(0, n - 1))
                    TT(hc[:, n % 2], hst[:, n % 2], bank[2 + n % 2].unsqueeze(1).broadcast_to((P, 2, T)), ALU.mult).then_inc(s["hc_sb"], 1)

                for n in range(1, NST):
                    states(g, n)
                    times_c(n - 1)
                times_c(NST - 1)
                dve.wait_ge(s["y_sum"], 1 + g * NST + NST)
                dve.wait_ge(s["sres_sb"], g * 2 + 2)
                TT(yg[:, :, :], y_ps, sres[:, :, :], ALU.mult).then_inc(s["yg_sb"], 1)
                dve.wait_ge(s["o_ps"], g + 1)
                layer_norm(bank[0].rearrange("p (s d) -> p s d", s=S), xn[:, :, :], x1, g, 0,
                           ("ln_sum", "ln_stat", "ln_var", "ln_rstd", "x1_sb"), 2)
                for n, i in enumerate((2, 3, 0, 1)):
                    bk = 2 + i
                    dve.wait_ge(s["proj_ps"], g * 4 + n + 1)
                    TT(rot[:, i, :].rearrange("p (s t) -> p s t", s=S), bank[bk].rearrange("p (s t) -> p s t", s=S),
                       rope[:, i, :].unsqueeze(1).broadcast_to((P, S, L)), ALU.mult).then_inc(s["rot_sb"], 1)

                dve.wait_ge(s["qk_sb"], g * 2 + 2)
                for j in range(4):
                    v_.tensor_scalar(k_heads[:, j, :], qk[:, 1, :], own[:, j:j + 1], None, ALU.mult).then_inc(s["k_heads_sb"], 1)

                def maxima(t, k):
                    sc = quad[:, 2 * k:2 * k + 2].rearrange("p c (j m) -> p (c j) m", j=4)
                    hs = slice(8 * k, 8 * k + 8)
                    dve.wait_ge(s["s_ps"], 1 + g * 8 + 2 * t + k + 1)
                    v_.tensor_reduce(out=smax[:, t % 2, hs], in_=sc, axis=AX.X, op=ALU.max).then_inc(s["s_max"], 1)
                    dve.wait_ge(s["s_max"], g * 8 + 2 * t + k + 1)
                    v_.tensor_scalar(nmax[:, t % 2, hs], smax[:, t % 2, hs], -1.0, None, ALU.mult).then_inc(s["s_neg"], 1)

                def normed(t, k):
                    hs = slice(8 * k, 8 * k + 8)
                    dve.wait_ge(s["p_sb"], g * 8 + 2 * t + k + 1)
                    v_.reciprocal(rden[:, t % 2, hs], den[:, t % 2, hs]).then_inc(s["rden_sb"], 1)
                    dve.wait_ge(s["rden_sb"], g * 8 + 2 * t + k + 1)
                    pr = prob[:, t % 2, 2 * k:2 * k + 2].rearrange("p c j m -> p (c j) m")
                    TT(pr, pr, rden[:, t % 2, hs].unsqueeze(2).broadcast_to((P, 8, L)), ALU.mult).then_inc(s["pn_sb"], 1)

                def own_heads(t):
                    dve.wait_ge(s["pv_ps"], g * 4 * S + 4 * t + 4)
                    TT(ao_own[:, t % 2], bank[t % 2].rearrange("p (j q) -> p j q", j=4), own[:, :].unsqueeze(2).broadcast_to((P, 4, L)),
                       ALU.mult).then_inc(s["ao_own_sb"], 1)
                    dve.wait_ge(s["ao_own_sb"], g * S + t + 1)
                    v_.tensor_reduce(out=aoT[:, t * L:(t + 1) * L], in_=ao_own[:, t % 2].rearrange("p j q -> p q j"), axis=AX.X,
                                     op=ALU.add).then_inc(s["aoT_sb"], 1)

                for k in range(2):
                    maxima(0, k)
                if not last:
                    bc_residue(g + 1)
                for k in range(2):
                    normed(0, k)
                if not last:
                    bc_low(g + 1)
                for t in range(S):
                    if t + 1 < S:
                        maxima(t + 1, 0)
                        if t:
                            own_heads(t - 1)
                        maxima(t + 1, 1)
                        normed(t + 1, 0)
                        normed(t + 1, 1)
                own_heads(S - 2)
                own_heads(S - 1)
                dve.wait_ge(s["wo_ps"], g + 1)
                dve.wait_ge(s["x1b_sb"], g + 1)
                dve.wait_ge(s["x2_sent"], 1 + g)
                layer_norm(bank[2].rearrange("p (s d) -> p s d", s=S), x1b[:, :, :], x2, g, 1,
                           ("ln_sum", "ln_stat", "ln_var", "ln_rstd", "x2_sb"), 2)
                c = [0]

                def link(ins):
                    c[0] += 1
                    ins.then_inc(s["route"], 1)
                    dve.wait_ge(s["route"], 1 + g * ROUTER_LINKS + c[0])

                def both(x):
                    return x.unsqueeze(2).broadcast_to((P, S, 2, E))

                dve.wait_ge(s["x2_sb"], g * S + S)
                link(v_.tensor_copy(x2_all[:, bass.ds(g * S, S), :], x2[:, :, :]))
                if not last:
                    states(g + 1, 0)
                dve.wait_ge(s["lg_ps"], g + 1)
                link(v_.tensor_copy(lg[:, :, :], bank[2][:, 0:S * E].rearrange("p (s e) -> p s e", s=S)))
                plain(dve)
                for t in range(S):
                    end = v_.max(m8[:, t, :], lg[:, t, :])
                link(end)
                plain(dve)
                for t in range(S):
                    end = v_.max_index(i8[:, t, :], m8[:, t, :], lg[:, t, :])
                link(end)
                link(v_.tensor_copy(idxf[:, :, :], i8[:, :, 0:2]))
                link(TT(oh[:, :, :, :], iota8[:, :].unsqueeze(1).unsqueeze(1).broadcast_to((P, S, 2, E)),
                        idxf[:, :, :].unsqueeze(3).broadcast_to((P, S, 2, E)), ALU.is_equal))
                link(TT(ohb[:, :, :], oh[:, :, 0, :], oh[:, :, 1, :], ALU.add))
                link(v_.scalar_tensor_tensor(lab[:, :, :], lg[:, :, :], -1.0, lg[:, :, :], ALU.mult, ALU.max))
                mm = m8[:, :, 0:2].unsqueeze(3).broadcast_to((P, S, 2, E))
                link(TT(fac[:, :, :, :], both(lab[:, :, :]), mm, ALU.max))
                link(TT(gap[:, :, :, :], mm, both(lg[:, :, :]), ALU.subtract))
                link(v_.tensor_scalar(thr[:, :, :, :], fac[:, :, :, :], 0.02, None, ALU.mult))
                link(TT(keep[:, :, :, :], thr[:, :, :, :], gap[:, :, :, :], ALU.is_ge))
                c[0] = 12
                link(TT(keep[:, :, 1, :], keep[:, :, 1, :], oh[:, :, 0, :], ALU.is_gt))
                dve.wait_ge(s["gexp_sb"], g + 1)
                link(v_.tensor_scalar(gexp[:, :, :, :], gexp[:, :, :, :], 1.0, None, ALU.min))
                link(TT(gexp[:, :, :, :], gexp[:, :, :, :], keep[:, :, :, :], ALU.mult))
                link(v_.tensor_reduce(out=gsum[:, :, :], in_=gexp[:, :, :, :], axis=AX.X, op=ALU.add))
                link(v_.reciprocal(gates_all[:, bass.ds(g * S, S), :], gsum[:, :, :]))
                dve.wait_ge(s["rank_ps"], g + 1)
                rk = bank[2][:, 2 * S * E:(3 * S + 1) * E].rearrange("p (s e) -> p s e", e=E)
                link(TT(rank[:, :, :], rk[:, 0:S, :], base[:, :].unsqueeze(1).broadcast_to((P, S, E)), ALU.add))
                link(TT(base[:, :], base[:, :], rk[:, S, :], ALU.add))
                link(TT(prk[:, :, :, :], both(rank[:, :, :]), oh[:, :, :, :], ALU.mult))
                link(v_.tensor_reduce(out=posf[:, :, :], in_=prk[:, :, :, :], axis=AX.X, op=ALU.add))
                assert c[0] == ROUTER_LINKS
                v_.tensor_copy(posf_all[:, bass.ds(g * S, S), :], posf[:, :, :])
                v_.tensor_copy(idxf_all[:, bass.ds(g * S, S), :], idxf[:, :, :])
                v_.tensor_copy(pos[:, :, :], posf[:, :, :]).then_inc(s["pos_sb"], 1)

            bc_residue(0)
            bc_low(0)
            states(0, 0)
            with dve.Fori(0, G - 1) as g:
                group(g, False)
            group(G - 1, True)

            v_.tensor_scalar(tail_f[:, :], base[:, :], pcol[:, 0:1], None, ALU.add).then_inc(s["tail"], 1)
            dve.wait_ge(s["tail"], 1)
            v_.tensor_copy(tail_i[:, :], tail_f[:, :]).then_inc(s["tail"], 1)
            k = [0]

            def tlink(ins):
                k[0] += 1
                ins.then_inc(s["table_link"], 1)
                dve.wait_ge(s["table_link"], k[0])

            N2 = NT + 8
            tlink(TT(cnt[:, :], base[:, :], erow[:, :], ALU.subtract))
            tlink(TT(full[:, :, :], cnt[:, :].unsqueeze(2).broadcast_to((P, E, B)), k128[:, :].unsqueeze(1).broadcast_to((P, E, B)), ALU.is_gt))
            tlink(v_.tensor_reduce(out=ntile[:, :], in_=full[:, :, :], axis=AX.X, op=ALU.add))
            tlink(v_.tensor_tensor_scan(cum[:, :], ones8[:, :], ntile[:, :], 0.0, ALU.mult, ALU.add))
            tlink(v_.tensor_scalar(lastt[:, :], cum[0:1, E - 1:E], -1.0, None, ALU.add))
            tlink(v_.tensor_scalar(jc[:, :], jrow[:, :], lastt[:, 0:1], None, ALU.min))
            tlink(TT(ind[:, :, :], jc[:, :].unsqueeze(2).broadcast_to((1, N2, E)), cum[0:1, :].unsqueeze(1).broadcast_to((1, N2, E)), ALU.is_ge))
            tlink(v_.tensor_reduce(out=t_e[:, :], in_=ind[:, :, :], axis=AX.X, op=ALU.add))
            tlink(v_.tensor_scalar(jump[:, :], ntile[0:1, :], float(-P), float(STRIDE), ALU.mult, ALU.add))
            tlink(TT(wsum[:, :, :], ind[:, :, :], jump[:, :].unsqueeze(1).broadcast_to((1, N2, E)), ALU.mult))
            tlink(v_.tensor_reduce(out=t_row[:, :], in_=wsum[:, :, :], axis=AX.X, op=ALU.add))
            tlink(v_.tensor_scalar(t_tmp[:, :], jc[:, :], float(P), None, ALU.mult))
            tlink(TT(t_row[:, :], t_row[:, :], t_tmp[:, :], ALU.add))
            tlink(v_.tensor_copy(table[:, 0, :], t_e[:, :]))
            v_.tensor_copy(table[:, 1, :], t_row[:, :]).then_inc(s["table_sb"], 1)
            tlink(TT(shift[:, :], cum[:, :], ntile[:, :], ALU.subtract))
            tlink(v_.tensor_scalar(shift[:, :], shift[:, :], float(P), None, ALU.mult))
            tlink(TT(shift[:, :], shift[:, :], erow[:, :], ALU.subtract))
            for e in range(E):
                tlink(v_.tensor_scalar(part[:, :, :], idxf_all[:, :, :], float(e), shift[:, e:e + 1], ALU.is_equal, ALU.mult))
                tlink(TT(posf_all[:, :, :], posf_all[:, :, :], part[:, :, :], ALU.add))
            tlink(v_.tensor_copy(pos_all[:, :, :], posf_all[:, :, :]))

            def gate(j, b):
                dve.wait_ge(s["up_ps"], 1 + 2 * j + 2)
                dve.wait_ge(s["silu_sb"], j + 1)
                TT(gg[:, b, :], sl[:, b, :], bank[2 + b], ALU.mult).then_inc(s["gate_sb"], 1)

            gate(0, 0)
            gate(1, 1)
            with dve.Fori(0, NT // 2) as it:
                for b in range(2):
                    j = it * 2 + b
                    gate(j + 2, b)
                    dve.wait_ge(s["y_ps_s"], j + 1)
                    dve.wait_ge(s[f"y_store{b}"], 16 + it * 16)
                    v_.tensor_copy(ys[:, b, :], bank[6][:, b * P:(b + 1) * P]).then_inc(s["y_sb"], 1)
            def indices(g, b):
                v_.tensor_copy(idx[:, b, :].rearrange("p (s k) -> p s k", s=S), pos_all[:, bass.ds(g * S, S), :]).then_inc(s["idx_sb"], 1)

            def combine(g, b, turn, more):
                if more:
                    indices(g + 1, 1 - b)
                dve.wait_ge(s[f"gath{b}"], (turn + 1) * 2 * S * 16)
                for k in range(2):
                    for t in range(S):
                        src = x2_all[:, bass.ds(g * S + t, 1), :].rearrange("p a d -> p (a d)") if k == 0 else acc[:, t, :]
                        v_.scalar_tensor_tensor(acc[:, t, :], yk[b][:, 2 * t + k, :],
                                                gates_all[:, bass.ds(g * S + t, 1), k], src, ALU.mult, ALU.add).then_inc(s["acc_s"], 1)
                    dve.wait_ge(s["acc_s"], 1 + g * 2 * S + (k + 1) * S)
                dve.wait_ge(s["fin_store"], 16 + g * 16)
                for t in range(S):
                    end = v_.bn_stats(stats[:, t, :], acc[:, t, :])
                end.then_inc(s["f_stat"], 1)
                dve.wait_ge(s["f_stat"], g + 1)
                plain(dve)
                for t in range(S):
                    end = v_.bn_aggr(mv[:, t, :], stats[:, t, :])
                end.then_inc(s["f_var"], 1)
                dve.wait_ge(s["f_rstd"], g + 1)
                for t in range(S):
                    v_.tensor_scalar(fin[:, t, :], acc[:, t, :], mv[:, t, 0:1], rstd[:, t:t + 1], ALU.subtract, ALU.mult).then_inc(s["fin_sb"], 1)
                dve.wait_ge(s["fin_sb"], g * S + S)

            indices(0, 0)
            with dve.Fori(0, G // 2 - 1) as it:
                for b in range(2):
                    combine(2 * it + b, b, it, True)
            combine(G - 2, 0, G // 2 - 1, True)
            combine(G - 1, 1, G // 2 - 1, False)

        @block.tensor
        def _(pe):
            MM = nc.tensor.matmul
            TR = nc.tensor.transpose
            early(pe, "s_ps xsT_ps up_ps y_sum")
            pe.wait_ge(s["w_load"], 16 * NW)
            pe.wait_ge(s["dve_const"], 9)

            def x_t(m):
                pe.wait_ge(s["x_load"], m * 16 + 16)
                for t in range(S):
                    last = TR(bank[7][:, t * L:(t + 1) * L], xn[:, t, :], ident[:, :])
                last.then_inc(s["xT_ps"], 1)

            def conv(m):
                pe.wait_ge(s["xT_sb"], m + 1)
                for h in range(2):
                    for k in range(KCONV):
                        last = MM(bank[h].rearrange("p (s t) -> p s t", s=S), w_conv[:, k, h * P:(h + 1) * P], xT[:, :, k:k + L],
                                  start=(k == 0), stop=(k == KCONV - 1))
                    last.then_inc(s["conv_ps"], 1)

            def res(m):
                for h in range(2):
                    MM(bank[6 + h].rearrange("p (s t) -> p s t", s=S), w_in[:, DIN + h * P:DIN + (h + 1) * P], xT[:, :, KCONV - 1:],
                       start=True, stop=True).then_inc(s["res_ps"], 1)

            def bc_dtl(m):
                pe.wait_ge(s["u_sb"], m * 2 + 2)
                for h in range(2):
                    last = MM(bank[0][0:96, :], w_bc[:, h].rearrange("p r n -> p (r n)"), u[:, h, :], start=(h == 0), stop=(h == 1))
                last.then_inc(s["bc_ps"], 1)
                for h in range(2):
                    last = MM(bank[1][0:DTR, :], w_dtl[:, h, :], u[:, h, :], start=(h == 0), stop=(h == 1))
                last.then_inc(s["dtl_ps"], 1)

            def steps(m):
                pe.wait_ge(s["dtl_sb"], m + 1)
                pe.wait_ge(s["sres_sb"], m * 2 + 2)
                for h in range(2):
                    MM(bank[6 + h], w_dt[:, h * P:(h + 1) * P], dtl[:, :], start=True, stop=True).then_inc(s["z_ps"], 1)

            def row_b(m, n):
                pe.wait_ge(s["b_sb"], 1 + m * NST + max(0, n - 1))
                MM(bank[n % 2], sel[:, n, :], bc3[:, :], start=True, stop=True).then_inc(s["b_ps"], 1)

            def scan_start(m):
                pe.wait_ge(s["bc3_sb"], m * 2 + 2)
                row_b(m, 0)
                row_b(m, 1)
                for h in range(2):
                    MM(bank[4 + h], d_diag[:, h, :], u[:, h, :], start=True, stop=False, skip_group_check=True)

            def group(g, final):
                def row_c(n):
                    pe.wait_ge(s["hc_sb"], 1 + g * NST + max(0, n - 1))
                    MM(bank[2 + n % 2], sel[:, NST + n, :], bc3[:, :], start=True, stop=True).then_inc(s["c_ps"], 1)

                pe.wait_ge(s["pos_sb"], 1 + g)
                row_c(0)
                for n in range(NST):
                    if n + 1 < NST:
                        row_c(n + 1)
                    if n + AHEAD + 1 < NST:
                        row_b(g, n + AHEAD + 1)
                    pe.wait_ge(s["hc_sb"], 1 + g * NST + n + 1)
                    for h in range(2):
                        last = MM(bank[4 + h], ident[:, :], hc[:, n % 2, h, :], start=False, stop=(n == NST - 1), skip_group_check=True)
                    last.then_inc(s["y_sum"], 1)
                pe.wait_ge(s["yg_sb"], g + 1)
                for t in range(S):
                    for h in range(2):
                        last = MM(bank[0][:, t * D:(t + 1) * D], yg[:, h, t * L:(t + 1) * L], w_out[:, h, :], start=(h == 0), stop=(h == 1))
                last.then_inc(s["o_ps"], 1)
                pe.wait_ge(s["ctx_load"], g * 16 + 16)
                for t in range(S):
                    last = TR(bank[1][:, t * L:(t + 1) * L], cn[:, t, :], ident[:, :])
                last.then_inc(s["cT_ps"], 1)
                pe.wait_ge(s["cT_sb"], g + 1)
                MM(bank[4], wkT[:, :], cT[:, :], start=True, stop=True).then_inc(s["proj_ps"], 1)
                MM(bank[5], wkrT[:, :], cT[:, :], start=True, stop=True).then_inc(s["proj_ps"], 1)
                for t in range(S):
                    last = MM(bank[6][:, t * D:(t + 1) * D], cT[:, t * L:(t + 1) * L], wvT[:, :], start=True, stop=True)
                last.then_inc(s["v_ps"], 1)
                pe.wait_ge(s["x1_sb"], g * S + S)
                for t in range(S):
                    last = TR(bank[0][:, t * L:(t + 1) * L], x1[:, t, :], ident[:, :])
                last.then_inc(s["x1T_ps"], 1)
                if not final:
                    x_t(g + 1)
                pe.wait_ge(s["x1T_sb"], g + 1)
                MM(bank[2], wqT[:, :], x1T[:, :], start=True, stop=True).then_inc(s["proj_ps"], 1)
                MM(bank[3], wqrT[:, :], x1T[:, :], start=True, stop=True).then_inc(s["proj_ps"], 1)
                if not final:
                    conv(g + 1)
                    pe.wait_ge(s["v_sb"], g + 1)
                    res(g + 1)
                pe.wait_ge(s["rot_sb"], g * 4 + 4)
                pe.wait_ge(s["mask_sb"], g + 1)

                def scores(t, k):
                    if t:
                        pe.wait_ge(s["p_sb"], g * 8 + 2 * (t - 1) + k + 1)
                    for c in (2 * k, 2 * k + 1):
                        o = bank[2 + c].rearrange("p (j m) -> p j m", j=4)
                        MM(o, identb[:, :], mbias[:, t, :].unsqueeze(1).broadcast_to((P, 4, L)), start=True, stop=False)
                        r = slice(32 * c, 32 * c + 32)
                        last = MM(o, qk[r, 0, t * L:(t + 1) * L], k_heads[r, :, t * L:(t + 1) * L], start=False, stop=True)
                    last.then_inc(s["s_ps"], 1)

                def head_t(t, c):
                    pe.wait_ge(s["pn_sb"], g * 8 + 2 * t + c // 2 + 1)
                    if 4 * t + c >= 2:
                        pe.wait_ge(s["pT_sb"], g * 16 + 4 * t + c - 1)
                    for j in range(4):
                        last = TR(bank[6 + c % 2][:, j * L:(j + 1) * L], prob[:, t % 2, c, j, :], ident[:, :])
                    last.then_inc(s["pT_ps"], 1)

                def head_v(t, c):
                    pe.wait_ge(s["pT_sb"], g * 16 + 4 * t + c + 1)
                    if c == 0 and t >= 2:
                        pe.wait_ge(s["ao_own_sb"], g * S + t - 1)
                    r = slice(32 * c, 32 * c + 32)
                    MM(bank[t % 2][r, :], v[:, t, r], pT[:, c % 2].rearrange("p j q -> p (j q)"), start=True, stop=True).then_inc(s["pv_ps"], 1)

                pe.wait_ge(s["k_heads_sb"], g * 4 + 4)
                scores(0, 0)
                scores(0, 1)
                if not final:
                    bc_dtl(g + 1)
                    steps(g + 1)
                    pe.wait_ge(s["zabs_sb"], g * 4 + 8)
                    pe.wait_ge(s["bc_res1"], g + 2)
                pe.wait_ge(s["v_sb"], g + 1)
                for t in range(S):
                    if t + 1 < S:
                        scores(t + 1, 0)
                    head_t(t, 0)
                    head_t(t, 1)
                    head_v(t, 0)
                    if t + 1 < S:
                        scores(t + 1, 1)
                    head_t(t, 2)
                    head_v(t, 1)
                    head_t(t, 3)
                    head_v(t, 2)
                    head_v(t, 3)
                pe.wait_ge(s["aoT_sb"], g * S + S)
                for t in range(S):
                    last = MM(bank[2][:, t * D:(t + 1) * D], aoT[:, t * L:(t + 1) * L], woT[:, :], start=True, stop=True)
                last.then_inc(s["wo_ps"], 1)
                if not final:
                    scan_start(g + 1)
                pe.wait_ge(s["x2_sb"], g * S + S)
                for t in range(S):
                    last = TR(bank[3][:, t * L:(t + 1) * L], x2[:, t, :], ident[:, :])
                last.then_inc(s["x2T_ps"], 1)
                pe.wait_ge(s["x2T_sb"], g + 1)
                for t in range(S):
                    last = MM(bank[2][:, t * E:(t + 1) * E], x2T[:, t * L:(t + 1) * L], gate_wT[:, :], start=True, stop=True)
                last.then_inc(s["lg_ps"], 1)
                if not final:
                    for n in range(2, AHEAD + 1):
                        row_b(g + 1, n)
                pe.wait_ge(s["route"], 1 + g * ROUTER_LINKS + 7)
                for t in range(S + 1):
                    o = bank[2][:, (2 * S + t) * E:(2 * S + t + 1) * E]
                    for r in range(t):
                        last = MM(o, ones_b[:, :], ohb[:, r, :], start=(r == 0), stop=(t == S and r == S - 1))
                    if t < S:
                        last = MM(o, tri[:, :], ohb[:, t, :], start=(t == 0), stop=True)
                last.then_inc(s["rank_ps"], 1)

            x_t(0)
            conv(0)
            res(0)
            bc_dtl(0)
            steps(0)
            pe.wait_ge(s["zabs_sb"], 4)
            scan_start(0)
            for n in range(2, AHEAD + 1):
                row_b(0, n)
            with pe.Fori(0, G - 1) as g:
                group(g, False)
            group(G - 1, True)

            def rows_t(j, b, turn, load):
                pe.wait_ge(s[f"xs_load{load}"], turn * 16 + 16)
                pe.wait_ge(s["xsT_sb"], j)
                TR(bank[7][:, b * P:(b + 1) * P], xs[:, load, :], ident[:, :]).then_inc(s["xsT_ps"], 1)

            def up(j, b):
                e = pe.value_load(table[0:1, 0, bass.ds(j, 1)], min_val=0, max_val=E - 1)
                pe.wait_ge(s["xsT_sb"], j + 1)
                MM(bank[b], xsT[:, b, :], w1[:, bass.ds(e, 1), :].rearrange("p a f -> p (a f)"), start=True, stop=True).then_inc(s["up_ps"], 1)
                MM(bank[2 + b], xsT[:, b, :], w3[:, bass.ds(e, 1), :].rearrange("p a f -> p (a f)"), start=True, stop=True).then_inc(s["up_ps"], 1)

            def gated_t(j, b):
                pe.wait_ge(s["gate_sb"], 1 + j + 1)
                for c in range(FC):
                    last = TR(bank[4 + b][:, c * P:(c + 1) * P], gg[:, b, c * P:(c + 1) * P], ident[:, :])
                last.then_inc(s["gT_ps"], 1)

            def down(j, b):
                e = pe.value_load(table[0:1, 0, bass.ds(j, 1)], min_val=0, max_val=E - 1)
                pe.wait_ge(s["gT_sb"], j + 1)
                pe.wait_ge(s["y_sb"], 1 + j)
                for c in range(FC):
                    last = MM(bank[6][:, b * P:(b + 1) * P], gT[:, b, c, :], w2[:, bass.ds(e, 1), c, :].rearrange("p a d -> p (a d)"),
                              start=(c == 0), stop=(c == FC - 1))
                last.then_inc(s["y_ps_s"], 1)

            pe.wait_ge(s["table_sb"], 1)
            pe.wait_ge(s["w13_load"], 32)
            pe.wait_ge(s["w2_load"], 16)
            rows_t(0, 0, 0, 0)
            rows_t(1, 1, 0, 1)
            up(0, 0)
            rows_t(2, 0, 0, 2)
            up(1, 1)
            gated_t(0, 0)
            with pe.Fori(0, NT // 4) as it:
                for b in range(4):
                    j = it * 4 + b
                    rows_t(j + 3, 1 - b % 2, it + (b + 3) // 4, (b + 3) % 4)
                    up(j + 2, b % 2)
                    gated_t(j + 1, 1 - b % 2)
                    down(j, b % 2)


def kernel(**inputs):
    import numpy as np
    import concourse.bacc as bacc
    from concourse import mybir as mb
    from concourse.bass_utils import run_bass_kernel_spmd as run

    c = np.ascontiguousarray
    i = {k.replace("L0_attn_", "").replace("L0_xattn_", "").replace("L0_ffn_", ""): np.asarray(v) for k, v in inputs.items()}

    def halves(w):
        return c(np.moveaxis(w.reshape((2, 128) + w.shape[1:]), 0, 1))

    swap = np.arange(128).reshape(64, 2)[:, ::-1].reshape(128)
    theta = (1.0 / np.float32(10000.0) ** (np.arange(0, HD, 2, dtype=np.float32) / np.float32(HD))).astype(np.float32)
    ang = (np.arange(L, dtype=np.float32)[:, None] * theta[None, :]).astype(np.float32)
    cos = np.repeat(np.tile(np.cos(ang).T, (H, 1)), 2, axis=0)
    sin = np.repeat(np.tile(np.sin(ang).T, (H, 1)), 2, axis=0)
    sin[0::2] *= -1
    scale = np.float32(1.0 / np.sqrt(np.float32(HD)))
    rope = np.stack([cos * scale, sin * scale, cos, sin], axis=1).astype(np.float32)
    arrays = {
        "x": c(i["x"]), "ctx_1024": c(i["ctx_1024"]), "mask": c(i["mask_BxS2_if1"].reshape(-1)),
        "W_in": c(i["W_in"]), "conv_w": c(i["conv_w"][:, 0, :].T), "conv_b": halves(i["conv_b"]),
        "W_x": halves(i["W_x"]), "W_dt": c(i["W_dt"]), "b_dt": halves(i["b_dt"]), "W_out": halves(i["W_out"]),
        "A_log": halves(i["A_log"]), "D": halves(i["D"]),
        "WqT": c(i["Wq"].T), "WqrT": c(i["Wq"].T[:, swap]),
        "WkT": c(i["Wk"].T), "WkrT": c(i["Wk"].T[:, swap]),
        "WvT": c(i["Wv"].T), "WoT": c(i["Wo"].T), "bo": c(i["bo"]), "rope": c(rope),
        "gate_wT": c(i["gate_w"].T), "w1T": c(i["w1"].transpose(2, 0, 1)), "w3T": c(i["w3"].transpose(2, 0, 1)),
        "w2T": c(i["w2"].transpose(2, 0, 1).reshape(FC, P, E, D).transpose(1, 2, 0, 3)),
    }
    nc = bacc.Bacc("TRN2", target_bir_lowering=False, num_devices=1)
    aps = {k: nc.dram_tensor(f"in_{k}", v.shape, mb.dt.from_np(v.dtype), kind="ExternalInput").ap() for k, v in arrays.items()}
    o = nc.dram_tensor("out_0", (B, L, D), mb.dt.float32, kind="ExternalOutput").ap()
    build(nc, aps, o)
    r = run(nc, [{f"in_{k}": v for k, v in arrays.items()}], core_ids=[0])
    return r.results[0]["out_0"]
```

```python
import concourse.bass as bass
from concourse import mybir
from contextlib import ExitStack

F32 = mybir.dt.float32
BF16 = mybir.dt.bfloat16
I32 = mybir.dt.int32
U32 = mybir.dt.uint32
ALU = mybir.AluOpType
ACT = mybir.ActivationFunctionType
AX = mybir.AxisListType

P = 128
B, L, D = 32, 128, 128
S = 4
G = B // S
T = S * L
DIN, NST, DTR, KCONV = 256, 16, 64, 4
H, HD = 16, 8
AHEAD = 3
E, F = 8, 512
FC = F // P
STRIDE = B * L + P
NT = (2 * B * L + E * (P - 1)) // P + 1
NT += -NT % 8
ROW = D + 2
EPS = 1e-5
NEG = -1e30
RESET = 1e25
ROUTER_LINKS, GAPS, CHOSEN = 24, 7, 11


def build(nc, a, out):
    ctx = ExitStack()
    with ctx:
        def sb(name, shape, dt=F32):
            return ctx.enter_context(nc.sbuf_tensor(name, shape, dt))

        def sem(name):
            return ctx.enter_context(nc.semaphore(name))

        ident = sb("ident", [P, P])
        identb = sb("identb", [P, P], BF16)
        w_in = sb("w_in", [P, 2 * DIN])
        w_conv = sb("w_conv", [P, KCONV, DIN])
        conv_b = sb("conv_b", [P, 2])
        w_dtl = sb("w_dtl", [P, 2, DTR])
        w_bc = sb("w_bc", [P, 2, 3, 2 * NST])
        w_dt = sb("w_dt", [DTR, DIN])
        b_dt = sb("b_dt", [P, 2])
        w_out = sb("w_out", [P, 2, D])
        a_log = sb("a_log", [P, 2, NST])
        a_neg = sb("a_neg", [P, 2, NST])
        d_col = sb("d_col", [P, 2])
        d_diag = sb("d_diag", [P, 2, P])
        sel32 = sb("sel32", [96, 2 * NST])
        sel = sb("sel", [96, 2 * NST, P], BF16)
        wqT = sb("wqT", [P, P])
        wqrT = sb("wqrT", [P, P])
        wkT = sb("wkT", [P, P])
        wkrT = sb("wkrT", [P, P])
        wvT = sb("wvT", [P, P])
        woT = sb("woT", [P, P])
        bo_b = sb("bo_b", [P, P])
        rope = sb("rope", [P, 4, L])
        causal = sb("causal", [P, L])
        mask_b = sb("mask_b", [P, T], I32)
        gate_wT = sb("gate_wT", [P, E])
        w1 = sb("w1", [P, E, F])
        w3 = sb("w3", [P, E, F])
        eps_col = sb("eps_col", [P, 1])
        one_col = sb("one_col", [P, 1])
        iota8 = sb("iota8", [P, E])
        hot = sb("hot", [P, H])
        own = sb("own", [P, 4])
        tri = sb("tri", [P, P], BF16)
        ones_b = sb("ones_b", [P, P], BF16)
        zrow = sb("zrow", [P, ROW])
        tok2 = sb("tok2", [P, S])

        xn = sb("xn", [P, S, D])
        xT = sb("xT", [P, S, KCONV - 1 + L])
        u = sb("u", [P, 2, T])
        sres = sb("sres", [P, 2, T])
        bc3 = sb("bc3", [96, T], BF16)
        bc_mid = sb("bc_mid", [96, T], BF16)
        dtl = sb("dtl", [DTR, T])
        zabs = sb("zabs", [P, 2, T])
        zpos = sb("zpos", [P, 2, T])
        delta = sb("delta", [P, 2, T])
        du = sb("du", [P, 2, T])
        b_row = sb("b_row", [P, AHEAD, T])
        scan = sb("scan", [P, 2, 3, 2, T])
        bu = scan[:, 0]
        hst = scan[:, 1]
        hc = sb("hc", [P, 3, 2, T])
        yg = zabs
        sx = sb("sx", [P, S, D])
        stats = sb("stats", [P, S, 6])
        mv = sb("mv", [P, S, 2])
        lnv = sb("lnv", [P, S])
        rstd = sb("rstd", [P, S])
        x1 = sb("x1", [P, S, D])
        x1b = sb("x1b", [P, S, D])
        cn = sb("cn", [P, S, D])
        cT = sb("cT", [P, T])
        rot = sb("rot", [P, 4, T])
        bc_rest = rot[0:96, 0, :]
        conv_taps = rot[:, 0:2, :].rearrange("p a t -> p (a t)").rearrange("p (k c) -> p k c", k=KCONV)
        qk = sb("qk", [P, 2, T])
        k_heads = scan[:, 0, 0:2].rearrange("p a b t -> p (a b) t")
        ao_own = scan[:, 1, 0].rearrange("p b (j q) -> p b j q", j=4)
        v = sb("v", [P, S, D])
        pad = sb("pad", [P, T])
        mbias = sb("mbias", [P, S, L], BF16)
        smax = sb("smax", [P, 2, H])
        nmax = sb("nmax", [P, 2, H])
        den = sb("den", [P, 2, H])
        prob = sb("prob", [P, 2, 4, 4, L])
        w2 = prob[:, :, :, :, :].rearrange("p a j c m -> p (a j) c m")
        pT = sb("pT", [P, 2, 4, L])
        rden = sb("rden", [P, 2, H])
        aoT = sb("aoT", [P, T])
        x1T = aoT
        x2 = sb("x2", [P, S, ROW])
        x2_all = sb("x2_all", [P, B, D])
        x2T = cT
        lg = sb("lg", [P, S, E])
        m8 = sb("m8", [P, S, 8])
        i8 = sb("i8", [P, S, 8], U32)
        idxf = sb("idxf", [P, S, 2])
        oh = sb("oh", [P, S, 2, E])
        ohb = sb("ohb", [P, S, E], BF16)
        lab = sb("lab", [P, S, E])
        fac = sb("fac", [P, S, 2, E])
        gap = sb("gap", [P, S, 2, E])
        thr = sb("thr", [P, S, 2, E])
        keep = sb("keep", [P, S, 2, E])
        gexp = sb("gexp", [P, S, 2, E])
        gsum = sb("gsum", [P, S, 2])
        gates_all = sb("gates_all", [P, B, 2])
        base = sb("base", [P, E])
        rank = sb("rank", [P, S, E])
        prk = sb("prk", [P, S, 2, E])
        posf = sb("posf", [P, S, 2])
        pos = sb("pos", [P, S, 2], I32)
        tail_i = sb("tail_i", [P, E], I32)
        erow = sb("erow", [P, E])
        cnt = sb("cnt", [P, E])
        k128 = sb("k128", [P, B])
        full = u[:, 0:2, :].rearrange("p h t -> p (h t)")[:, 0:(E) * B].rearrange("p (a b) -> p a b", b=B)
        ntile = sb("ntile", [P, E])
        ones8 = sb("ones8", [P, E])
        cum = sb("cum", [P, E])
        jrow = sb("jrow", [P, NT + 8])
        ind = sres[:, 0:2, :].rearrange("p h t -> p (h t)")[:, 0:(NT + 8) * E].rearrange("p (a b) -> p a b", b=E)
        jump = sb("jump", [P, E])
        wsum = yg[:, 0:2, :].rearrange("p h t -> p (h t)")[:, 0:(NT + 8) * E].rearrange("p (a b) -> p a b", b=E)
        t_e = sb("t_e", [P, NT + 8])
        t_row = sb("t_row", [P, NT + 8])
        j128 = sb("j128", [P, NT + 8])
        table = sb("table", [P, 2, NT + 8], I32)
        free = qk[:, :, :].rearrange("p i t -> p (i t)")
        xs = free[:, 0:4 * ROW].rearrange("p (b d) -> p b d", b=4)
        xsT = free[:, 4 * ROW:4 * ROW + 2 * P].rearrange("p (b n) -> p b n", b=2)
        sl = zabs
        gg = zpos
        gT = delta[:, :, :].rearrange("p b (c n) -> p b c n", c=FC)
        ys = aoT[:, 0:4 * D].rearrange("p (b d) -> p b d", b=4)
        spare = sb("spare", [P, 8])
        place = sb("place", [P, 8])
        dest = sb("dest", [P, 8], I32)
        yk = [x[:, :, :].rearrange("p k (s d) -> p (k s) d", s=S) for x in (du, u, sres, zabs)]
        acc = (sx, pT[:, 0])
        fstats = pT[:, 1, 0, 0:2 * S * 6].rearrange("p (b s k) -> p b s k", b=2, k=6)
        fmv = pT[:, 1, 1, 0:2 * S * 2].rearrange("p (b s k) -> p b s k", b=2, k=2)
        frstd = pT[:, 1, 2, 0:2 * S].rearrange("p (b s) -> p b s", b=2)
        fin = (x1, x1b)

        bank = [ctx.enter_context(nc.psum_tensor(f"bank{i}", [P, 512], F32)) for i in (0, 1)]
        quad = ctx.enter_context(nc.psum_tensor("quad", [P, 4, 512], F32))
        bank += [quad[:, i] for i in range(4)]
        pair = ctx.enter_context(nc.psum_tensor("pair", [P, 2, 512], F32))
        bank += [pair[:, i] for i in range(2)]
        bank = [b if i > 1 else b[:, :] for i, b in enumerate(bank)]
        y_ps = quad[:, 2:4]

        xg = nc.dram_tensor("xg", (E * STRIDE + P, ROW), F32, kind="Internal").ap()
        y2 = nc.dram_tensor("y2", (2 * B * L + (NT + 1) * P, D), F32, kind="Internal").ap()
        y2r = y2[0:2 * B * L, :].rearrange("(g s t k) d -> g t s (k d)", s=S, t=L, k=2)

        names = """passed w_load w_later w13_load pool_const dve_const act_const
        x_load ctx_load mask_load w2_load xT_ps xT_sb conv_ps res_ps u_sb sres_sb bc_ps dtl_ps bc_hi bc_res1 bc_mid_s bc3_sb dtl_sb
        z_ps zabs_sb zexp_sb softp delta_sb du_sb delta_set
        b_ps b_sb bu_sb a_ps h_sb c_ps hc_sb y_sum yg_sb o_ps
        ln_sum ln_stat ln_var ln_log ln_rstd x1_sb x1b_sb ln_part x1T_ps x1T_sb cT_ps cT_sb proj_ps v_ps v_sb rot_sb qk_sb k_heads_sb
        pad_sb mask_sb s_ps s_max s_neg p_sb rden_sb pn_sb pT_ps pT_sb pT3_sb pv_ps ao_own_sb aoT_sb wo_ps
        x2_sb x2T_ps x2T_sb lg_ps route gexp_sb rank_ps pos_sb scat x2_sent
        tail tail_store table_sb table_link
        xs_load0 xs_load1 xs_load2 xs_load3 xsT_ps xsT_sb up_ps silu_sb gate_sb gT_ps gT_sb y_ps_s y_sb place_sb dest_sb y_out0 y_out1 y_out2 y_out3
        yk_load0 yk_load1 yk_load2 yk_load3 acc_s f_stat f_var f_log f_rstd fin_sb fin_rest fin_store0 fin_store1""".split()
        s = {n: sem(n) for n in names}

        xr = a["x"].rearrange("(g s) t d -> g t s d", s=S)
        cr = a["ctx_1024"].rearrange("(g s) t d -> g t s d", s=S)
        mr = a["mask"].rearrange("(g t) -> g t", t=T)
        outr = out.rearrange("(g s) t d -> g t s d", s=S)
        block = ctx.enter_context(nc.Block())

        W_LOADS, W_LATER = [], []

        def load(dst, src):
            W_LOADS.append((dst, src))

        def load_later(dst, src):
            W_LATER.append((dst, src))

        load(w_in[:, :], a["W_in"])
        load(conv_taps, a["conv_w"].partition_broadcast(P))
        load(conv_b[:, :], a["conv_b"])
        load(w_dtl[:, :, :], a["W_x"][:, :, 0:DTR])
        for r in range(3):
            load(w_bc[:, :, r, :], a["W_x"][:, :, DTR:DTR + 2 * NST])
        load(w_dt[:, :], a["W_dt"])
        load(b_dt[:, :], a["b_dt"])
        load_later(w_out[:, :, :], a["W_out"])
        load(a_log[:, :, :], a["A_log"])
        load(d_col[:, :], a["D"])
        for dst, n in ((wqT, "WqT"), (wqrT, "WqrT"), (wkT, "WkT"), (wkrT, "WkrT"), (wvT, "WvT"), (woT, "WoT")):
            load_later(dst[:, :], a[n])
        load_later(bo_b[:, :], a["bo"].partition_broadcast(P))
        load_later(rope[:, :, :], a["rope"])
        load_later(gate_wT[:, :], a["gate_wT"])
        NW, NL = len(W_LOADS), len(W_LATER)

        def early(eng, which):
            for n in which.split():
                eng.sem_inc(s[n], 16 if n in ("fin_store0", "fin_store1") else 1)

        def plain(eng):
            eng.sem_inc(s["passed"], 1)

        @block.sync
        def _(sp):
            early(sp, "fin_store0 fin_store1")
            sp.dma_start(xn[:, :, :], xr[0]).then_inc(s["x_load"], 16)
            for dst, src in W_LOADS[::2]:
                sp.dma_start(dst, src).then_inc(s["w_load"], 16)
            for dst, src in W_LATER:
                sp.dma_start(dst, src).then_inc(s["w_later"], 16)

            def group_in(g, dst, src, count):
                sp.dma_start(dst[:, :, :], src[bass.ds(g, 1)].rearrange("g t s d -> (g t) s d")).then_inc(s[count], 16)

            def mask_in(g):
                sp.dma_start(mask_b[:, :], mr[bass.ds(g, 1)].rearrange("a t -> (a t)").partition_broadcast(P)).then_inc(s["mask_load"], 16)

            group_in(0, cn, cr, "ctx_load")
            mask_in(0)
            for dst, src in ((w1, a["w1T"]), (w3, a["w3T"])):
                sp.dma_start(dst[:, :, :], src).then_inc(s["w13_load"], 16)
            with sp.Fori(0, G - 1) as g:
                sp.wait_ge(s["cT_ps"], g + 1)
                plain(sp)
                group_in(g + 1, cn, cr, "ctx_load")
                sp.wait_ge(s["ln_sum"], 1 + g * 2 + 1)
                plain(sp)
                group_in(g + 1, xn, xr, "x_load")
                sp.wait_ge(s["pad_sb"], 1 + g + 1)
                plain(sp)
                mask_in(g + 1)
            sp.wait_ge(s["pv_ps"], G * 4 * S)
            sp.dma_start(w2, a["w2T"]).then_inc(s["w2_load"], 16)
            sp.wait_ge(s["tail"], 1)
            for e in range(E):
                r = sp.value_load(tail_i[0:1, e:e + 1], min_val=0, max_val=E * STRIDE - P)
                sp.dma_start(xg[bass.ds(r, P), :], zrow[:, :]).then_inc(s["tail_store"], 16)
            sp.dma_start(xg[E * STRIDE:, :], zrow[:, :]).then_inc(s["tail_store"], 16)
            sp.wait_ge(s["table_sb"], 1)
            sp.wait_ge(s["scat"], G * 2 * S * 16)
            sp.wait_ge(s["tail_store"], (E + 1) * 16)

            def rows_in(j, b):
                r = sp.value_load(table[0:1, 1, bass.ds(j, 1)], min_val=0, max_val=E * STRIDE)
                sp.dma_start(xs[:, b, :], xg[bass.ds(r, P), :]).then_inc(s[f"xs_load{b}"], 16)

            for j in range(4):
                rows_in(j, j)
            for j in range(3):
                sp.wait_ge(s["xsT_ps"], 1 + j + 1)
                sp.wait_ge(s["dest_sb"], j + 1)
                rows_in(j + 4, j)
            with sp.Fori(0, NT // 4) as it:
                for b in range(4):
                    j = it * 4 + b
                    sp.wait_ge(s["xsT_ps"], 1 + j + 4)
                    plain(sp)
                    sp.wait_ge(s["dest_sb"], j + 4)
                    plain(sp)
                    rows_in(j + 7, (b + 3) % 4)

            def results_in(g, b):
                sp.dma_start(yk[b].rearrange("p (s k) d -> p s (k d)", k=2), y2r[bass.ds(g, 1)].rearrange("g t s d -> (g t) s d")).then_inc(s[f"yk_load{b}"], 16)

            def store(g, b):
                for n in ("fin_sb", "fin_rest"):
                    sp.wait_ge(s[n], (g + 1) * (S // 2))
                    if not isinstance(g, int):
                        plain(sp)
                sp.dma_start(outr[bass.ds(g, 1)].rearrange("g t s d -> (g t) s d"), fin[b][:, :, :]).then_inc(s[f"fin_store{b}"], 16)

            for b in range(4):
                sp.wait_ge(s[f"y_out{b}"], NT // 4 * 16)
            for b in range(4):
                results_in(b, b)
            with sp.Fori(0, G // 4 - 1) as it:
                for b in range(4):
                    store(4 * it + b, b % 2)
                    results_in(4 * it + b + 4, b)
            for b in range(4):
                store(G - 4 + b, b % 2)
            for b in range(2):
                sp.wait_ge(s[f"fin_store{b}"], 16 + 16 * (G // 2))

        @block.gpsimd
        def _(pool):
            g_ = nc.gpsimd
            early(pool, "pad_sb delta_sb bu_sb x2_sent")
            cs = [0]

            def link(ins):
                cs[0] += 1
                ins.then_inc(s["pool_const"], 1)
                pool.wait_ge(s["pool_const"], cs[0])

            link(g_.memset(ident[:, :], 0.0))
            link(g_.affine_select(out=ident[:, :], in_=ident[:, :], compare_op=ALU.not_equal, fill=1.0, base=0,
                                  pattern=[[-1, P]], channel_multiplier=1))
            link(g_.memset(causal[:, :], 0.0))
            link(g_.affine_select(out=causal[:, :], in_=causal[:, :], compare_op=ALU.is_ge, fill=NEG, base=0,
                                  pattern=[[-1, L]], channel_multiplier=1))
            link(g_.memset(ones_b[:, :], 1.0))
            link(g_.affine_select(out=tri[:, :], in_=ones_b[:, :], compare_op=ALU.is_gt, fill=0.0, base=0,
                                  pattern=[[1, P]], channel_multiplier=-1))
            link(g_.memset(zrow[:, :], 0.0))
            link(g_.iota(zrow[:, D:D + 1], pattern=[[1, 1]], base=2 * B * L, channel_multiplier=1, allow_small_or_imprecise_dtypes=True))
            link(g_.memset(zrow[:, D + 1:D + 2], -1.0))
            link(g_.memset(xT[:, :, :], 0.0))
            link(g_.memset(eps_col[:, :], EPS))
            link(g_.memset(one_col[:, :], 1.0))
            link(g_.memset(ones8[:, :], 1.0))
            link(g_.iota(iota8[:, :], pattern=[[1, E]], base=0, channel_multiplier=0, allow_small_or_imprecise_dtypes=True))
            link(g_.iota(base[:, :], pattern=[[STRIDE, E]], base=0, channel_multiplier=0, allow_small_or_imprecise_dtypes=True))
            link(g_.iota(erow[:, :], pattern=[[STRIDE, E]], base=0, channel_multiplier=0, allow_small_or_imprecise_dtypes=True))
            link(g_.iota(tok2[:, :], pattern=[[2 * L, S]], base=0, channel_multiplier=2, allow_small_or_imprecise_dtypes=True))
            link(g_.iota(k128[:, :], pattern=[[P, B]], base=0, channel_multiplier=0, allow_small_or_imprecise_dtypes=True))
            link(g_.iota(jrow[:, :], pattern=[[1, NT + 8]], base=0, channel_multiplier=0, allow_small_or_imprecise_dtypes=True))

            def work(g):
                pool.wait_ge(s["softp"], g + 1)
                pool.wait_ge(s["a_ps"], 1 + g * 2 * NST)
                g_.tensor_tensor(delta[:, :, :], zpos[:, :, :], zabs[:, :, :], ALU.add).then_inc(s["delta_sb"], 1)
                pool.wait_ge(s["delta_sb"], 1 + g + 1)
                g_.tensor_tensor(du[:, :, :], delta[:, :, :], u[:, :, :], ALU.mult).then_inc(s["du_sb"], 1)
                pool.wait_ge(s["du_sb"], g + 1)
                plain(pool)
                for h in range(2):
                    last = g_.memset(delta[:, h, :].rearrange("p (s t) -> p s t", s=S)[:, :, 0:1], RESET)
                    last.then_inc(s["delta_set"], 1)
                for n in range(NST):
                    pool.wait_ge(s["b_sb"], 1 + g * NST + n + 1)
                    pool.wait_ge(s["h_sb"], 1 + g * 2 * NST + max(0, 2 * n - 4))
                    g_.tensor_tensor(bu[:, n % 3], du[:, :, :], b_row[:, n % AHEAD, :].unsqueeze(1).broadcast_to((P, 2, T)),
                                     ALU.mult).then_inc(s["bu_sb"], 1)
                pool.wait_ge(s["mask_load"], g * 16 + 16)
                plain(pool)
                g_.tensor_scalar(pad[:, :], mask_b[:, :], 0.0, NEG, ALU.is_equal, ALU.mult).then_inc(s["pad_sb"], 1)
                pool.wait_ge(s["pad_sb"], 1 + g + 1)
                pool.wait_ge(s["s_ps"], 1 + g * 8)
                g_.tensor_tensor(mbias[:, :, :], pad[:, :].rearrange("p (s t) -> p s t", s=S),
                                 causal[:, :].unsqueeze(1).broadcast_to((P, S, L)), ALU.add).then_inc(s["mask_sb"], 1)
                for i in (1, 0):
                    pool.wait_ge(s["rot_sb"], g * 4 + 4 - 2 * i)
                    g_.tensor_tensor(qk[:, i, :], rot[:, 2 * i, :], rot[:, 2 * i + 1, :], ALU.add).then_inc(s["qk_sb"], 1)
                pool.wait_ge(s["x1_sb"], g * S + S)
                pool.wait_ge(s["ln_sum"], 1 + g * 2)
                g_.tensor_tensor(x1b[:, :, :], x1[:, :, :], bo_b[:, :].unsqueeze(1).broadcast_to((P, S, D)), ALU.add).then_inc(s["x1b_sb"], 1)

            def scatter(g):
                pool.wait_ge(s["pos_sb"], 1 + g + 1)
                plain(pool)
                for t in range(S):
                    for k in range(2):
                        pool.indirect_dma_start(xg[:, :], bass.IndirectOffsetOnAxis(ap=pos[:, t, k:k + 1], axis=0),
                                                x2[:, t, :], None).then_inc(s["scat"], 16)
                pool.wait_ge(s["scat"], (g + 1) * 2 * S * 16)
                pool.sem_inc(s["x2_sent"], 1)

            pool.wait_ge(s["w_later"], 16 * NL)
            work(0)
            with pool.Fori(1, G) as g:
                work(g)
                scatter(g - 1)
            scatter(G - 1)
            with pool.Fori(0, NT // 8) as it:
                for b in range(8):
                    pool.wait_ge(s["y_sb"], 1 + it * 8 + b + 1)
                    plain(pool)
                    pool.indirect_dma_start(y2[:, :], bass.IndirectOffsetOnAxis(ap=dest[:, b:b + 1], axis=0),
                                            ys[:, b % 4, :], None).then_inc(s[f"y_out{b % 4}"], 16)

            with pool.Fori(0, G // 2) as it:
                for b in range(2):
                    pool.wait_ge(s["f_rstd"], 2 * it + b + 1)
                    plain(pool)
                    pool.wait_ge(s[f"fin_store{b}"], 16 + it * 16)
                    plain(pool)
                    for t in range(S // 2, S):
                        g_.tensor_scalar(fin[b][:, t, :], acc[b][:, t, :], fmv[:, b, t, 0:1], frstd[:, b, t:t + 1],
                                         ALU.subtract, ALU.mult).then_inc(s["fin_rest"], 1)

        @block.scalar
        def _(act):
            A = nc.scalar.activation
            early(act, "a_ps b_sb")
            for dst, src in W_LOADS[1::2]:
                act.dma_start(dst, src).then_inc(s["w_load"], 16)
            act.wait_ge(s["w_load"], 16 * NW)
            act.wait_ge(s["pool_const"], 19)
            A(a_neg[:, :, :], a_log[:, :, :], ACT.Exp).then_inc(s["act_const"], 1)
            act.wait_ge(s["dve_const"], 8)

            def x_in(m):
                act.wait_ge(s["xT_ps"], m + 1)
                A(xT[:, :, KCONV - 1:], bank[7].rearrange("p (s t) -> p s t", s=S), ACT.Copy).then_inc(s["xT_sb"], 1)

            def silus(m):
                nc.scalar.preload_act_table_set("silu_and_others")
                for h in range(2):
                    act.wait_ge(s["conv_ps"], m * 2 + h + 1)
                    A(u[:, h, :], bank[h], ACT.Silu, bias=conv_b[:, h:h + 1]).then_inc(s["u_sb"], 1)
                for h in range(2):
                    act.wait_ge(s["res_ps"], m * 2 + h + 1)
                    A(sres[:, h, :], bank[6 + h], ACT.Silu).then_inc(s["sres_sb"], 1)
                nc.scalar.preload_act_table_set("natural_log_exp_and_others")

            def bc_hi(m):
                act.wait_ge(s["bc_ps"], m + 1)
                A(bc3[:, :], bank[0][0:96, :], ACT.Copy).then_inc(s["bc_hi"], 1)
                act.wait_ge(s["dtl_ps"], m + 1)
                A(dtl[:, :], bank[1][0:DTR, :], ACT.Copy).then_inc(s["dtl_sb"], 1)

            def bc_middle(m):
                act.wait_ge(s["bc_res1"], m + 1)
                A(bc_mid[:, :], bc_rest[:, :], ACT.Copy).then_inc(s["bc_mid_s"], 1)

            def step_parts(m, h):
                act.wait_ge(s["delta_sb"], 1 + m)
                act.wait_ge(s["z_ps"], m * 2 + h + 1)
                A(zabs[:, h, :], bank[1], ACT.Abs, bias=b_dt[:, h:h + 1]).then_inc(s["zabs_sb"], 1)
                A(zpos[:, h, :], bank[1], ACT.Relu, bias=b_dt[:, h:h + 1]).then_inc(s["zabs_sb"], 1)

            def step_exp(m):
                act.wait_ge(s["zabs_sb"], m * 4 + 4)
                A(zabs[:, :, :], zabs[:, :, :], ACT.Exp, scale=-1.0).then_inc(s["zexp_sb"], 1)

            def step_log(m):
                act.wait_ge(s["zexp_sb"], m + 1)
                A(zabs[:, :, :], zabs[:, :, :], ACT.Ln, bias=one_col[:, :]).then_inc(s["softp"], 1)

            def b_out(m, n):
                act.wait_ge(s["b_ps"], m * NST + n + 1)
                act.wait_ge(s["bu_sb"], 1 + m * NST + max(0, n - AHEAD + 1))
                A(b_row[:, n % AHEAD, :], bank[n % 2], ACT.Copy).then_inc(s["b_sb"], 1)

            def decay(m, n):
                for h in range(2):
                    act.wait_ge(s["h_sb"], 1 + m * 2 * NST + max(0, 2 * n + h - 1))
                    A(bank[6 + h], delta[:, h, :], ACT.Exp, scale=a_neg[:, h, n:n + 1]).then_inc(s["a_ps"], 1)

            def scan_start(m):
                for n in range(AHEAD - 1):
                    b_out(m, n)
                act.wait_ge(s["delta_set"], m * 2 + 2)
                decay(m, 0)

            def group(g, last):
                for n in range(1, NST):
                    decay(g, n)
                    if n + AHEAD - 1 < NST:
                        b_out(g, n + AHEAD - 1)

                def ln_scale(k):
                    act.wait_ge(s["ln_var"], g * 2 + k + 1)
                    A(lnv[:, :], mv[:, :, 1], ACT.Ln, bias=eps_col[:, :]).then_inc(s["ln_log"], 1)
                    act.wait_ge(s["ln_log"], g * 2 + k + 1)
                    A(rstd[:, :], lnv[:, :], ACT.Exp, scale=-0.5).then_inc(s["ln_rstd"], 1)

                def exps(t, k):
                    act.wait_ge(s["s_neg"], g * 8 + 2 * t + k + 1)
                    if t >= 2:
                        act.wait_ge(s["pT_ps"], g * 16 + 4 * (t - 2) + 2 * k + 2)
                    for h in range(8 * k, 8 * k + 8):
                        c, j = divmod(h, 4)
                        last = A(prob[:, t % 2, c, j, :], bank[2 + c][:, j * L:(j + 1) * L], ACT.Exp, bias=nmax[:, t % 2, h:h + 1],
                                 accum_out=den[:, t % 2, h:h + 1])
                    last.then_inc(s["p_sb"], 1)

                def pT_out(t, c):
                    act.wait_ge(s["pT_ps"], g * 16 + 4 * t + c + 1)
                    A(pT[:, c % 2], bank[6 + c % 2].rearrange("p (j q) -> p j q", j=4), ACT.Copy).then_inc(s["pT_sb"], 1)

                act.wait_ge(s["cT_ps"], g + 1)
                A(cT[:, :], bank[1], ACT.Copy).then_inc(s["cT_sb"], 1)
                ln_scale(0)
                act.wait_ge(s["x1T_ps"], g + 1)
                A(x1T[:, :], bank[0], ACT.Copy).then_inc(s["x1T_sb"], 1)
                if not last:
                    x_in(g + 1)
                act.wait_ge(s["v_ps"], g + 1)
                A(v[:, :, :], bank[6].rearrange("p (s d) -> p s d", s=S), ACT.Copy).then_inc(s["v_sb"], 1)
                if not last:
                    silus(g + 1)
                exps(0, 0)
                if not last:
                    bc_hi(g + 1)
                exps(0, 1)
                for t in range(S):
                    for k in range(2):
                        pT_out(t, 2 * k)
                        if k == 0:
                            pT_out(t, 1)
                        if t == 0 and not last:
                            step_parts(g + 1, k)
                            if k == 0:
                                bc_middle(g + 1)
                        if t + 1 < S:
                            exps(t + 1, k)
                        if t == 1 and not last:
                            (step_exp, step_log)[k](g + 1)
                ln_scale(1)
                if not last:
                    scan_start(g + 1)
                act.wait_ge(s["x2T_ps"], g + 1)
                A(x2T[:, :], bank[3], ACT.Copy).then_inc(s["x2T_sb"], 1)
                if not last:
                    b_out(g + 1, AHEAD - 1)
                act.wait_ge(s["route"], 1 + g * ROUTER_LINKS + GAPS)
                A(gexp[:, :, :, :], gap[:, :, :, :], ACT.Exp, scale=-1.0).then_inc(s["gexp_sb"], 1)

            x_in(0)
            silus(0)
            bc_hi(0)
            bc_middle(0)
            step_parts(0, 0)
            step_parts(0, 1)
            step_exp(0)
            step_log(0)
            scan_start(0)
            b_out(0, AHEAD - 1)
            with act.Fori(0, G - 1) as g:
                group(g, False)
            group(G - 1, True)
            def x_out(j, b):
                act.wait_ge(s["xsT_ps"], 1 + j + 1)
                A(xsT[:, b, :], bank[7][:, b * P:(b + 1) * P], ACT.Copy).then_inc(s["xsT_sb"], 1)

            def silu(j, b):
                act.wait_ge(s["up_ps"], 1 + 2 * j + 1)
                A(sl[:, b, :], bank[b], ACT.Silu).then_inc(s["silu_sb"], 1)

            nc.scalar.preload_act_table_set("silu_and_others")
            x_out(0, 0)
            x_out(1, 1)
            silu(0, 0)
            act.wait_ge(s["up_ps"], 1 + 2)
            x_out(2, 0)
            silu(1, 1)
            with act.Fori(0, NT // 2) as it:
                for b in range(2):
                    j = it * 2 + b
                    act.wait_ge(s["gT_ps"], j + 1)
                    A(gT[:, b], bank[4 + b].rearrange("p (c n) -> p c n", c=FC), ACT.Copy).then_inc(s["gT_sb"], 1)
                    x_out(j + 3, 1 - b)
                    silu(j + 2, b)
            nc.scalar.preload_act_table_set("natural_log_exp_and_others")
            with act.Fori(0, G // 2) as it:
                for b in range(2):
                    g = 2 * it + b
                    act.wait_ge(s["f_var"], g + 1)
                    A(lnv[:, :], fmv[:, b, :, 1], ACT.Ln, bias=eps_col[:, :]).then_inc(s["f_log"], 1)
                    act.wait_ge(s["f_log"], g + 1)
                    A(frstd[:, b, :], lnv[:, :], ACT.Exp, scale=-0.5).then_inc(s["f_rstd"], 1)
                    act.wait_ge(s["f_rstd"], g + 1)

        @block.vector
        def _(dve):
            v_ = nc.vector
            TT = v_.tensor_tensor
            early(dve, "ln_sum h_sb hc_sb acc_s route pos_sb gate_sb y_sb")
            dve.wait_ge(s["pool_const"], 19)
            v_.tensor_copy(identb[:, :], ident[:, :]).then_inc(s["dve_const"], 1)
            v_.tensor_reduce(out=hot[:, :], in_=ident[:, :].rearrange("p (h d) -> p h d", h=H), axis=AX.X, op=ALU.add).then_inc(s["dve_const"], 1)
            v_.tensor_reduce(out=sel32[:, :], in_=ident[0:96, 0:96].rearrange("p (r j) -> p j r", r=3), axis=AX.X, op=ALU.add).then_inc(s["dve_const"], 1)
            dve.wait_ge(s["dve_const"], 3)
            v_.tensor_reduce(out=own[:, :], in_=hot[:, :].rearrange("p (c j) -> p j c", c=4), axis=AX.X, op=ALU.add).then_inc(s["dve_const"], 1)
            v_.tensor_copy(sel[:, :, :], sel32[:, :].unsqueeze(2).broadcast_to((96, 2 * NST, P))).then_inc(s["dve_const"], 1)
            dve.wait_ge(s["w_load"], 16 * NW)
            TT(w_conv[:, :, :], conv_taps, w_in[:, 0:DIN].unsqueeze(1).broadcast_to((P, KCONV, DIN)), ALU.mult).then_inc(s["dve_const"], 1)
            for h in range(2):
                last = v_.tensor_scalar(d_diag[:, h, :], ident[:, :], d_col[:, h:h + 1], None, ALU.mult)
            last.then_inc(s["dve_const"], 1)
            dve.wait_ge(s["act_const"], 1)
            v_.tensor_scalar(a_neg[:, :, :], a_neg[:, :, :], -1.0, None, ALU.mult).then_inc(s["dve_const"], 1)
            dve.wait_ge(s["dve_const"], 8)

            def layer_norm(src, res, dst, g, k, added=range(S)):
                r = slice(added[0], S)
                TT(sx[:, r, :], src[:, r, :], res[:, r, :], ALU.add).then_inc(s["ln_sum"], 1)
                dve.wait_ge(s["ln_sum"], 1 + g * 2 + k + 1)
                for t in added:
                    end = v_.bn_stats(stats[:, t, :], sx[:, t, :])
                end.then_inc(s["ln_stat"], 1)
                dve.wait_ge(s["ln_stat"], g * 2 + k + 1)
                plain(dve)
                for t in range(S):
                    end = v_.bn_aggr(mv[:, t, :], stats[:, t, :])
                end.then_inc(s["ln_var"], 1)
                dve.wait_ge(s["ln_rstd"], g * 2 + k + 1)
                for t in range(S):
                    v_.tensor_scalar(dst[:, t, 0:D], sx[:, t, :], mv[:, t, 0:1], rstd[:, t:t + 1], ALU.subtract, ALU.mult).then_inc(s[("x1_sb", "x2_sb")[k]], 1)

            def bc_residue(m):
                dve.wait_ge(s["bc_hi"], m + 1)
                TT(bc_rest[:, :], bank[0][0:96, :], bc3[:, :], ALU.subtract).then_inc(s["bc_res1"], 1)

            def bc_low(m):
                dve.wait_ge(s["bc_mid_s"], m + 1)
                TT(bc3[64:96, :], bc_rest[64:96, :], bc_mid[64:96, :], ALU.subtract).then_inc(s["bc3_sb"], 1)
                v_.tensor_copy(bc3[32:64, :], bc_mid[32:64, :]).then_inc(s["bc3_sb"], 1)

            def states(m, n):
                dve.wait_ge(s["hc_sb"], 1 + m * NST + max(0, n - 2))
                for h in range(2):
                    dve.wait_ge(s["a_ps"], 1 + m * 2 * NST + 2 * n + h + 1)
                    dve.wait_ge(s["bu_sb"], 1 + m * NST + n + 1)
                    v_.tensor_tensor_scan(hst[:, n % 3, h, :], bank[6 + h], bu[:, n % 3, h, :], 0.0, ALU.mult, ALU.add).then_inc(s["h_sb"], 1)

            def group(g, last):
                def times_c(n):
                    dve.wait_ge(s["h_sb"], 1 + g * 2 * NST + 2 * n + 2)
                    dve.wait_ge(s["c_ps"], g * NST + n + 1)
                    dve.wait_ge(s["y_sum"], 1 + g * NST + max(0, n - 2))
                    TT(hc[:, n % 3], hst[:, n % 3], bank[2 + n % 2].unsqueeze(1).broadcast_to((P, 2, T)), ALU.mult).then_inc(s["hc_sb"], 1)

                for n in range(2, NST):
                    times_c(n - 2)
                    states(g, n)
                times_c(NST - 2)
                times_c(NST - 1)
                dve.wait_ge(s["y_sum"], 1 + g * NST + NST)
                dve.wait_ge(s["sres_sb"], g * 2 + 2)
                TT(yg[:, :, :], y_ps, sres[:, :, :], ALU.mult).then_inc(s["yg_sb"], 1)
                dve.wait_ge(s["o_ps"], g + 1)
                layer_norm(bank[0].rearrange("p (s d) -> p s d", s=S), xn, x1, g, 0)
                for n, i in enumerate((2, 3, 0, 1)):
                    bk = 2 + i
                    dve.wait_ge(s["proj_ps"], g * 4 + n + 1)
                    TT(rot[:, i, :].rearrange("p (s t) -> p s t", s=S), bank[bk].rearrange("p (s t) -> p s t", s=S),
                       rope[:, i, :].unsqueeze(1).broadcast_to((P, S, L)), ALU.mult).then_inc(s["rot_sb"], 1)

                dve.wait_ge(s["qk_sb"], g * 2 + 2)
                for j in range(4):
                    v_.tensor_scalar(k_heads[:, j, :], qk[:, 1, :], own[:, j:j + 1], None, ALU.mult).then_inc(s["k_heads_sb"], 1)

                def maxima(t, k):
                    sc = quad[:, 2 * k:2 * k + 2].rearrange("p c (j m) -> p (c j) m", j=4)
                    hs = slice(8 * k, 8 * k + 8)
                    dve.wait_ge(s["s_ps"], 1 + g * 8 + 2 * t + k + 1)
                    v_.tensor_reduce(out=smax[:, t % 2, hs], in_=sc, axis=AX.X, op=ALU.max).then_inc(s["s_max"], 1)
                    dve.wait_ge(s["s_max"], g * 8 + 2 * t + k + 1)
                    v_.tensor_scalar(nmax[:, t % 2, hs], smax[:, t % 2, hs], -1.0, None, ALU.mult).then_inc(s["s_neg"], 1)

                def normed(t, k):
                    hs = slice(8 * k, 8 * k + 8)
                    dve.wait_ge(s["p_sb"], g * 8 + 2 * t + k + 1)
                    v_.reciprocal(rden[:, t % 2, hs], den[:, t % 2, hs]).then_inc(s["rden_sb"], 1)
                    dve.wait_ge(s["rden_sb"], g * 8 + 2 * t + k + 1)
                    pr = prob[:, t % 2, 2 * k:2 * k + 2].rearrange("p c j m -> p (c j) m")
                    TT(pr, pr, rden[:, t % 2, hs].unsqueeze(2).broadcast_to((P, 8, L)), ALU.mult).then_inc(s["pn_sb"], 1)

                def pT_out(t):
                    dve.wait_ge(s["pT_ps"], g * 16 + 4 * t + 4)
                    v_.tensor_copy(pT[:, 1], bank[7].rearrange("p (j q) -> p j q", j=4)).then_inc(s["pT3_sb"], 1)

                def own_heads(t):
                    dve.wait_ge(s["pv_ps"], g * 4 * S + 4 * t + 4)
                    TT(ao_own[:, t % 2], bank[t % 2].rearrange("p (j q) -> p j q", j=4), own[:, :].unsqueeze(2).broadcast_to((P, 4, L)),
                       ALU.mult).then_inc(s["ao_own_sb"], 1)
                    dve.wait_ge(s["ao_own_sb"], g * S + t + 1)
                    v_.tensor_reduce(out=aoT[:, t * L:(t + 1) * L], in_=ao_own[:, t % 2].rearrange("p j q -> p q j"), axis=AX.X,
                                     op=ALU.add).then_inc(s["aoT_sb"], 1)

                for k in range(2):
                    maxima(0, k)
                if not last:
                    bc_residue(g + 1)
                for k in range(2):
                    normed(0, k)
                for t in range(S):
                    if t + 1 < S:
                        maxima(t + 1, 0)
                        if t:
                            own_heads(t - 1)
                        maxima(t + 1, 1)
                        pT_out(t)
                        normed(t + 1, 0)
                        if t == 0 and not last:
                            bc_low(g + 1)
                        normed(t + 1, 1)
                own_heads(S - 2)
                pT_out(S - 1)
                dve.wait_ge(s["wo_ps"], g * 2 + 1)
                dve.wait_ge(s["x1b_sb"], g + 1)
                TT(sx[:, 0:S - 1, :], bank[2][:, 0:(S - 1) * D].rearrange("p (s d) -> p s d", d=D), x1b[:, 0:S - 1, :], ALU.add).then_inc(s["ln_part"], 1)
                dve.wait_ge(s["ln_part"], g + 1)
                plain(dve)
                for t in range(S - 1):
                    v_.bn_stats(stats[:, t, :], sx[:, t, :])
                own_heads(S - 1)
                dve.wait_ge(s["wo_ps"], g * 2 + 2)
                dve.wait_ge(s["x2_sent"], 1 + g)
                layer_norm(bank[3].rearrange("p (s d) -> p s d", s=S), x1b, x2, g, 1, range(S - 1, S))
                c = [0]

                def step(ins, wait=True):
                    c[0] += 1
                    ins.then_inc(s["route"], 1)
                    if wait:
                        dve.wait_ge(s["route"], 1 + g * ROUTER_LINKS + c[0])

                def both(x):
                    return x.unsqueeze(2).broadcast_to((P, S, 2, E))

                dve.wait_ge(s["x2_sb"], g * S + S)
                step(v_.tensor_copy(x2_all[:, bass.ds(g * S, S), :], x2[:, :, 0:D]), False)
                if not last:
                    states(g + 1, 0)
                dve.wait_ge(s["lg_ps"], g + 1)
                step(v_.tensor_copy(lg[:, :, :], bank[2][:, 0:S * E].rearrange("p (s e) -> p s e", s=S)))
                plain(dve)
                for t in range(S):
                    end = v_.max(m8[:, t, :], lg[:, t, :])
                step(end, False)
                step(v_.scalar_tensor_tensor(lab[:, :, :], lg[:, :, :], -1.0, lg[:, :, :], ALU.mult, ALU.max))
                plain(dve)
                for t in range(S):
                    end = v_.max_index(i8[:, t, :], m8[:, t, :], lg[:, t, :])
                step(end, False)
                mm = m8[:, :, 0:2].unsqueeze(3).broadcast_to((P, S, 2, E))
                step(TT(fac[:, :, :, :], both(lab[:, :, :]), mm, ALU.max), False)
                step(TT(gap[:, :, :, :], mm, both(lg[:, :, :]), ALU.subtract))
                assert c[0] == GAPS
                step(v_.tensor_copy(idxf[:, :, :], i8[:, :, 0:2]), False)
                step(v_.tensor_scalar(thr[:, :, :, :], fac[:, :, :, :], 0.02, None, ALU.mult))
                step(TT(oh[:, :, :, :], iota8[:, :].unsqueeze(1).unsqueeze(1).broadcast_to((P, S, 2, E)),
                        idxf[:, :, :].unsqueeze(3).broadcast_to((P, S, 2, E)), ALU.is_equal))
                step(TT(ohb[:, :, :], oh[:, :, 0, :], oh[:, :, 1, :], ALU.add), False)
                assert c[0] == CHOSEN
                step(TT(keep[:, :, :, :], thr[:, :, :, :], gap[:, :, :, :], ALU.is_ge))
                step(v_.tensor_copy(x2[:, :, D], tok2[:, :]), False)
                step(v_.tensor_copy(x2[:, :, D + 1], idxf[:, :, 1]), False)
                dve.wait_ge(s["rank_ps"], g + 1)
                rk = bank[2][:, 2 * S * E:(3 * S + 1) * E].rearrange("p (s e) -> p s e", e=E)
                step(TT(rank[:, :, :], rk[:, 0:S, :], base[:, :].unsqueeze(1).broadcast_to((P, S, E)), ALU.add))
                step(TT(base[:, :], base[:, :], rk[:, S, :], ALU.add), False)
                step(TT(prk[:, :, :, :], both(rank[:, :, :]), oh[:, :, :, :], ALU.mult))
                step(v_.tensor_reduce(out=posf[:, :, :], in_=prk[:, :, :, :], axis=AX.X, op=ALU.add))
                v_.tensor_copy(pos[:, :, :], posf[:, :, :]).then_inc(s["pos_sb"], 1)
                if not last:
                    states(g + 1, 1)
                step(v_.tensor_scalar(tok2[:, :], tok2[:, :], float(2 * S * L), None, ALU.add), False)
                step(TT(keep[:, :, 1, :], keep[:, :, 1, :], oh[:, :, 0, :], ALU.is_gt), False)
                dve.wait_ge(s["gexp_sb"], g + 1)
                step(v_.tensor_scalar(gexp[:, :, :, :], gexp[:, :, :, :], 1.0, None, ALU.min))
                step(TT(gexp[:, :, :, :], gexp[:, :, :, :], keep[:, :, :, :], ALU.mult))
                step(v_.tensor_reduce(out=gsum[:, :, :], in_=gexp[:, :, :, :], axis=AX.X, op=ALU.add))
                step(v_.reciprocal(gates_all[:, bass.ds(g * S, S), :], gsum[:, :, :]))
                assert c[0] == ROUTER_LINKS

            bc_residue(0)
            bc_low(0)
            states(0, 0)
            states(0, 1)
            dve.wait_ge(s["w_later"], 16 * NL)
            with dve.Fori(0, G - 1) as g:
                group(g, False)
            group(G - 1, True)

            v_.tensor_copy(tail_i[:, :], base[:, :]).then_inc(s["tail"], 1)
            k = [0]

            def tlink(ins):
                k[0] += 1
                ins.then_inc(s["table_link"], 1)
                dve.wait_ge(s["table_link"], k[0])

            N2 = NT + 8
            tlink(TT(cnt[:, :], base[:, :], erow[:, :], ALU.subtract))
            tlink(TT(full[:, :, :], cnt[:, :].unsqueeze(2).broadcast_to((P, E, B)), k128[:, :].unsqueeze(1).broadcast_to((P, E, B)), ALU.is_gt))
            tlink(v_.tensor_reduce(out=ntile[:, :], in_=full[:, :, :], axis=AX.X, op=ALU.add))
            tlink(v_.tensor_tensor_scan(cum[:, :], ones8[:, :], ntile[:, :], 0.0, ALU.mult, ALU.add))
            tlink(TT(ind[:, :, :], jrow[:, :].unsqueeze(2).broadcast_to((P, N2, E)), cum[:, :].unsqueeze(1).broadcast_to((P, N2, E)), ALU.is_ge))
            tlink(v_.tensor_reduce(out=t_e[:, :], in_=ind[:, :, :], axis=AX.X, op=ALU.add))
            tlink(v_.tensor_scalar(jump[:, :], ntile[:, :], float(-P), float(STRIDE), ALU.mult, ALU.add))
            tlink(TT(wsum[:, :, :], ind[:, :, :], jump[:, :].unsqueeze(1).broadcast_to((P, N2, E)), ALU.mult))
            tlink(v_.tensor_reduce(out=t_row[:, :], in_=wsum[:, :, :], axis=AX.X, op=ALU.add))
            tlink(v_.tensor_scalar(j128[:, :], jrow[:, :], float(P), None, ALU.mult))
            tlink(TT(t_row[:, :], t_row[:, :], j128[:, :], ALU.add))
            tlink(v_.tensor_scalar(t_row[:, :], t_row[:, :], float(E * STRIDE), None, ALU.min))
            tlink(v_.tensor_scalar(t_e[:, :], t_e[:, :], float(E - 1), None, ALU.min))
            tlink(v_.tensor_copy(table[:, 0, :], t_e[:, :]))
            v_.tensor_copy(table[:, 1, :], t_row[:, :]).then_inc(s["table_sb"], 1)

            def gate(j, b):
                dve.wait_ge(s["up_ps"], 1 + 2 * j + 2)
                dve.wait_ge(s["silu_sb"], j + 1)
                TT(gg[:, b, :], sl[:, b, :], bank[2 + b], ALU.mult).then_inc(s["gate_sb"], 1)

            def destinations(j, load, turn, slot):
                dve.wait_ge(s[f"xs_load{load}"], turn * 16 + 16)
                second = xs[:, load, D + 1:D + 2]
                v_.tensor_scalar(spare[:, slot:slot + 1], second, 0.0, j128[:, bass.ds(j, 1)], ALU.is_lt, ALU.mult)
                v_.scalar_tensor_tensor(place[:, slot:slot + 1], second, t_e[:, bass.ds(j, 1)], xs[:, load, D:D + 1],
                                        ALU.is_equal, ALU.add).then_inc(s["place_sb"], 1)
                dve.wait_ge(s["place_sb"], j + 1)
                TT(dest[:, slot:slot + 1], spare[:, slot:slot + 1], place[:, slot:slot + 1], ALU.add).then_inc(s["dest_sb"], 1)

            def eight_tiles(it):
                for b in range(8):
                    j = it * 8 + b
                    gate(j + 2, b % 2)
                    dve.wait_ge(s["y_ps_s"], j + 1)
                    if not (isinstance(it, int) and b < 4):
                        dve.wait_ge(s[f"y_out{b % 4}"], (2 * it + b // 4) * 16)
                    v_.tensor_copy(ys[:, b % 4, :], bank[6][:, b % 2 * P:(b % 2 + 1) * P]).then_inc(s["y_sb"], 1)
                    destinations(j + 3, (b + 3) % 4, 2 * it + (b + 3) // 4, (b + 3) % 8)

            for j in range(3):
                destinations(j, j, 0, j)
            gate(0, 0)
            gate(1, 1)
            eight_tiles(0)
            with dve.Fori(1, NT // 8) as it:
                eight_tiles(it)
            def combine(g, load, turn):
                b = load % 2
                dve.wait_ge(s[f"yk_load{load}"], (turn + 1) * 16)
                if not (isinstance(g, int) and g < 2):
                    dve.wait_ge(s["fin_sb"], (g - 1) * (S // 2))
                    dve.wait_ge(s["fin_rest"], (g - 1) * (S // 2))
                for k in range(2):
                    for t in range(S):
                        src = x2_all[:, bass.ds(g * S + t, 1), :].rearrange("p a d -> p (a d)") if k == 0 else acc[b][:, t, :]
                        v_.scalar_tensor_tensor(acc[b][:, t, :], yk[load][:, 2 * t + k, :],
                                                gates_all[:, bass.ds(g * S + t, 1), k], src, ALU.mult, ALU.add).then_inc(s["acc_s"], 1)
                    dve.wait_ge(s["acc_s"], 1 + g * 2 * S + (k + 1) * S)
                for t in range(S):
                    end = v_.bn_stats(fstats[:, b, t, :], acc[b][:, t, :])
                end.then_inc(s["f_stat"], 1)
                dve.wait_ge(s["f_stat"], g + 1)
                plain(dve)
                for t in range(S):
                    end = v_.bn_aggr(fmv[:, b, t, :], fstats[:, b, t, :])
                end.then_inc(s["f_var"], 1)

            def last_norm(g, b, turn):
                dve.wait_ge(s["f_rstd"], g + 1)
                dve.wait_ge(s[f"fin_store{b}"], 16 + turn * 16)
                for t in range(S // 2):
                    v_.tensor_scalar(fin[b][:, t, :], acc[b][:, t, :], fmv[:, b, t, 0:1], frstd[:, b, t:t + 1],
                                     ALU.subtract, ALU.mult).then_inc(s["fin_sb"], 1)

            def four_groups(it, first=False):
                for b in range(4):
                    combine(4 * it + b, b, it)
                    if not (first and b == 0):
                        last_norm(4 * it + b - 1, (b + 1) % 2, 2 * it + (b - 1) // 2)

            four_groups(0, True)
            with dve.Fori(1, G // 4) as it:
                four_groups(it)
            last_norm(G - 1, 1, G // 2 - 1)

        @block.tensor
        def _(pe):
            MM = nc.tensor.matmul
            TR = nc.tensor.transpose
            early(pe, "s_ps xsT_ps up_ps y_sum")
            pe.wait_ge(s["w_load"], 16 * NW)
            pe.wait_ge(s["dve_const"], 8)

            def x_t(m):
                pe.wait_ge(s["x_load"], m * 16 + 16)
                for t in range(S):
                    last = TR(bank[7][:, t * L:(t + 1) * L], xn[:, t, :], ident[:, :])
                last.then_inc(s["xT_ps"], 1)

            def conv(m):
                pe.wait_ge(s["xT_sb"], m + 1)
                for h in range(2):
                    for k in range(KCONV):
                        last = MM(bank[h].rearrange("p (s t) -> p s t", s=S), w_conv[:, k, h * P:(h + 1) * P], xT[:, :, k:k + L],
                                  start=(k == 0), stop=(k == KCONV - 1))
                    last.then_inc(s["conv_ps"], 1)

            def res(m):
                for h in range(2):
                    MM(bank[6 + h].rearrange("p (s t) -> p s t", s=S), w_in[:, DIN + h * P:DIN + (h + 1) * P], xT[:, :, KCONV - 1:],
                       start=True, stop=True).then_inc(s["res_ps"], 1)

            def bc_dtl(m):
                pe.wait_ge(s["u_sb"], m * 2 + 2)
                for h in range(2):
                    last = MM(bank[0][0:96, :], w_bc[:, h].rearrange("p r n -> p (r n)"), u[:, h, :], start=(h == 0), stop=(h == 1))
                last.then_inc(s["bc_ps"], 1)
                for h in range(2):
                    last = MM(bank[1][0:DTR, :], w_dtl[:, h, :], u[:, h, :], start=(h == 0), stop=(h == 1))
                last.then_inc(s["dtl_ps"], 1)

            def steps(m, h):
                pe.wait_ge(s["dtl_sb"], m + 1)
                if h:
                    pe.wait_ge(s["zabs_sb"], m * 4 + 2)
                MM(bank[1], w_dt[:, h * P:(h + 1) * P], dtl[:, :], start=True, stop=True).then_inc(s["z_ps"], 1)

            def row_b(m, n):
                pe.wait_ge(s["b_sb"], 1 + m * NST + max(0, n - 1))
                MM(bank[n % 2], sel[:, n, :], bc3[:, :], start=True, stop=True).then_inc(s["b_ps"], 1)

            def scan_start(m):
                pe.wait_ge(s["bc3_sb"], m * 2 + 2)
                row_b(m, 0)
                row_b(m, 1)
                for h in range(2):
                    MM(bank[4 + h], d_diag[:, h, :], u[:, h, :], start=True, stop=False, skip_group_check=True)

            def group(g, final):
                def row_c(n):
                    pe.wait_ge(s["hc_sb"], 1 + g * NST + max(0, n - 1))
                    MM(bank[2 + n % 2], sel[:, NST + n, :], bc3[:, :], start=True, stop=True).then_inc(s["c_ps"], 1)

                pe.wait_ge(s["pos_sb"], 1 + g)
                row_c(0)
                row_c(1)
                for n in range(NST):
                    if n + AHEAD + 1 < NST:
                        row_b(g, n + AHEAD + 1)
                    if n + 2 < NST:
                        row_c(n + 2)
                    pe.wait_ge(s["hc_sb"], 1 + g * NST + n + 1)
                    for h in range(2):
                        last = MM(bank[4 + h], ident[:, :], hc[:, n % 3, h, :], start=False, stop=(n == NST - 1), skip_group_check=True)
                    last.then_inc(s["y_sum"], 1)
                pe.wait_ge(s["yg_sb"], g + 1)
                for t in range(S):
                    for h in range(2):
                        last = MM(bank[0][:, t * D:(t + 1) * D], yg[:, h, t * L:(t + 1) * L], w_out[:, h, :], start=(h == 0), stop=(h == 1))
                last.then_inc(s["o_ps"], 1)
                pe.wait_ge(s["ctx_load"], g * 16 + 16)
                for t in range(S):
                    last = TR(bank[1][:, t * L:(t + 1) * L], cn[:, t, :], ident[:, :])
                last.then_inc(s["cT_ps"], 1)
                pe.wait_ge(s["cT_sb"], g + 1)
                MM(bank[4], wkT[:, :], cT[:, :], start=True, stop=True).then_inc(s["proj_ps"], 1)
                MM(bank[5], wkrT[:, :], cT[:, :], start=True, stop=True).then_inc(s["proj_ps"], 1)
                for t in range(S):
                    last = MM(bank[6][:, t * D:(t + 1) * D], cT[:, t * L:(t + 1) * L], wvT[:, :], start=True, stop=True)
                last.then_inc(s["v_ps"], 1)
                pe.wait_ge(s["x1_sb"], g * S + S)
                for t in range(S):
                    last = TR(bank[0][:, t * L:(t + 1) * L], x1[:, t, :], ident[:, :])
                last.then_inc(s["x1T_ps"], 1)
                if not final:
                    x_t(g + 1)
                pe.wait_ge(s["x1T_sb"], g + 1)
                MM(bank[2], wqT[:, :], x1T[:, :], start=True, stop=True).then_inc(s["proj_ps"], 1)
                MM(bank[3], wqrT[:, :], x1T[:, :], start=True, stop=True).then_inc(s["proj_ps"], 1)
                if not final:
                    conv(g + 1)
                    pe.wait_ge(s["v_sb"], g + 1)
                    res(g + 1)
                pe.wait_ge(s["rot_sb"], g * 4 + 4)
                pe.wait_ge(s["mask_sb"], g + 1)

                def scores(t, k):
                    if t:
                        pe.wait_ge(s["p_sb"], g * 8 + 2 * (t - 1) + k + 1)
                    for c in (2 * k, 2 * k + 1):
                        o = bank[2 + c].rearrange("p (j m) -> p j m", j=4)
                        MM(o, identb[:, :], mbias[:, t, :].unsqueeze(1).broadcast_to((P, 4, L)), start=True, stop=False)
                        r = slice(32 * c, 32 * c + 32)
                        last = MM(o, qk[r, 0, t * L:(t + 1) * L], k_heads[r, :, t * L:(t + 1) * L], start=False, stop=True)
                    last.then_inc(s["s_ps"], 1)

                def head_t(t, c):
                    pe.wait_ge(s["pn_sb"], g * 8 + 2 * t + c // 2 + 1)
                    if c == 1 and t:
                        pe.wait_ge(s["pT3_sb"], g * S + t)
                    elif c != 1 and (c or t):
                        pe.wait_ge(s["pT_sb"], g * 12 + 3 * t + (0, 0, 1, 2)[c])
                    for j in range(4):
                        last = TR(bank[6 + c % 2][:, j * L:(j + 1) * L], prob[:, t % 2, c, j, :], ident[:, :])
                    last.then_inc(s["pT_ps"], 1)

                def head_v(t, c):
                    if c == 3:
                        pe.wait_ge(s["pT3_sb"], g * S + t + 1)
                    else:
                        pe.wait_ge(s["pT_sb"], g * 12 + 3 * t + c + 1)
                    if c == 0 and t >= 2:
                        pe.wait_ge(s["ao_own_sb"], g * S + t - 1)
                    r = slice(32 * c, 32 * c + 32)
                    MM(bank[t % 2][r, :], v[:, t, r], pT[:, c % 2].rearrange("p j q -> p (j q)"), start=True, stop=True).then_inc(s["pv_ps"], 1)

                def out_proj(ts, b):
                    pe.wait_ge(s["aoT_sb"], g * S + ts[-1] + 1)
                    for t in ts:
                        last = MM(bank[b][:, t * D:(t + 1) * D], aoT[:, t * L:(t + 1) * L], woT[:, :], start=True, stop=True)
                    last.then_inc(s["wo_ps"], 1)

                pe.wait_ge(s["k_heads_sb"], g * 4 + 4)
                scores(0, 0)
                scores(0, 1)
                if not final:
                    bc_dtl(g + 1)
                    pe.wait_ge(s["sres_sb"], g * 2 + 4)
                pe.wait_ge(s["v_sb"], g + 1)
                for t in range(S):
                    if t + 1 < S:
                        scores(t + 1, 0)
                    head_t(t, 0)
                    head_t(t, 1)
                    if t == 0 and not final:
                        steps(g + 1, 0)
                        pe.wait_ge(s["bc_res1"], g + 2)
                    if t == 1 and not final:
                        pe.wait_ge(s["zabs_sb"], g * 4 + 8)
                    head_v(t, 0)
                    if t + 1 < S:
                        scores(t + 1, 1)
                    if t == 0 and not final:
                        steps(g + 1, 1)
                    head_t(t, 2)
                    head_v(t, 1)
                    head_t(t, 3)
                    head_v(t, 2)
                    if t == S - 1:
                        out_proj(range(S - 1), 2)
                    head_v(t, 3)
                out_proj((S - 1,), 3)
                if not final:
                    scan_start(g + 1)
                pe.wait_ge(s["x2_sb"], g * S + S)
                for t in range(S):
                    last = TR(bank[3][:, t * L:(t + 1) * L], x2[:, t, 0:D], ident[:, :])
                last.then_inc(s["x2T_ps"], 1)
                pe.wait_ge(s["x2T_sb"], g + 1)
                for t in range(S):
                    last = MM(bank[2][:, t * E:(t + 1) * E], x2T[:, t * L:(t + 1) * L], gate_wT[:, :], start=True, stop=True)
                last.then_inc(s["lg_ps"], 1)
                if not final:
                    for n in range(2, AHEAD + 1):
                        row_b(g + 1, n)
                pe.wait_ge(s["route"], 1 + g * ROUTER_LINKS + CHOSEN)
                for t in range(S + 1):
                    o = bank[2][:, (2 * S + t) * E:(2 * S + t + 1) * E]
                    for r in range(t):
                        last = MM(o, ones_b[:, :], ohb[:, r, :], start=(r == 0), stop=(t == S and r == S - 1))
                    if t < S:
                        last = MM(o, tri[:, :], ohb[:, t, :], start=(t == 0), stop=True)
                last.then_inc(s["rank_ps"], 1)

            x_t(0)
            conv(0)
            res(0)
            bc_dtl(0)
            steps(0, 0)
            steps(0, 1)
            pe.wait_ge(s["zabs_sb"], 4)
            pe.wait_ge(s["bc_res1"], 1)
            scan_start(0)
            for n in range(2, AHEAD + 1):
                row_b(0, n)
            pe.wait_ge(s["w_later"], 16 * NL)
            with pe.Fori(0, G - 1) as g:
                group(g, False)
            group(G - 1, True)

            def rows_t(j, b, turn, load):
                pe.wait_ge(s[f"xs_load{load}"], turn * 16 + 16)
                pe.wait_ge(s["xsT_sb"], j)
                TR(bank[7][:, b * P:(b + 1) * P], xs[:, load, 0:D], ident[:, :]).then_inc(s["xsT_ps"], 1)

            def up(j, b):
                e = pe.value_load(table[0:1, 0, bass.ds(j, 1)], min_val=0, max_val=E - 1)
                pe.wait_ge(s["xsT_sb"], j + 1)
                MM(bank[b], xsT[:, b, :], w1[:, bass.ds(e, 1), :].rearrange("p a f -> p (a f)"), start=True, stop=True).then_inc(s["up_ps"], 1)
                MM(bank[2 + b], xsT[:, b, :], w3[:, bass.ds(e, 1), :].rearrange("p a f -> p (a f)"), start=True, stop=True).then_inc(s["up_ps"], 1)

            def gated_t(j, b):
                pe.wait_ge(s["gate_sb"], 1 + j + 1)
                for c in range(FC):
                    last = TR(bank[4 + b][:, c * P:(c + 1) * P], gg[:, b, c * P:(c + 1) * P], ident[:, :])
                last.then_inc(s["gT_ps"], 1)

            def down(j, b):
                e = pe.value_load(table[0:1, 0, bass.ds(j, 1)], min_val=0, max_val=E - 1)
                pe.wait_ge(s["gT_sb"], j + 1)
                pe.wait_ge(s["y_sb"], 1 + j)
                for c in range(FC):
                    last = MM(bank[6][:, b * P:(b + 1) * P], gT[:, b, c, :], w2[:, bass.ds(e, 1), c, :].rearrange("p a d -> p (a d)"),
                              start=(c == 0), stop=(c == FC - 1))
                last.then_inc(s["y_ps_s"], 1)

            pe.wait_ge(s["table_sb"], 1)
            pe.wait_ge(s["w13_load"], 32)
            pe.wait_ge(s["w2_load"], 16)
            rows_t(0, 0, 0, 0)
            rows_t(1, 1, 0, 1)
            up(0, 0)
            rows_t(2, 0, 0, 2)
            up(1, 1)
            gated_t(0, 0)
            with pe.Fori(0, NT // 4) as it:
                for b in range(4):
                    j = it * 4 + b
                    rows_t(j + 3, 1 - b % 2, it + (b + 3) // 4, (b + 3) % 4)
                    up(j + 2, b % 2)
                    gated_t(j + 1, 1 - b % 2)
                    down(j, b % 2)


def kernel(**inputs):
    import numpy as np
    import concourse.bacc as bacc
    from concourse import mybir as mb
    from concourse.bass_utils import run_bass_kernel_spmd as run

    c = np.ascontiguousarray
    i = {k.replace("L0_attn_", "").replace("L0_xattn_", "").replace("L0_ffn_", ""): np.asarray(v) for k, v in inputs.items()}

    def halves(w):
        return c(np.moveaxis(w.reshape((2, 128) + w.shape[1:]), 0, 1))

    swap = np.arange(128).reshape(64, 2)[:, ::-1].reshape(128)
    theta = (1.0 / np.float32(10000.0) ** (np.arange(0, HD, 2, dtype=np.float32) / np.float32(HD))).astype(np.float32)
    ang = (np.arange(L, dtype=np.float32)[:, None] * theta[None, :]).astype(np.float32)
    cos = np.repeat(np.tile(np.cos(ang).T, (H, 1)), 2, axis=0)
    sin = np.repeat(np.tile(np.sin(ang).T, (H, 1)), 2, axis=0)
    sin[0::2] *= -1
    scale = np.float32(1.0 / np.sqrt(np.float32(HD)))
    rope = np.stack([cos * scale, sin * scale, cos, sin], axis=1).astype(np.float32)
    arrays = {
        "x": c(i["x"]), "ctx_1024": c(i["ctx_1024"]), "mask": c(i["mask_BxS2_if1"].reshape(-1)),
        "W_in": c(i["W_in"]), "conv_w": c(i["conv_w"][:, 0, :].T), "conv_b": halves(i["conv_b"]),
        "W_x": halves(i["W_x"]), "W_dt": c(i["W_dt"]), "b_dt": halves(i["b_dt"]), "W_out": halves(i["W_out"]),
        "A_log": halves(i["A_log"]), "D": halves(i["D"]),
        "WqT": c(i["Wq"].T), "WqrT": c(i["Wq"].T[:, swap]),
        "WkT": c(i["Wk"].T), "WkrT": c(i["Wk"].T[:, swap]),
        "WvT": c(i["Wv"].T), "WoT": c(i["Wo"].T), "bo": c(i["bo"]), "rope": c(rope),
        "gate_wT": c(i["gate_w"].T), "w1T": c(i["w1"].transpose(2, 0, 1)), "w3T": c(i["w3"].transpose(2, 0, 1)),
        "w2T": c(i["w2"].transpose(2, 0, 1).reshape(FC, P, E, D).transpose(1, 2, 0, 3)),
    }
    nc = bacc.Bacc("TRN2", target_bir_lowering=False, num_devices=1)
    aps = {k: nc.dram_tensor(f"in_{k}", v.shape, mb.dt.from_np(v.dtype), kind="ExternalInput").ap() for k, v in arrays.items()}
    o = nc.dram_tensor("out_0", (B, L, D), mb.dt.float32, kind="ExternalOutput").ap()
    build(nc, aps, o)
    r = run(nc, [{f"in_{k}": v for k, v in arrays.items()}], core_ids=[0])
    return r.results[0]["out_0"]
```
